# Optimizing a Trainium2 kernel written in Bass

```python
import numpy as np
import jax
import jax.numpy as jnp

def _softmax(x, axis=-1):
    return jax.nn.softmax(x, axis=axis)

def _gelu(x):
    return jax.nn.gelu(x, approximate=True)

def _silu(x):
    return jax.nn.silu(x)

def _sigmoid(x):
    return jax.nn.sigmoid(x)

def _layernorm(x, axis=-1, eps=1e-05):
    m = jnp.mean(x, axis=axis, keepdims=True)
    v = jnp.var(x, axis=axis, keepdims=True)
    return (x - m) / jnp.sqrt(v + eps)

def _scatter_add(tgt, idx, src, axis=0):
    return tgt.at[idx].add(src)

def _segment_sum(src, seg, n):
    return jax.ops.segment_sum(src, seg, n)
kernel_name = 'mk_adj_preln_d4_adj_r2_8f47ef'

def setup_inputs(seed: int=0):
    np.random.seed(seed)
    _w = jnp.asarray

    def _rec_inputs():
        import jax
        import jax.numpy as jnp
        _gk = jax.random.key(seed)
        x = -0.0003929 + 0.9999 * jax.random.normal(jax.random.fold_in(_gk, 1), (16, 512, 128), jnp.float32)
        _w = (1.0 + jnp.arange(512, dtype=jnp.float32)) ** (-0.5)
        _w = _w / _w.mean()
        _pij = jnp.clip(0.00390625 * _w[:, None] * _w[None, :], 0.0, 1.0)
        _a = jax.random.uniform(jax.random.fold_in(_gk, 2), (512, 512)) < _pij
        _a = jnp.logical_or(_a, jnp.swapaxes(_a, -1, -2))
        _a = jnp.logical_or(_a, jnp.eye(512, dtype=bool))
        _af = _a.astype(jnp.float32)
        _af = _af * jax.random.uniform(jax.random.fold_in(_gk, 3), (512, 512), jnp.float32, 0.05, 1)
        adj = _af
        return (x, adj)
    x, adj = _rec_inputs()

    def _L0_gnn_setup():
        import jax, jax.numpy as jnp
        import numpy as np
        EPS = 1e-05

        def _batchnorm(x, gamma, beta):
            mu = jnp.mean(x, axis=0)
            var = jnp.var(x, axis=0)
            return (x - mu) * jax.lax.rsqrt(var + EPS) * gamma + beta
        key = jax.random.key(seed)
        ks = jax.random.split(key, 4)
        b, n, d, h, o = (32, 1024, 128, 256, 128)
        features = jax.random.normal(ks[0], (b, n, d), dtype=jnp.float32)
        A = jax.random.uniform(ks[1], (n, n), dtype=jnp.float32)
        lim1 = float(np.sqrt(6.0 / (d + h)))
        W1 = jax.random.uniform(ks[2], (h, d), minval=-lim1, maxval=lim1, dtype=jnp.float32)
        b1 = jnp.zeros((h,), jnp.float32)
        lim2 = float(np.sqrt(6.0 / (h + o)))
        W2 = jax.random.uniform(ks[3], (o, h), minval=-lim2, maxval=lim2, dtype=jnp.float32)
        b2 = jnp.zeros((o,), jnp.float32)
        g1 = jnp.ones((h,), jnp.float32)
        be1 = jnp.zeros((h,), jnp.float32)
        g2 = jnp.ones((o,), jnp.float32)
        be2 = jnp.zeros((o,), jnp.float32)
        return {'features': features, 'A': A, 'W1': W1, 'b1': b1, 'g1': g1, 'be1': be1, 'W2': W2, 'b2': b2, 'g2': g2, 'be2': be2}
    _L0_gnn_all = _L0_gnn_setup()
    _L0_gnn_in = {k: v for k, v in _L0_gnn_all.items() if k in ('W1', 'b1', 'g1', 'be1', 'W2', 'b2', 'g2', 'be2')}
    del _L0_gnn_all

    def _L1_gnn_setup():
        import jax, jax.numpy as jnp
        import numpy as np
        B, T, D, H = (64, 1024, 128, 128)
        MAX_SKIP = 4

        def _lstm_last(Wih, Whh, bih, bhh, xs):
            N, _, Hd = xs.shape
            bias = bih + bhh

            def step(carry, x_t):
                h, c = carry
                g = x_t @ Wih.T + h @ Whh.T + bias
                i, f, gg, o = jnp.split(g, 4, axis=-1)
                c = jax.nn.sigmoid(f) * c + jax.nn.sigmoid(i) * jnp.tanh(gg)
                h = jax.nn.sigmoid(o) * jnp.tanh(c)
                return ((h, c), None)
            init = (jnp.zeros((N, Hd), xs.dtype), jnp.zeros((N, Hd), xs.dtype))
            (h_last, _), _ = jax.lax.scan(step, init, jnp.swapaxes(xs, 0, 1))
            return h_last
        key = jax.random.key(seed)
        ks = jax.random.split(key, 8)
        s = 0.05
        x = jax.random.normal(ks[0], (B, T, D), jnp.float32)
        adj = jax.random.uniform(ks[1], (T, T), jnp.float32) / T
        Wg0 = jax.random.normal(ks[2], (D, H), jnp.float32) * s
        bg0 = jnp.zeros((H,), jnp.float32)
        Wg1 = jax.random.normal(ks[3], (H, H), jnp.float32) * s
        bg1 = jnp.zeros((H,), jnp.float32)
        Wih = jax.random.normal(ks[4], (MAX_SKIP, 4 * H, H), jnp.float32) * s
        Whh = jax.random.normal(ks[5], (MAX_SKIP, 4 * H, H), jnp.float32) * s
        bih = jax.random.normal(ks[6], (MAX_SKIP, 4 * H), jnp.float32) * s
        bhh = jax.random.normal(ks[7], (MAX_SKIP, 4 * H), jnp.float32) * s
        return dict(x=x, adj=adj, Wg0=Wg0, bg0=bg0, Wg1=Wg1, bg1=bg1, Wih=Wih, Whh=Whh, bih=bih, bhh=bhh)
    _L1_gnn_all = _L1_gnn_setup()
    _L1_gnn_in = {k: v for k, v in _L1_gnn_all.items() if k in ('Wg0', 'bg0', 'Wg1', 'bg1', 'Wih', 'Whh', 'bih', 'bhh')}
    del _L1_gnn_all

    def _L2_gnn_setup():
        import jax, jax.numpy as jnp
        import numpy as np
        N_STEPS = 8
        SPATIAL_SCALE = 1.0
        key = jax.random.key(seed)
        ks = jax.random.split(key, 6)
        B, N, D = (32, 512, 128)
        x = jax.random.normal(ks[0], (B, N, D), dtype=jnp.float32)
        adj_mx = jax.random.uniform(ks[1], (N, N), dtype=jnp.float32) / N
        alpha_train = jnp.ones((N,), dtype=jnp.float32)
        w = jnp.eye(D, dtype=jnp.float32) + 0.01 * jax.random.normal(ks[2], (D, D), dtype=jnp.float32)
        d = jax.random.uniform(ks[3], (D,), dtype=jnp.float32)
        fc_in_w = jax.random.normal(ks[4], (D, D), dtype=jnp.float32) * (1.0 / np.sqrt(D))
        fc_in_b = jnp.zeros((D,), dtype=jnp.float32)
        return {'x': x, 'adj_mx': adj_mx, 'alpha_train': alpha_train, 'w': w, 'd': d, 'fc_in_w': fc_in_w, 'fc_in_b': fc_in_b, 'vt': 0}
    _L2_gnn_all = _L2_gnn_setup()
    _L2_gnn_in = {k: v for k, v in _L2_gnn_all.items() if k in ('alpha_train', 'w', 'd', 'fc_in_w', 'fc_in_b')}
    del _L2_gnn_all

    def _L3_gnn_setup():
        import jax, jax.numpy as jnp
        import numpy as np
        N = 2048
        NFEAT, NHID, NCLASS = (128, 256, 128)
        B = 4

        def _slconv(x, adj, S, W):
            support = jnp.einsum('bnf,fh->bnh', x, W)
            weighting = adj * S
            return jnp.einsum('nm,bmh->bnh', weighting, support)
        key = jax.random.key(seed)
        ks = jax.random.split(key, 6)
        x = jax.random.normal(ks[0], (B, N, NFEAT), dtype=jnp.float32)
        adj = jax.random.uniform(ks[1], (N, N), dtype=jnp.float32)
        S = jnp.ones((N, N), dtype=jnp.float32)
        W1 = jax.random.normal(ks[2], (NFEAT, NHID), dtype=jnp.float32) / np.sqrt(NFEAT)
        W2 = jax.random.normal(ks[3], (NHID, 2 * NHID), dtype=jnp.float32) / np.sqrt(NHID)
        W3 = jax.random.normal(ks[4], (2 * NHID, NCLASS), dtype=jnp.float32) / np.sqrt(2 * NHID)
        return {'x': x, 'adj': adj, 'S': S, 'W1': W1, 'W2': W2, 'W3': W3}
    _L3_gnn_all = _L3_gnn_setup()
    _L3_gnn_in = {k: v for k, v in _L3_gnn_all.items() if k in ('W1', 'W2', 'W3')}
    del _L3_gnn_all
    return {'x': x, 'adj': adj, 'L0_gnn_W1': _L0_gnn_in['W1'], 'L0_gnn_b1': _L0_gnn_in['b1'], 'L0_gnn_g1': _L0_gnn_in['g1'], 'L0_gnn_be1': _L0_gnn_in['be1'], 'L0_gnn_W2': _L0_gnn_in['W2'], 'L0_gnn_b2': _L0_gnn_in['b2'], 'L0_gnn_g2': _L0_gnn_in['g2'], 'L0_gnn_be2': _L0_gnn_in['be2'], 'L1_gnn_Wg0': _L1_gnn_in['Wg0'], 'L1_gnn_bg0': _L1_gnn_in['bg0'], 'L1_gnn_Wg1': _L1_gnn_in['Wg1'], 'L1_gnn_bg1': _L1_gnn_in['bg1'], 'L1_gnn_Wih': _L1_gnn_in['Wih'], 'L1_gnn_Whh': _L1_gnn_in['Whh'], 'L1_gnn_bih': _L1_gnn_in['bih'], 'L1_gnn_bhh': _L1_gnn_in['bhh'], 'L2_gnn_alpha_train': _L2_gnn_in['alpha_train'], 'L2_gnn_w': _L2_gnn_in['w'], 'L2_gnn_d': _L2_gnn_in['d'], 'L2_gnn_fc_in_w': _L2_gnn_in['fc_in_w'], 'L2_gnn_fc_in_b': _L2_gnn_in['fc_in_b'], 'L3_gnn_W1': _L3_gnn_in['W1'], 'L3_gnn_W2': _L3_gnn_in['W2'], 'L3_gnn_W3': _L3_gnn_in['W3']}

def reference(x, adj, L0_gnn_W1, L0_gnn_b1, L0_gnn_g1, L0_gnn_be1, L0_gnn_W2, L0_gnn_b2, L0_gnn_g2, L0_gnn_be2, L1_gnn_Wg0, L1_gnn_bg0, L1_gnn_Wg1, L1_gnn_bg1, L1_gnn_Wih, L1_gnn_Whh, L1_gnn_bih, L1_gnn_bhh, L2_gnn_alpha_train, L2_gnn_w, L2_gnn_d, L2_gnn_fc_in_w, L2_gnn_fc_in_b, L3_gnn_W1, L3_gnn_W2, L3_gnn_W3):
    import jax
    import jax.numpy as jnp

    def _L0_gnn_ref(features, A, W1, b1, g1, be1, W2, b2, g2, be2):
        import jax, jax.numpy as jnp
        import numpy as np
        EPS = 1e-05

        def _batchnorm(x, gamma, beta):
            mu = jnp.mean(x, axis=0)
            var = jnp.var(x, axis=0)
            return (x - mu) * jax.lax.rsqrt(var + EPS) * gamma + beta
        b, n, d = features.shape
        A_norm = A + jnp.eye(n, dtype=A.dtype)
        deg = jnp.sum(A_norm, axis=0) + jnp.sum(A_norm, axis=1) - jnp.diagonal(A_norm)
        dinv = jax.lax.rsqrt(deg)
        A_hat = A_norm * dinv[:, None] * dinv[None, :]
        agg = jnp.einsum('nm,bmd->bnd', A_hat, features)
        x = agg.reshape(-1, d)
        h = jax.nn.relu(_batchnorm(x @ W1.T + b1, g1, be1))
        out = h @ W2.T + b2
        out = _batchnorm(out, g2, be2)
        return out.reshape(b, n, -1)

    def _L1_gnn_ref(x, adj, Wg0, bg0, Wg1, bg1, Wih, Whh, bih, bhh):
        import jax, jax.numpy as jnp
        import numpy as np
        B, T, D, H = (64, 1024, 128, 128)
        MAX_SKIP = 4

        def _lstm_last(Wih, Whh, bih, bhh, xs):
            N, _, Hd = xs.shape
            bias = bih + bhh

            def step(carry, x_t):
                h, c = carry
                g = x_t @ Wih.T + h @ Whh.T + bias
                i, f, gg, o = jnp.split(g, 4, axis=-1)
                c = jax.nn.sigmoid(f) * c + jax.nn.sigmoid(i) * jnp.tanh(gg)
                h = jax.nn.sigmoid(o) * jnp.tanh(c)
                return ((h, c), None)
            init = (jnp.zeros((N, Hd), xs.dtype), jnp.zeros((N, Hd), xs.dtype))
            (h_last, _), _ = jax.lax.scan(step, init, jnp.swapaxes(xs, 0, 1))
            return h_last
        h = jax.nn.relu(jnp.einsum('ts,bsh->bth', adj, x @ Wg0 + bg0))
        h = jax.nn.relu(jnp.einsum('ts,bsh->bth', adj, h @ Wg1 + bg1))
        Bv, Tv, Hd = h.shape
        for p in range(1, MAX_SKIP + 1):
            nw = Tv // p
            wins = h[:, :nw * p, :].reshape(Bv * nw, p, Hd)
            last = _lstm_last(Wih[p - 1], Whh[p - 1], bih[p - 1], bhh[p - 1], wins)
            idx = jnp.arange(nw) * p + (p - 1)
            h = h.at[:, idx, :].set(last.reshape(Bv, nw, Hd))
        return h

    def _L2_gnn_ref(x, adj_mx, alpha_train, w, d, fc_in_w, fc_in_b, vt):
        import jax, jax.numpy as jnp
        import numpy as np
        N_STEPS = 8
        SPATIAL_SCALE = 1.0
        x0 = jax.lax.stop_gradient(x)
        h = jnp.einsum('bnd,ed->bne', x, fc_in_w) + fc_in_b
        alph = jax.nn.sigmoid(alpha_train)[:, None]
        d_clamped = jnp.clip(d, 0.0, 1.0)
        w_eff = w * d_clamped @ w.T
        dt = jnp.float32(SPATIAL_SCALE / N_STEPS)

        def euler_step(h, _):
            ax = jnp.einsum('nm,bmd->bnd', adj_mx, h)
            f = alph * 0.5 * (ax - h) + h @ w_eff - h + x0
            return (h + dt * f, None)
        h, _ = jax.lax.scan(euler_step, h, None, length=N_STEPS)
        return h

    def _L3_gnn_ref(x, adj, S, W1, W2, W3):
        import jax, jax.numpy as jnp
        import numpy as np
        N = 2048
        NFEAT, NHID, NCLASS = (128, 256, 128)
        B = 4

        def _slconv(x, adj, S, W):
            support = jnp.einsum('bnf,fh->bnh', x, W)
            weighting = adj * S
            return jnp.einsum('nm,bmh->bnh', weighting, support)
        h = jax.nn.relu(_slconv(x, adj, S, W1))
        h = jax.nn.relu(_slconv(h, adj, S, W2))
        return _slconv(h, adj, S, W3)
    h = jnp.maximum(_layernorm(x, axis=-1), 0.0)
    x = x + _L0_gnn_ref(h, adj, L0_gnn_W1, L0_gnn_b1, L0_gnn_g1, L0_gnn_be1, L0_gnn_W2, L0_gnn_b2, L0_gnn_g2, L0_gnn_be2)
    h = jnp.maximum(_layernorm(x, axis=-1), 0.0)
    x = x + _L1_gnn_ref(h, adj, L1_gnn_Wg0, L1_gnn_bg0, L1_gnn_Wg1, L1_gnn_bg1, L1_gnn_Wih, L1_gnn_Whh, L1_gnn_bih, L1_gnn_bhh)
    h = jnp.maximum(_layernorm(x, axis=-1), 0.0)
    x = x + _L2_gnn_ref(h, adj, L2_gnn_alpha_train, L2_gnn_w, L2_gnn_d, L2_gnn_fc_in_w, L2_gnn_fc_in_b, 0)
    h = jnp.maximum(_layernorm(x, axis=-1), 0.0)
    x = x + _L3_gnn_ref(h, adj, adj, L3_gnn_W1, L3_gnn_W2, L3_gnn_W3)
    return x

_drawn_inputs = setup_inputs


def setup_inputs(seed=0):
    import zlib

    import numpy as np

    out = dict(_drawn_inputs(seed))
    spreads = {'L0_gnn_b1': (0.0, 0.8),
     'L0_gnn_g1': (1.0, 0.2),
     'L0_gnn_be1': (0.0, 0.304),
     'L0_gnn_b2': (0.0, 0.8),
     'L0_gnn_g2': (1.0, 0.2),
     'L0_gnn_be2': (0.0, 0.1),
     'L1_gnn_bg0': (0.0, 0.623),
     'L1_gnn_bg1': (0.0, 0.8),
     'L2_gnn_alpha_train': (1.0, 0.6),
     'L2_gnn_fc_in_b': (0.0, 0.1)}
    factors = {'L1_gnn_Whh': 8.0, 'L1_gnn_bih': 5.852, 'L1_gnn_bhh': 6.004}
    for name, (base, spread) in spreads.items():
        noise = np.random.default_rng([zlib.crc32(name.encode()), seed]).standard_normal(out[name].shape)
        drawn = base * np.exp(spread * noise) if base else spread * noise
        out[name] = jnp.asarray(drawn.astype(out[name].dtype))
    for name, factor in factors.items():
        out[name] = (out[name] * factor).astype(out[name].dtype)
    return out
```

```python
import numpy as np


def graph_stack_kernel(nc, d):
    import concourse.bass as bass
    from concourse import mybir
    from concourse.alu_op_type import AluOpType as ALU
    from contextlib import ExitStack, contextmanager
    from math import comb

    ACT = mybir.ActivationFunctionType
    AX = mybir.AxisListType
    f32, f32r = mybir.dt.float32, mybir.dt.float32r

    B, N, D = d["x"].shape
    P = 128
    NT = N // P
    C1 = d["L0_gnn_W1"].shape[0] // P
    H3A = d["L3_gnn_W1"].shape[1] // P
    H3B = d["L3_gnn_W2"].shape[1] // P
    SKIPS = d["L1_gnn_Wih"].shape[0]
    GATES = 4
    EPS = 1e-5
    STEPS = 8
    DT = 1.0 / STEPS
    PAIRS = B // 2
    QUADS = B // 4
    I_, F_, G_, O_ = range(GATES)

    rows = {}
    at = 0
    for name, n in (("bih", 4 * SKIPS), ("bhh", 4 * SKIPS), ("b1", C1), ("g1", C1), ("be1", C1), ("b2", 1),
                    ("g2", 1), ("be2", 1), ("bg1", 1), ("alpha", NT), ("d", 1), ("fcb", 1)):
        rows[name] = (at, n)
        at += n
    NVEC = at

    def as_f32(ap):
        return ap.bitcast(f32)

    def products(out, w, m, first, last):
        nc.tensor.matmul(out, w[0], m[0], start=first, stop=False)
        nc.tensor.matmul(out, w[0], m[1], start=False, stop=False)
        return nc.tensor.matmul(out, w[1], m[0], start=False, stop=last)

    with ExitStack() as top:
        def sb(ctx, name, shape, dt=f32):
            return ctx.enter_context(nc.sbuf_tensor(name, shape, dt))

        def sb2(ctx, name, shape):
            return sb(ctx, name + "_hi", shape, f32r), sb(ctx, name + "_lo", shape, f32r)

        in_stage = []
        windows = [sorted(nc.free_semaphores)[38 * n:38 * (n + 1)] for n in range(4)]

        def sem(ctx, name):
            in_stage.append(nc.alloc_semaphore(name=name, num=windows[0][len(in_stage)]))
            return in_stage[-1]

        @contextmanager
        def stage():
            with ExitStack() as ctx:
                yield ctx
            nc.clear_and_free_semaphores(in_stage)
            in_stage.clear()
            windows.append(windows.pop(0))

        bank = [top.enter_context(nc.psum_tensor(f"bank{i}", [P, 512], f32)) for i in range(8)]

        X = sb(top, "X", [P, B, NT, D])
        ident = sb(top, "ident", [P, P])
        ident_r = sb(top, "ident_r", [P, P], f32r)
        ones = sb(top, "ones", [P, P])
        ones_r = sb(top, "ones_r", [P, P], f32r)
        vec = sb(top, "vec", [P, NVEC])
        lstm_bias = sb(top, "lstm_bias", [P, 4 * SKIPS])
        eps_col = sb(top, "eps_col", [P, 1])
        stats = sb(top, "stats", [P, 2, NT, 6])
        mv = sb(top, "mv", [P, 2, NT, 2])
        std = sb(top, "std", [P, 2, NT])
        rstd = sb(top, "rstd", [P, 2, NT])
        shift = sb(top, "shift", [P, 2, NT])
        XN = [sb(top, f"XN{s}", [P, NT, D]) for s in range(2)]
        HN = [sb2(top, f"HN{s}", [P, NT, D]) for s in range(2)]

        def col(name, i=0):
            a, n = rows[name]
            return vec[:, a + i:a + i + 1]

        last_three = sorted(nc.free_semaphores)[-3:]
        s_passed = [(nc.scalar, nc.alloc_semaphore(name="act_waits_passed", num=last_three[0])),
                    (nc.vector, nc.alloc_semaphore(name="dve_waits_passed", num=last_three[1])),
                    (nc.gpsimd, nc.alloc_semaphore(name="pool_waits_passed", num=last_three[2]))]

        def wait_apart(eng, semaphore, value):
            eng.wait_ge(semaphore, value)
            for engine, passed in s_passed:
                if engine is eng:
                    eng.sem_inc(passed, 1)

        class LN:
            def __init__(self, ctx, tag):
                self.stats_ready = sem(ctx, tag + "_ln_stats_ready")
                self.mv_ready = sem(ctx, tag + "_ln_mv_ready")
                self.std_ready = sem(ctx, tag + "_ln_std_ready")
                self.rstd_ready = sem(ctx, tag + "_ln_rstd_ready")
                self.xn_ready = [sem(ctx, f"{tag}_ln_xn_ready_{s}") for s in range(2)]
                self.hi_ready = [sem(ctx, f"{tag}_ln_hi_ready_{s}") for s in range(2)]
                self.ready = [sem(ctx, f"{tag}_ln_ready_{s}") for s in range(2)]

        def ln_stats(dve, ln, q):
            for s in range(2):
                for t in range(NT):
                    last = nc.vector.bn_stats(stats[:, s, t], X[:, bass.ds(2 * q + s, 1), t].rearrange("p a f -> p (a f)"))
            last.then_inc(ln.stats_ready, 1)
            wait_apart(dve, ln.stats_ready, q + 1)
            for s in range(2):
                for t in range(NT):
                    last = nc.vector.bn_aggr(mv[:, s, t], stats[:, s, t])
            last.then_inc(ln.mv_ready, 1)

        def ln_std(act, ln, q):
            act.wait_ge(ln.mv_ready, q + 1)
            nc.scalar.activation(std[:], mv[:, :, :, 1], ACT.Sqrt, bias=eps_col[:]).then_inc(ln.std_ready, 1)

        def ln_rstd(dve, ln, q):
            dve.wait_ge(ln.std_ready, q + 1)
            if not isinstance(q, int) or q > 0:
                for s in range(2):
                    dve.wait_ge(ln.xn_ready[s], q)
            nc.vector.reciprocal(rstd[:], std[:]).then_inc(ln.rstd_ready, 1)
            dve.wait_ge(ln.rstd_ready, 2 * q + 1)
            nc.vector.scalar_tensor_tensor(out=shift[:], in0=mv[:, :, :, 0], scalar=-1.0, in1=rstd[:],
                                           op0=ALU.mult, op1=ALU.mult).then_inc(ln.rstd_ready, 1)

        def ln_apply(act, ln, s, q):
            act.wait_ge(ln.rstd_ready, 2 * q + 2)
            wait_apart(act, ln.ready[s], q + 1)
            for t in range(NT):
                last = nc.scalar.activation(XN[s][:, t], X[:, bass.ds(2 * q + s, 1), t].rearrange("p a f -> p (a f)"), ACT.Relu,
                                            bias=shift[:, s, t:t + 1], scale=rstd[:, s, t:t + 1])
            last.then_inc(ln.xn_ready[s], 1)

        def ln_split(pool, ln, s, q, used=None, used_at=None):
            if used is not None:
                pool.wait_ge(used, used_at)
            wait_apart(pool, ln.xn_ready[s], q + 1)
            nc.gpsimd.tensor_copy(HN[s][0][:], XN[s][:]).then_inc(ln.hi_ready[s], 1)
            pool.wait_ge(ln.hi_ready[s], q + 1)
            nc.gpsimd.tensor_tensor(HN[s][1][:], XN[s][:], as_f32(HN[s][0][:]), ALU.subtract).then_inc(ln.ready[s], 1)

        def ln_split_all(pool, ln, used, per=1):
            for s in range(2):
                pool.sem_inc(ln.ready[s], 1)
            ln_split(pool, ln, 0, 0)
            ln_split(pool, ln, 1, 0)
            ln_split(pool, ln, 0, 1, used, per)
            with pool.Fori(0, PAIRS - 2) as q:
                ln_split(pool, ln, 1, q + 1, used, per * (2 * q + 2))
                ln_split(pool, ln, 0, q + 2, used, per * (2 * q + 3))
            ln_split(pool, ln, 1, PAIRS - 1, used, per * (2 * PAIRS - 2))

        def aggregate(out, h, matT):
            for m in range(NT):
                last = products(out, (h[0][:, m], h[1][:, m]), (matT[0][:, m], matT[1][:, m]), m == 0, m == NT - 1)
            return last

        l1 = top.enter_context(ExitStack())
        AT = sb2(l1, "AT", [P, NT, N])
        bias_g0 = sb(l1, "bias_g0", [P, NT, D])
        bias_g1 = sb(l1, "bias_g1", [P, N])
        Wg0 = sb2(l1, "Wg0", [P, D])
        Wg1 = sb2(l1, "Wg1", [P, D])
        W1T = sb2(l1, "W1T", [P, C1 * P])
        W2T = sb2(l1, "W2T", [P, C1, D])
        WihT = sb2(l1, "WihT", [P, SKIPS, GATES * D])
        WhhT = sb2(l1, "WhhT", [P, SKIPS - 1, GATES * D])
        l0 = l1.enter_context(ExitStack())
        H1 = sb(l0, "H1", [P, C1, B, N])
        st1 = sb(l0, "st1", [P, C1, B, 6])
        st2 = sb(l0, "st2", [P, B, 6])
        bn = sb(l0, "bn", [P, C1 + 1, 2])
        bn_std = sb(l0, "bn_std", [P, C1 + 1])
        bn_rstd = sb(l0, "bn_rstd", [P, C1 + 1])
        bn_scale = sb(l0, "bn_scale", [P, C1 + 1])
        bn_shift = sb(l0, "bn_shift", [P, C1 + 1])

        l0a = l0.enter_context(ExitStack())
        AhT = sb2(l0a, "AhT", [P, NT, N])

        with stage() as c:
            A = H1[:, 0, 0:NT]
            wih = H1[:, 0, 4:4 + SKIPS].rearrange("p l (g k) -> p l g k", g=GATES)
            whh = H1[:, 0, 8:8 + SKIPS].rearrange("p l (g k) -> p l g k", g=GATES)
            vrows = sb(c, "vrows", [NVEC, P])
            bg0_row = sb(c, "bg0_row", [1, D])
            w1n = sb(c, "w1n", [P, C1, D])
            w2n = sb(c, "w2n", [P, C1 * P])
            wgn = sb(c, "wgn", [P, 2, D])
            diag_blocks = sb(c, "diag_blocks", [P, NT, P])
            rowsum = sb(c, "rowsum", [P, NT])
            colsum = sb(c, "colsum", [P, NT])
            diag = sb(c, "diag", [P, NT])
            deg = sb(c, "deg", [P, NT])
            dstd = sb(c, "dstd", [P, NT])
            dinv = sb(c, "dinv", [P, NT])
            s_A = sem(c, "adj_loaded")
            s_vec = sem(c, "vectors_loaded")
            s_w = sem(c, "small_weights_loaded")
            s_lw = sem(c, "lstm_weights_loaded")
            s_x = sem(c, "x_loaded")
            s_const = sem(c, "constants_set")
            s_constr = sem(c, "rounded_constants_set")
            s_vecT = sem(c, "vectors_transposed")
            s_vecs = sem(c, "vector_columns_ready")
            s_tr = sem(c, "weights_transposed")
            s_hi = sem(c, "weight_hi_ready")
            s_lo = sem(c, "weight_lo_ready")
            s_wg = sem(c, "gcn_weights_hi_ready")
            s_AT = sem(c, "adj_transposed")
            s_AThi = sem(c, "AT_hi_ready")
            s_ATlo = sem(c, "AT_lo_ready")
            s_sum = sem(c, "degree_parts_ready")
            s_deg = sem(c, "degree_ready")
            s_dstd = sem(c, "degree_root_ready")
            s_dinv = sem(c, "degree_inverse_root_ready")
            s_scaled = sem(c, "scaled_rows_ready")
            s_AhT = sem(c, "scaled_adj_transposed")
            s_Ahhi = sem(c, "AhT_hi_ready")
            s_bc = sem(c, "broadcasts_ready")
            w_jobs = [([w1n[:, 0], w1n[:, 1]], (W1T[0][:], W1T[1][:])),
                      ([w2n[:, 0:P], w2n[:, P:2 * P]], (W2T[0][:].rearrange("p c d -> p (c d)"), W2T[1][:].rearrange("p c d -> p (c d)")))]
            w_jobs += [([wih[:, l, g] for g in range(GATES)], (WihT[0][:, l], WihT[1][:, l])) for l in range(SKIPS)]
            w_jobs += [([whh[:, l, g] for g in range(GATES)], (WhhT[0][:, l - 1], WhhT[1][:, l - 1])) for l in range(1, SKIPS)]
            W_BANKS = 4

            block = c.enter_context(nc.Block())

            @block.sync
            def _(sp):
                sp.dma_start(A, d["adj"].rearrange("(t p) n -> p t n", p=P)).then_inc(s_A, 16)
                srcs = {"bih": d["L1_gnn_bih"], "bhh": d["L1_gnn_bhh"]}
                for name in ("bih", "bhh"):
                    a, n = rows[name]
                    sp.dma_start(vrows[a:a + n, :], srcs[name].rearrange("l (g p) -> (l g) p", p=P)).then_inc(s_vec, 16)
                for name, key in (("b1", "L0_gnn_b1"), ("g1", "L0_gnn_g1"), ("be1", "L0_gnn_be1"), ("b2", "L0_gnn_b2"),
                                  ("g2", "L0_gnn_g2"), ("be2", "L0_gnn_be2"), ("bg1", "L1_gnn_bg1"),
                                  ("alpha", "L2_gnn_alpha_train"), ("d", "L2_gnn_d"), ("fcb", "L2_gnn_fc_in_b")):
                    a, n = rows[name]
                    sp.dma_start(vrows[a:a + n, :], d[key].rearrange("(r p) -> r p", p=P)).then_inc(s_vec, 16)
                sp.dma_start(wih, d["L1_gnn_Wih"].rearrange("l (g p) k -> p l g k", p=P)).then_inc(s_lw, 16)
                sp.dma_start(whh, d["L1_gnn_Whh"].rearrange("l (g p) k -> p l g k", p=P)).then_inc(s_lw, 16)

            @block.scalar
            def _(act):
                act.dma_start(w1n[:], d["L0_gnn_W1"].rearrange("(c p) k -> p c k", p=P)).then_inc(s_w, 16)
                act.dma_start(w2n[:], d["L0_gnn_W2"]).then_inc(s_w, 16)
                act.dma_start(wgn[:, 0], d["L1_gnn_Wg0"]).then_inc(s_w, 16)
                act.dma_start(wgn[:, 1], d["L1_gnn_Wg1"]).then_inc(s_w, 16)
                act.dma_start(bg0_row[:], d["L1_gnn_bg0"].rearrange("(a n) -> a n", a=1)).then_inc(s_w, 16)
                for q in range(4):
                    act.dma_start(X[:, 4 * q:4 * q + 4], d["x"][4 * q:4 * q + 4].rearrange("b (t p) f -> p b t f", p=P)).then_inc(s_x, 16)
                for u in range(NT):
                    act.wait_ge(s_AT, u + 1)
                    nc.scalar.activation(AT[0][:, u], bank[u][:], ACT.Copy).then_inc(s_AThi, 1)
                act.wait_ge(s_deg, 1)
                nc.scalar.activation(dstd[:], deg[:], ACT.Sqrt).then_inc(s_dstd, 1)
                act.wait_ge(s_w, 80)
                nc.scalar.activation(Wg0[0][:], wgn[:, 0], ACT.Copy).then_inc(s_wg, 1)
                nc.scalar.activation(Wg1[0][:], wgn[:, 1], ACT.Copy).then_inc(s_wg, 1)
                for u in range(NT):
                    act.wait_ge(s_AhT, u + 1)
                    act.wait_ge(s_dinv, 1)
                    nc.scalar.activation(AhT[0][:, u], bank[u][:], ACT.Copy, scale=dinv[:, u:u + 1]).then_inc(s_Ahhi, 1)
                for j, (tiles, dst) in enumerate(w_jobs):
                    act.wait_ge(s_tr, j + 1)
                    nc.scalar.activation(dst[0], bank[4 + j % W_BANKS][:, 0:P * len(tiles)], ACT.Copy).then_inc(s_hi, 1)

            @block.gpsimd
            def _(pool):
                nc.gpsimd.memset(ident[:], 0.0).then_inc(s_const, 1)
                nc.gpsimd.memset(ones[:], 1.0).then_inc(s_const, 1)
                nc.gpsimd.memset(eps_col[:], EPS).then_inc(s_const, 1)
                pool.wait_ge(s_const, 3)
                nc.gpsimd.affine_select(out=ident[:], in_=ident[:], compare_op=ALU.not_equal, fill=1.0, base=0,
                                        pattern=[[-1, P]], channel_multiplier=1).then_inc(s_const, 1)

            @block.tensor
            def _(pe):
                pe.wait_ge(s_const, 4)
                pe.wait_ge(s_vec, 16 * 12)
                nc.tensor.transpose(bank[7][:, 0:NVEC], vrows[:], ident[0:NVEC, 0:NVEC]).then_inc(s_vecT, 1)
                pe.wait_ge(s_A, 16)
                for u in range(NT):
                    for t in range(NT):
                        last = nc.tensor.transpose(bank[u][:, t * P:(t + 1) * P], A[:, t, u * P:(u + 1) * P], ident[:])
                    last.then_inc(s_AT, 1)
                pe.wait_ge(s_w, 80)
                nc.tensor.matmul(bank[4][:, 0:D], ones[0:1, :], bg0_row[:], start=True, stop=True)
                pe.wait_ge(s_constr, 2)
                pe.wait_ge(s_ATlo, NT)
                for u in range(NT):
                    nc.tensor.matmul(bank[5][:], ones_r[:], AT[0][:, u], start=(u == 0), stop=False)
                    last = nc.tensor.matmul(bank[5][:], ones_r[:], AT[1][:, u], start=False, stop=(u == NT - 1))
                last.then_inc(s_bc, 1)
                pe.wait_ge(s_scaled, NT)
                for u in range(NT):
                    for t in range(NT):
                        last = nc.tensor.transpose(bank[u][:, t * P:(t + 1) * P], A[:, t, u * P:(u + 1) * P], ident[:])
                    last.then_inc(s_AhT, 1)
                pe.wait_ge(s_lw, 32)
                pe.wait_ge(s_bc, 3)
                for j, (tiles, dst) in enumerate(w_jobs):
                    if j == 3:
                        pe.wait_ge(s_vecs, 1)
                    if j >= W_BANKS:
                        pe.wait_ge(s_lo, j - W_BANKS + 1)
                    for i, tile in enumerate(tiles):
                        last = nc.tensor.transpose(bank[4 + j % W_BANKS][:, i * P:(i + 1) * P], tile, ident[:])
                    last.then_inc(s_tr, 1)

            @block.vector
            def _(dve):
                dve.wait_ge(s_const, 4)
                nc.vector.tensor_copy(ident_r[:], ident[:]).then_inc(s_constr, 1)
                nc.vector.tensor_copy(ones_r[:], ones[:]).then_inc(s_constr, 1)
                dve.wait_ge(s_vecT, 1)
                nc.vector.tensor_copy(vec[:], bank[7][:, 0:NVEC]).then_inc(s_vecs, 1)
                dve.wait_ge(s_vecs, 1)
                a, b = rows["bih"][0], rows["bhh"][0]
                nc.vector.tensor_tensor(lstm_bias[:], vec[:, a:a + 4 * SKIPS], vec[:, b:b + 4 * SKIPS], ALU.add).then_inc(s_vecs, 1)
                dve.wait_ge(s_A, 16)
                nc.vector.tensor_reduce(rowsum[:], A, AX.X, ALU.add).then_inc(s_sum, 1)
                for t in range(NT):
                    last = nc.vector.tensor_tensor(diag_blocks[:, t], A[:, t, t * P:(t + 1) * P], ident[:], ALU.mult)
                last.then_inc(s_sum, 1)
                dve.wait_ge(s_sum, 2)
                nc.vector.tensor_reduce(diag[:], diag_blocks[:], AX.X, ALU.add).then_inc(s_sum, 1)
                for u in range(NT):
                    dve.wait_ge(s_AThi, u + 1)
                    nc.vector.tensor_reduce(colsum[:, u:u + 1], bank[u][:], AX.X, ALU.add).then_inc(s_sum, 1)
                dve.wait_ge(s_sum, 3 + NT)
                nc.vector.scalar_tensor_tensor(out=deg[:], in0=rowsum[:], scalar=1.0, in1=colsum[:],
                                               op0=ALU.add, op1=ALU.add).then_inc(s_sum, 1)
                dve.wait_ge(s_sum, 4 + NT)
                nc.vector.tensor_tensor(deg[:], deg[:], diag[:], ALU.subtract).then_inc(s_deg, 1)
                for u in range(NT):
                    dve.wait_ge(s_AThi, u + 1)
                    nc.vector.tensor_tensor(AT[1][:, u], bank[u][:], as_f32(AT[0][:, u]), ALU.subtract).then_inc(s_ATlo, 1)
                dve.wait_ge(s_dstd, 1)
                nc.vector.reciprocal(dinv[:], dstd[:]).then_inc(s_dinv, 1)
                for t in range(NT):
                    last = nc.vector.tensor_tensor(A[:, t, t * P:(t + 1) * P], A[:, t, t * P:(t + 1) * P], ident[:], ALU.add)
                last.then_inc(s_deg, 1)
                dve.wait_ge(s_deg, 2)
                dve.wait_ge(s_dinv, 1)
                for t in range(NT):
                    nc.vector.tensor_scalar(A[:, t], A[:, t], dinv[:, t:t + 1], None, ALU.mult).then_inc(s_scaled, 1)
                dve.wait_ge(s_bc, 1)
                for t in range(NT):
                    last = nc.vector.tensor_scalar(bias_g0[:, t], bank[4][:, 0:D], rowsum[:, t:t + 1], None, ALU.mult)
                last.then_inc(s_bc, 1)
                nc.vector.tensor_scalar(bias_g1[:], bank[5][:], col("bg1"), None, ALU.mult).then_inc(s_bc, 1)
                dve.wait_ge(s_wg, 2)
                nc.vector.tensor_tensor(Wg0[1][:], wgn[:, 0], as_f32(Wg0[0][:]), ALU.subtract)
                nc.vector.tensor_tensor(Wg1[1][:], wgn[:, 1], as_f32(Wg1[0][:]), ALU.subtract)
                for u in range(NT):
                    dve.wait_ge(s_Ahhi, u + 1)
                    nc.vector.scalar_tensor_tensor(out=AhT[1][:, u], in0=bank[u][:], scalar=dinv[:, u:u + 1],
                                                   in1=as_f32(AhT[0][:, u]), op0=ALU.mult, op1=ALU.subtract)
                for j, (tiles, dst) in enumerate(w_jobs):
                    dve.wait_ge(s_hi, j + 1)
                    nc.vector.tensor_tensor(dst[1], bank[4 + j % W_BANKS][:, 0:P * len(tiles)], as_f32(dst[0]),
                                            ALU.subtract).then_inc(s_lo, 1)
                dve.wait_ge(s_x, 64)

        with stage() as c:
            AG = [sb2(c, f"AG{s}", [P, N]) for s in range(2)]
            ln = LN(c, "l0")
            s_agg = sem(c, "l0_aggregated")
            s_ahi = sem(c, "l0_agg_hi_ready")
            s_alo = sem(c, "l0_agg_lo_ready")
            s_w1 = sem(c, "l0_w1_done")
            s_h1 = sem(c, "l0_h1_ready")
            FREE = 2 * C1
            s_st = sem(c, "l0_stats_done")
            block = c.enter_context(nc.Block())

            @block.tensor
            def _(pe):
                def agg(q, s):
                    pe.wait_ge(ln.ready[s], q + 2)
                    aggregate(bank[s][:], HN[s], AhT).then_inc(s_agg, 1)

                def pair(q, more):
                    for s in range(2):
                        b = 2 * q + s
                        pe.wait_ge(s_alo, b + 1)
                        for h in range(C1):
                            pe.wait_ge(s_h1, C1 * b + h + 1)
                            products(bank[2 + 2 * s + h][:], (W1T[0][:, h * P:(h + 1) * P], W1T[1][:, h * P:(h + 1) * P]),
                                     (AG[s][0][:], AG[s][1][:]), True, True).then_inc(s_w1, 1)
                        if more:
                            agg(q + 1, s)

                agg(0, 0)
                agg(0, 1)
                with pe.Fori(0, PAIRS - 1) as q:
                    pair(q, True)
                pair(PAIRS - 1, False)

            @block.scalar
            def _(act):
                def agg_hi(q, s):
                    act.wait_ge(s_agg, 2 * q + s + 1)
                    nc.scalar.activation(AG[s][0][:], bank[s][:], ACT.Copy).then_inc(s_ahi, 1)

                def h1(q, s):
                    b = 2 * q + s
                    for h in range(C1):
                        wait_apart(act, s_w1, C1 * b + h + 1)
                        out = H1[:, h, bass.ds(b, 1)].rearrange("p a n -> p (a n)")
                        nc.scalar.activation(out, bank[2 + 2 * s + h][:], ACT.Identity, bias=col("b1", h)).then_inc(s_h1, 1)

                def pair(q, more, more2):
                    h1(q, 0)
                    if more2:
                        ln_std(act, ln, q + 2)
                    if more:
                        agg_hi(q + 1, 0)
                    h1(q, 1)
                    if more2:
                        ln_apply(act, ln, 0, q + 2)
                    if more:
                        agg_hi(q + 1, 1)
                    if more2:
                        ln_apply(act, ln, 1, q + 2)

                act.sem_inc(s_h1, FREE)
                ln_std(act, ln, 0)
                ln_apply(act, ln, 0, 0)
                ln_apply(act, ln, 1, 0)
                ln_std(act, ln, 1)
                ln_apply(act, ln, 0, 1)
                agg_hi(0, 0)
                ln_apply(act, ln, 1, 1)
                agg_hi(0, 1)
                with act.Fori(0, PAIRS - 2) as q:
                    pair(q, True, True)
                pair(PAIRS - 2, True, False)
                pair(PAIRS - 1, False, False)

            @block.gpsimd
            def _(pool):
                ln_split_all(pool, ln, s_agg)

            @block.vector
            def _(dve):
                def agg_lo(q, s):
                    dve.wait_ge(s_ahi, 2 * q + s + 1)
                    nc.vector.tensor_tensor(AG[s][1][:], bank[s][:], as_f32(AG[s][0][:]), ALU.subtract).then_inc(s_alo, 1)

                def h1_stats(q, s):
                    b = 2 * q + s
                    for h in range(C1):
                        dve.wait_ge(s_h1, FREE + C1 * b + h + 1)
                        nc.vector.bn_stats(st1[:, h, bass.ds(b, 1)].rearrange("p a k -> p (a k)"),
                                           H1[:, h, bass.ds(b, 1)].rearrange("p a n -> p (a n)"))

                def pair(q, more, more2):
                    if more2:
                        ln_stats(dve, ln, q + 2)
                    if more2:
                        ln_rstd(dve, ln, q + 2)
                    if more:
                        agg_lo(q + 1, 0)
                    h1_stats(q, 0)
                    if more:
                        agg_lo(q + 1, 1)
                    h1_stats(q, 1)

                ln_stats(dve, ln, 0)
                ln_rstd(dve, ln, 0)
                ln_stats(dve, ln, 1)
                ln_rstd(dve, ln, 1)
                agg_lo(0, 0)
                agg_lo(0, 1)
                with dve.Fori(0, PAIRS - 2) as q:
                    pair(q, True, True)
                pair(PAIRS - 2, True, False)
                pair(PAIRS - 1, False, False)

        l0a.close()
        with stage() as c:
            Y1 = [sb(c, f"Y1_{s}", [P, C1, N]) for s in range(2)]
            Y1s = [sb2(c, f"Y1s_{s}", [P, C1, N]) for s in range(2)]
            s_mv = sem(c, "bn1_mv_ready")
            s_std = sem(c, "bn1_std_ready")
            s_sc = sem(c, "bn1_scale_ready")
            s_y = sem(c, "bn1_applied")
            s_hi = sem(c, "bn1_hi_ready")
            s_lo = sem(c, "bn1_lo_ready")
            s_lo1 = sem(c, "bn1_lo_second_ready")
            s_w2 = sem(c, "w2_done")
            s_o = sem(c, "out2_ready")
            block = c.enter_context(nc.Block())

            @block.scalar
            def _(act):
                act.wait_ge(s_mv, 1)
                nc.scalar.activation(bn_std[:, 0:C1], bn[:, 0:C1, 1], ACT.Sqrt, bias=eps_col[:]).then_inc(s_std, 1)
                act.wait_ge(s_sc, 4)

                def bn1(q, s, ahead=True):
                    if ahead:
                        act.wait_ge(s_lo, 2 * (q - 1) + s + 1)
                        wait_apart(act, s_lo1, 2 * (q - 1) + s + 1)
                    for h in range(C1):
                        nc.scalar.activation(Y1[s][:, h], H1[:, h, bass.ds(2 * q + s, 1)].rearrange("p a n -> p (a n)"), ACT.Relu,
                                             bias=bn_shift[:, h:h + 1], scale=bn_scale[:, h:h + 1]).then_inc(s_y, 1)

                def out2(q, s):
                    b = 2 * q + s
                    wait_apart(act, s_w2, b + 1)
                    nc.scalar.activation(H1[:, 0, bass.ds(b, 1)].rearrange("p a n -> p (a n)"), bank[s][:], ACT.Identity,
                                         bias=col("b2")).then_inc(s_o, 1)

                act.sem_inc(s_o, 2)
                bn1(0, 0, ahead=False)
                bn1(0, 1, ahead=False)
                with act.Fori(0, PAIRS - 1) as q:
                    for s in range(2):
                        bn1(q + 1, s)
                        out2(q, s)
                out2(PAIRS - 1, 0)
                out2(PAIRS - 1, 1)

            @block.vector
            def _(dve):
                for h in range(C1):
                    last = nc.vector.bn_aggr(bn[:, h], st1[:, h].rearrange("p b k -> p (b k)"))
                last.then_inc(s_mv, 1)
                dve.wait_ge(s_std, 1)
                nc.vector.reciprocal(bn_rstd[:, 0:C1], bn_std[:, 0:C1]).then_inc(s_sc, 1)
                dve.wait_ge(s_sc, 1)
                g, be = rows["g1"][0], rows["be1"][0]
                nc.vector.tensor_tensor(bn_scale[:, 0:C1], bn_rstd[:, 0:C1], vec[:, g:g + C1], ALU.mult).then_inc(s_sc, 1)
                dve.wait_ge(s_sc, 2)
                nc.vector.tensor_tensor(bn_shift[:, 0:C1], bn[:, 0:C1, 0], bn_scale[:, 0:C1], ALU.mult).then_inc(s_sc, 1)
                dve.wait_ge(s_sc, 3)
                nc.vector.tensor_tensor(bn_shift[:, 0:C1], vec[:, be:be + C1], bn_shift[:, 0:C1], ALU.subtract).then_inc(s_sc, 1)

                def split(q, s, ahead=True):
                    b = 2 * q + s
                    dve.wait_ge(s_y, C1 * b + C1)
                    if ahead:
                        dve.wait_ge(s_w2, b - 1)
                    nc.vector.tensor_copy(Y1s[s][0][:], Y1[s][:]).then_inc(s_hi, 1)
                    dve.wait_ge(s_hi, b + 1)
                    nc.vector.tensor_tensor(Y1s[s][1][:, 0], Y1[s][:, 0], as_f32(Y1s[s][0][:, 0]), ALU.subtract).then_inc(s_lo, 1)

                def out2_stats(q, s):
                    b = 2 * q + s
                    dve.wait_ge(s_o, 2 + b + 1)
                    nc.vector.bn_stats(st2[:, bass.ds(b, 1)].rearrange("p a k -> p (a k)"),
                                       H1[:, 0, bass.ds(b, 1)].rearrange("p a n -> p (a n)"))

                split(0, 0, ahead=False)
                split(0, 1, ahead=False)
                with dve.Fori(0, PAIRS - 1) as q:
                    for s in range(2):
                        split(q + 1, s)
                        out2_stats(q, s)
                out2_stats(PAIRS - 1, 0)
                out2_stats(PAIRS - 1, 1)

            @block.gpsimd
            def _(pool):
                with pool.Fori(0, PAIRS) as i:
                    for s in range(2):
                        b = 2 * i + s
                        pool.wait_ge(s_hi, b + 1)
                        nc.gpsimd.tensor_tensor(Y1s[s][1][:, 1], Y1[s][:, 1], as_f32(Y1s[s][0][:, 1]), ALU.subtract).then_inc(s_lo1, 1)

            @block.tensor
            def _(pe):
                with pe.Fori(0, PAIRS) as i:
                    for s in range(2):
                        b = 2 * i + s
                        pe.wait_ge(s_lo, b + 1)
                        pe.wait_ge(s_lo1, b + 1)
                        pe.wait_ge(s_o, b + 1)
                        for h in range(C1):
                            last = products(bank[s][:], (W2T[0][:, h], W2T[1][:, h]), (Y1s[s][0][:, h], Y1s[s][1][:, h]),
                                            h == 0, h == C1 - 1)
                        last.then_inc(s_w2, 1)

        with stage() as c:
            Y2 = [sb(c, f"Y2_{s}", [P, N]) for s in range(4)]
            s_mv = sem(c, "bn2_mv_ready")
            s_std = sem(c, "bn2_std_ready")
            s_sc = sem(c, "bn2_scale_ready")
            s_y = sem(c, "bn2_applied")
            s_t = sem(c, "bn2_transposed")
            s_x = sem(c, "l0_x_added")
            block = c.enter_context(nc.Block())

            @block.scalar
            def _(act):
                act.wait_ge(s_mv, 1)
                nc.scalar.activation(bn_std[:, C1:C1 + 1], bn[:, C1, 1:2], ACT.Sqrt, bias=eps_col[:]).then_inc(s_std, 1)
                act.wait_ge(s_sc, 4)

                with act.Fori(0, QUADS) as i:
                    for s in range(4):
                        b = 4 * i + s
                        wait_apart(act, s_t, b + 1)
                        nc.scalar.activation(Y2[s][:], H1[:, 0, bass.ds(b, 1)].rearrange("p a n -> p (a n)"), ACT.Identity,
                                             bias=bn_shift[:, C1:C1 + 1], scale=bn_scale[:, C1:C1 + 1]).then_inc(s_y, 1)

            @block.tensor
            def _(pe):
                pe.sem_inc(s_t, 4)
                with pe.Fori(0, QUADS) as i:
                    for s in range(4):
                        b = 4 * i + s
                        pe.wait_ge(s_y, b + 1)
                        pe.wait_ge(s_x, b + 1)
                        for t in range(NT):
                            last = nc.tensor.transpose(bank[s][:, t * P:(t + 1) * P], Y2[s][:, t * P:(t + 1) * P], ident[:])
                        last.then_inc(s_t, 1)

            @block.vector
            def _(dve):
                dve.sem_inc(s_x, 4)
                nc.vector.bn_aggr(bn[:, C1], st2[:].rearrange("p b k -> p (b k)")).then_inc(s_mv, 1)
                dve.wait_ge(s_std, 1)
                nc.vector.reciprocal(bn_rstd[:, C1:C1 + 1], bn_std[:, C1:C1 + 1]).then_inc(s_sc, 1)
                dve.wait_ge(s_sc, 1)
                nc.vector.tensor_tensor(bn_scale[:, C1:C1 + 1], bn_rstd[:, C1:C1 + 1], col("g2"), ALU.mult).then_inc(s_sc, 1)
                dve.wait_ge(s_sc, 2)
                nc.vector.tensor_tensor(bn_shift[:, C1:C1 + 1], bn[:, C1, 0:1], bn_scale[:, C1:C1 + 1], ALU.mult).then_inc(s_sc, 1)
                dve.wait_ge(s_sc, 3)
                nc.vector.tensor_tensor(bn_shift[:, C1:C1 + 1], col("be2"), bn_shift[:, C1:C1 + 1], ALU.subtract).then_inc(s_sc, 1)
                with dve.Fori(0, QUADS) as i:
                    for s in range(4):
                        b = 4 * i + s
                        dve.wait_ge(s_t, 4 + b + 1)
                        xb = X[:, bass.ds(b, 1)].rearrange("p a t f -> p (a t f)")
                        nc.vector.tensor_tensor(xb, bank[s][:], xb, ALU.add).then_inc(s_x, 1)
        l0.close()

        H = sb2(l1, "H", [P, B, N])
        with stage() as c:
            AG = [sb2(c, f"AG1_{s}", [P, N]) for s in range(2)]
            T1 = [sb(c, f"T1_{s}", [P, NT, D]) for s in range(2)]
            G1 = [sb2(c, f"G1_{s}", [P, NT, D]) for s in range(2)]
            AG2 = [sb2(c, f"AG2_{s}", [P, N]) for s in range(2)]
            T2 = [sb(c, f"T2_{s}", [P, N]) for s in range(2)]
            ln = LN(c, "l1")
            s_a1 = sem(c, "l1_first_aggregated")
            s_a1hi = sem(c, "l1_first_agg_hi_ready")
            s_a1lo = sem(c, "l1_first_agg_lo_ready")
            s_g0 = sem(c, "l1_wg0_done")
            s_t1 = sem(c, "l1_first_sum_ready")
            s_h1hi = sem(c, "l1_h1_hi_ready")
            s_h1lo = sem(c, "l1_h1_lo_ready")
            s_a2 = sem(c, "l1_second_aggregated")
            s_a2hi = sem(c, "l1_second_agg_hi_ready")
            s_a2lo = sem(c, "l1_second_agg_lo_ready")
            s_g1 = sem(c, "l1_wg1_done")
            s_t2 = sem(c, "l1_second_sum_ready")
            s_Hhi = sem(c, "l1_H_hi_ready")
            block = c.enter_context(nc.Block())

            @block.tensor
            def _(pe):
                def agg1(q, s):
                    pe.wait_ge(ln.ready[s], q + 2)
                    aggregate(bank[s][:], HN[s], AT).then_inc(s_a1, 1)

                def wg0(q, s):
                    pe.wait_ge(s_a1lo, 2 * q + s + 1)
                    for t in range(NT):
                        cols = slice(t * P, (t + 1) * P)
                        last = products(bank[2 + s][:, cols], (AG[s][0][:, cols], AG[s][1][:, cols]), (Wg0[0][:], Wg0[1][:]), True, True)
                    last.then_inc(s_g0, 1)

                def agg2(q, s):
                    pe.wait_ge(s_h1lo, 2 * q + s + 1)
                    aggregate(bank[4 + s][:], G1[s], AT).then_inc(s_a2, 1)

                def wg1(q, s):
                    pe.wait_ge(s_a2lo, 2 * q + s + 1)
                    pe.wait_ge(s_t2, 2 * q + s + 1)
                    products(bank[6 + s][:], (Wg1[0][:], Wg1[1][:]), (AG2[s][0][:], AG2[s][1][:]), True, True).then_inc(s_g1, 1)

                def pair(q, more):
                    wg0(q, 0)
                    if more:
                        agg1(q + 1, 0)
                    wg0(q, 1)
                    agg2(q, 0)
                    agg2(q, 1)
                    if more:
                        agg1(q + 1, 1)
                    wg1(q, 0)
                    wg1(q, 1)

                agg1(0, 0)
                agg1(0, 1)
                with pe.Fori(0, PAIRS - 1) as q:
                    pair(q, True)
                pair(PAIRS - 1, False)

            @block.scalar
            def _(act):
                def agg1_hi(q, s):
                    act.wait_ge(s_a1, 2 * q + s + 1)
                    nc.scalar.activation(AG[s][0][:], bank[s][:], ACT.Copy).then_inc(s_a1hi, 1)

                def h1_hi(q, s):
                    act.wait_ge(s_t1, 2 * q + s + 1)
                    nc.scalar.activation(G1[s][0][:], T1[s][:], ACT.Relu).then_inc(s_h1hi, 1)

                def agg2_hi(q, s):
                    act.wait_ge(s_a2, 2 * q + s + 1)
                    nc.scalar.activation(AG2[s][0][:], bank[4 + s][:], ACT.Copy).then_inc(s_a2hi, 1)

                def H_hi(q, s):
                    b = 2 * q + s
                    wait_apart(act, s_t2, 2 + b + 1)
                    nc.scalar.activation(H[0][:, bass.ds(b, 1)].rearrange("p a n -> p (a n)"), T2[s][:], ACT.Relu).then_inc(s_Hhi, 1)

                def pair(q, more, more2):
                    h1_hi(q, 0)
                    if more:
                        agg1_hi(q + 1, 0)
                    h1_hi(q, 1)
                    if more2:
                        ln_std(act, ln, q + 2)
                    agg2_hi(q, 0)
                    if more2:
                        ln_apply(act, ln, 0, q + 2)
                    agg2_hi(q, 1)
                    if more2:
                        ln_apply(act, ln, 1, q + 2)
                    if more:
                        agg1_hi(q + 1, 1)
                    H_hi(q, 0)
                    H_hi(q, 1)

                ln_std(act, ln, 0)
                ln_apply(act, ln, 0, 0)
                ln_apply(act, ln, 1, 0)
                ln_std(act, ln, 1)
                ln_apply(act, ln, 0, 1)
                agg1_hi(0, 0)
                ln_apply(act, ln, 1, 1)
                agg1_hi(0, 1)
                with act.Fori(0, PAIRS - 2) as q:
                    pair(q, True, True)
                pair(PAIRS - 2, True, False)
                pair(PAIRS - 1, False, False)

            @block.gpsimd
            def _(pool):
                ln_split_all(pool, ln, s_a1)

            @block.vector
            def _(dve):
                def agg1_lo(q, s):
                    dve.wait_ge(s_a1hi, 2 * q + s + 1)
                    nc.vector.tensor_tensor(AG[s][1][:], bank[s][:], as_f32(AG[s][0][:]), ALU.subtract).then_inc(s_a1lo, 1)

                def t1(q, s):
                    dve.wait_ge(s_g0, 2 * q + s + 1)
                    nc.vector.tensor_tensor(T1[s][:].rearrange("p t f -> p (t f)"), bank[2 + s][:],
                                            bias_g0[:].rearrange("p t f -> p (t f)"), ALU.add).then_inc(s_t1, 1)

                def h1_lo(q, s):
                    dve.wait_ge(s_h1hi, 2 * q + s + 1)
                    nc.vector.scalar_tensor_tensor(out=G1[s][1][:], in0=T1[s][:], scalar=0.0, in1=as_f32(G1[s][0][:]),
                                                   op0=ALU.max, op1=ALU.subtract).then_inc(s_h1lo, 1)

                def agg2_lo(q, s):
                    dve.wait_ge(s_a2hi, 2 * q + s + 1)
                    nc.vector.tensor_tensor(AG2[s][1][:], bank[4 + s][:], as_f32(AG2[s][0][:]), ALU.subtract).then_inc(s_a2lo, 1)

                def t2(q, s):
                    dve.wait_ge(s_g1, 2 * q + s + 1)
                    nc.vector.tensor_tensor(T2[s][:], bank[6 + s][:], bias_g1[:], ALU.add).then_inc(s_t2, 1)

                def H_lo(q, s):
                    b = 2 * q + s
                    dve.wait_ge(s_Hhi, b + 1)
                    nc.vector.scalar_tensor_tensor(out=H[1][:, bass.ds(b, 1)].rearrange("p a n -> p (a n)"), in0=T2[s][:], scalar=0.0,
                                                   in1=as_f32(H[0][:, bass.ds(b, 1)]).rearrange("p a n -> p (a n)"),
                                                   op0=ALU.max, op1=ALU.subtract)

                def pair(q, more, more2):
                    t1(q, 0)
                    h1_lo(q, 0)
                    if more:
                        agg1_lo(q + 1, 0)
                    t1(q, 1)
                    h1_lo(q, 1)
                    if more2:
                        ln_stats(dve, ln, q + 2)
                        ln_rstd(dve, ln, q + 2)
                    agg2_lo(q, 0)
                    agg2_lo(q, 1)
                    if more:
                        agg1_lo(q + 1, 1)
                    t2(q, 0)
                    H_lo(q, 0)
                    t2(q, 1)
                    H_lo(q, 1)

                dve.sem_inc(s_t2, 2)
                ln_stats(dve, ln, 0)
                ln_rstd(dve, ln, 0)
                ln_stats(dve, ln, 1)
                ln_rstd(dve, ln, 1)
                agg1_lo(0, 0)
                agg1_lo(0, 1)
                with dve.Fori(0, PAIRS - 2) as q:
                    pair(q, True, True)
                pair(PAIRS - 2, True, False)
                pair(PAIRS - 1, False, False)

        for p in range(1, SKIPS + 1):
            l = p - 1
            W = N // p
            CB = {1: 1, 2: 2, 3: 2, 4: 4}[p]
            CC = CB * W
            ITERS = B // CB // 2
            GC = 3 + 4 * (p - 1)
            order = lambda t: (I_, G_, O_) if t == 0 else (F_, I_, G_, O_)
            before = lambda t: 0 if t == 0 else 3 + 4 * (t - 1)

            def columns(h, b0, t):
                return h[:, bass.ds(b0, CB), t:t + (W - 1) * p + 1:p]

            with stage() as c:
                gate = [[sb(c, f"lstm{p}_gate{g}_{s}", [P, CB, W]) for g in range(GATES)] for s in range(2)]
                cell = [sb(c, f"lstm{p}_cell_{s}", [P, CB, W]) for s in range(2)]
                inp = [XN[s][:].rearrange("p t f -> p (t f)")[:, 0:CC].rearrange("p (b w) -> p b w", b=CB) for s in range(2)]
                th = [sb(c, f"lstm{p}_tanh_{s}", [P, CB, W]) for s in range(2)]
                hf = [sb(c, f"lstm{p}_h_{s}", [P, CB, W]) for s in range(2)]
                hs = [sb2(c, f"lstm{p}_hs_{s}", [P, CB, W]) for s in range(2)]
                s_mm = [sem(c, f"lstm{p}_gate_summed_{s}") for s in range(2)]
                s_gate = [sem(c, f"lstm{p}_gate_ready_{s}") for s in range(2)]
                s_dve = [sem(c, f"lstm{p}_cell_parts_{s}") for s in range(2)]
                s_cell = [sem(c, f"lstm{p}_cell_ready_{s}") for s in range(2)]
                s_th = [sem(c, f"lstm{p}_tanh_ready_{s}") for s in range(2)]
                s_hf = [sem(c, f"lstm{p}_h_ready_{s}") for s in range(2)]
                s_h = [sem(c, f"lstm{p}_h_split_{s}") for s in range(2)]
                block = c.enter_context(nc.Block())

                def flat(ap):
                    return ap.rearrange("p b w -> p (b w)")

                @block.tensor
                def _(pe):
                    with pe.Fori(0, ITERS) as i:
                        for t in range(p):
                            for s in range(2):
                                b0 = (2 * i + s) * CB
                                for n, g in enumerate(order(t)):
                                    if n == 0:
                                        pe.wait_ge(s_gate[s], GC * i + before(t) + 1)
                                    wx = (WihT[0][:, l, g * P:(g + 1) * P], WihT[1][:, l, g * P:(g + 1) * P])
                                    last = products(bank[4 * s + g][:, 0:CC].rearrange("p (b w) -> p b w", b=CB), wx,
                                                    (columns(H[0], b0, t), columns(H[1], b0, t)), True, t == 0)
                                    if t == 0:
                                        last.then_inc(s_mm[s], 1)
                                if t > 0:
                                    pe.wait_ge(s_h[s], p * i + t + 1)
                                    for g in order(t):
                                        wh = (WhhT[0][:, l - 1, g * P:(g + 1) * P], WhhT[1][:, l - 1, g * P:(g + 1) * P])
                                        products(bank[4 * s + g][:, 0:CC], wh, (flat(hs[s][0][:]), flat(hs[s][1][:])),
                                                 False, True).then_inc(s_mm[s], 1)

                @block.scalar
                def _(act):
                    for s in range(2):
                        act.sem_inc(s_gate[s], 1)
                    with act.Fori(0, ITERS) as i:
                        for t in range(p):
                            for s in range(2):
                                if t == 0:
                                    act.wait_ge(s_h[s], p * i + 1)
                                for n, g in enumerate(order(t)):
                                    act.wait_ge(s_mm[s], GC * i + before(t) + n + 1)
                                    nc.scalar.activation(flat(gate[s][g][:]), bank[4 * s + g][:, 0:CC], ACT.Tanh if g == G_ else ACT.Sigmoid,
                                                         bias=lstm_bias[:, 4 * l + g:4 * l + g + 1]).then_inc(s_gate[s], 1)
                                act.wait_ge(s_cell[s], p * i + t + 1)
                                nc.scalar.activation(th[s][:], cell[s][:], ACT.Tanh).then_inc(s_th[s], 1)

                @block.vector
                def _(dve):
                    for s in range(2):
                        dve.sem_inc(s_h[s], 1)
                    with dve.Fori(0, ITERS) as i:
                        for t in range(p):
                            for s in range(2):
                                done = GC * i + before(t) + 1
                                if t == 0:
                                    dve.wait_ge(s_gate[s], done + 2)
                                    nc.vector.tensor_tensor(cell[s][:], gate[s][I_][:], gate[s][G_][:], ALU.mult).then_inc(s_cell[s], 1)
                                else:
                                    dve.wait_ge(s_gate[s], done + 1)
                                    nc.vector.tensor_tensor(cell[s][:], gate[s][F_][:], cell[s][:], ALU.mult)
                                    dve.wait_ge(s_gate[s], done + 3)
                                    nc.vector.tensor_tensor(inp[s], gate[s][I_][:], gate[s][G_][:], ALU.mult).then_inc(s_dve[s], 1)
                                    dve.wait_ge(s_dve[s], (p - 1) * i + t)
                                    nc.vector.tensor_tensor(cell[s][:], cell[s][:], inp[s], ALU.add).then_inc(s_cell[s], 1)
                                b0 = (2 * i + s) * CB
                                dve.wait_ge(s_th[s], p * i + t + 1)
                                nc.vector.tensor_tensor(hf[s][:], gate[s][O_][:], th[s][:], ALU.mult).then_inc(s_hf[s], 1)
                                hi = columns(H[0], b0, t) if t == p - 1 else hs[s][0][:]
                                lo = columns(H[1], b0, t) if t == p - 1 else hs[s][1][:]
                                dve.wait_ge(s_hf[s], 2 * (p * i + t) + 1)
                                nc.vector.tensor_copy(hi, hf[s][:]).then_inc(s_hf[s], 1)
                                dve.wait_ge(s_hf[s], 2 * (p * i + t) + 2)
                                nc.vector.tensor_tensor(lo, hf[s][:], as_f32(hi), ALU.subtract).then_inc(s_h[s], 1)

        with stage() as c:
            Y = [sb(c, f"Yl1_{s}", [P, N]) for s in range(4)]
            s_y = [sem(c, f"l1_h_joined_{s}") for s in range(4)]
            s_t = sem(c, "l1_h_transposed")
            s_x = sem(c, "l1_x_added")
            block = c.enter_context(nc.Block())

            def join(eng, b, s):
                eng.wait_ge(s_t, b + 1)
                eng.tensor_tensor(Y[s][:], as_f32(H[0][:, bass.ds(b, 1)]).rearrange("p a n -> p (a n)"),
                                  as_f32(H[1][:, bass.ds(b, 1)]).rearrange("p a n -> p (a n)"), ALU.add).then_inc(s_y[s], 1)

            @block.gpsimd
            def _(pool):
                with pool.Fori(0, QUADS) as g:
                    join(nc.gpsimd, 4 * g, 0)
                    join(nc.gpsimd, 4 * g + 2, 2)

            @block.tensor
            def _(pe):
                pe.sem_inc(s_t, 4)
                with pe.Fori(0, QUADS) as g:
                    for s in range(4):
                        b = 4 * g + s
                        pe.wait_ge(s_y[s], g + 1)
                        pe.wait_ge(s_x, b + 1)
                        for t in range(NT):
                            last = nc.tensor.transpose(bank[s][:, t * P:(t + 1) * P], Y[s][:, t * P:(t + 1) * P], ident[:])
                        last.then_inc(s_t, 1)

            @block.vector
            def _(dve):
                def add(b, s):
                    dve.wait_ge(s_t, 4 + b + 1)
                    xb = X[:, bass.ds(b, 1)].rearrange("p a t f -> p (a t f)")
                    nc.vector.tensor_tensor(xb, bank[s][:], xb, ALU.add).then_inc(s_x, 1)

                dve.sem_inc(s_x, 4)
                with dve.Fori(0, QUADS) as g:
                    join(nc.vector, 4 * g + 1, 1)
                    join(nc.vector, 4 * g + 3, 3)
                    for s in range(4):
                        add(4 * g + s, s)
        l1.close()

        KB = 3
        KI = (STEPS + KB) // KB
        assert KB * KI == STEPS + 1
        l2 = top.enter_context(ExitStack())
        PT = sb2(l2, "PT", [P, NT, N])
        P2T = sb2(l2, "P2T", [P, NT, N])
        P3T = sb2(l2, "P3T", [P, NT, N])
        Ms = sb2(l2, "Ms", [P, KB, KI, D])
        bias_w = sb(l2, "bias_w", [P, NT, KI, D])
        with stage() as c:
            Pn = sb(c, "Pn", [P, NT, N])
            Pns = sb2(c, "Pns", [P, NT, N])
            w_n = sb(c, "w_n", [P, D])
            fc_n = sb(c, "fc_n", [P, D])
            alpha_half = sb(c, "alpha_half", [P, NT])
            diag_col = sb(c, "diag_col", [P, NT])
            d_col = sb(c, "d_col", [P, 1])
            wT = sb(c, "wT", [P, D])
            wTd = sb(c, "wTd", [P, D])
            fcb_all = sb(c, "fcb_all", [P, P])
            Q = sb(c, "Q", [P, STEPS + 1, D])
            M = sb(c, "M", [P, KB, KI, D])
            R = sb(c, "R", [P, KB, KI, D])
            p1 = sb(c, "p1", [P, NT])
            p1s = sb(c, "p1s", [P, NT, 2], f32r)
            p2 = sb(c, "p2", [P, NT])
            p2pair = sb(c, "p2pair", [P, NT, 2])
            s_A = sem(c, "l2_adj_loaded")
            s_w = sem(c, "l2_weights_loaded")
            s_sig = sem(c, "l2_alpha_ready")
            s_v = sem(c, "l2_columns_ready")
            s_Pn = sem(c, "P_rows_ready")
            s_wt = sem(c, "l2_w_transposed")
            s_wts = sem(c, "l2_w_columns_ready")
            s_weff = sem(c, "Q_product_done")
            s_q = sem(c, "Q_power_ready")
            s_F = sem(c, "F_and_r_done")
            s_m = sem(c, "M_terms_added")
            s_PT = sem(c, "P_transposed")
            s_PThi = sem(c, "PT_hi_ready")
            s_PTlo = sem(c, "PT_lo_ready")
            s_Pnhi = sem(c, "Pn_hi_ready")
            s_Pnlo = sem(c, "Pn_lo_ready")
            s_pow = sem(c, "P_power_tile_done")
            s_powhi = sem(c, "P_power_hi_ready")
            s_powlo = sem(c, "P_power_lo_ready")
            s_p1 = sem(c, "p1_ready")
            s_p2 = sem(c, "p2_done")
            s_mhi = sem(c, "M_hi_ready")
            s_b = sem(c, "bias_parts_ready")
            block = c.enter_context(nc.Block())

            def place(j):
                return j % KB, j // KB

            def power(n):
                return (P2T, n) if n < NT else (P3T, n - NT)

            @block.sync
            def _(sp):
                sp.dma_start(Pn[:], d["adj"].rearrange("(t p) n -> p t n", p=P)).then_inc(s_A, 16)
                sp.dma_start(w_n[:], d["L2_gnn_w"]).then_inc(s_w, 16)
                sp.dma_start(fc_n[:], d["L2_gnn_fc_in_w"]).then_inc(s_w, 16)

            @block.scalar
            def _(act):
                a = rows["alpha"][0]
                nc.scalar.activation(alpha_half[:], vec[:, a:a + NT], ACT.Sigmoid).then_inc(s_sig, 1)
                act.wait_ge(s_Pn, NT + 1)
                for t in range(NT):
                    nc.scalar.activation(Pns[0][:, t], Pn[:, t], ACT.Copy).then_inc(s_Pnhi, 1)
                for u in range(NT):
                    act.wait_ge(s_PT, u + 1)
                    nc.scalar.activation(PT[0][:, u], bank[u][:], ACT.Copy).then_inc(s_PThi, 1)
                for n in range(2 * NT):
                    act.wait_ge(s_pow, n + 1)
                    m, u = power(n)
                    nc.scalar.activation(m[0][:, u], bank[u][:], ACT.Copy).then_inc(s_powhi, 1)
                act.wait_ge(s_m, STEPS + 1)
                nc.scalar.activation(Ms[0][:], M[:], ACT.Copy).then_inc(s_mhi, 1)

            @block.tensor
            def _(pe):
                pe.wait_ge(s_w, 32)
                nc.tensor.transpose(bank[4][:, 0:D], w_n[:], ident[:]).then_inc(s_wt, 1)
                pe.wait_ge(s_wts, 2)
                nc.tensor.matmul(bank[4][:, 0:D], wTd[:], wT[:], start=True, stop=True).then_inc(s_weff, 1)
                pe.wait_ge(s_Pn, NT + 1)
                for u in range(NT):
                    for t in range(NT):
                        last = nc.tensor.transpose(bank[u][:, t * P:(t + 1) * P], Pn[:, t, u * P:(u + 1) * P], ident[:])
                    last.then_inc(s_PT, 1)
                for i in range(STEPS + 1):
                    pe.wait_ge(s_q, i + 1)
                    if i >= 2:
                        pe.wait_ge(s_m, i - 1)
                    fr = bank[5 + i % 2]
                    nc.tensor.matmul(fr[:, 0:D], fc_n[:], Q[:, i], start=True, stop=True)
                    nc.tensor.matmul(fr[:, D:2 * D], fcb_all[:], Q[:, i], start=True, stop=True).then_inc(s_F, 1)
                    if 1 <= i < STEPS:
                        nc.tensor.matmul(bank[4][:, 0:D], Q[:, i], Q[:, 1], start=True, stop=True).then_inc(s_weff, 1)
                    if i >= 1:
                        n = i - 1
                        if n == 0:
                            pe.wait_ge(s_PTlo, NT)
                            pe.wait_ge(s_Pnlo, NT)
                        if n == NT:
                            pe.wait_ge(s_powlo, NT)
                        rhs = PT if n < NT else P2T
                        u = n % NT
                        for k in range(NT):
                            last = products(bank[u][:], (Pns[0][:, k, u * P:(u + 1) * P], Pns[1][:, k, u * P:(u + 1) * P]),
                                            (rhs[0][:, k], rhs[1][:, k]), k == 0, k == NT - 1)
                        last.then_inc(s_pow, 1)
                pe.wait_ge(s_p1, 3)
                for t in range(NT):
                    for m in range(NT):
                        for part in range(2):
                            last = nc.tensor.matmul(bank[7][:, 2 * t:2 * t + 2], PT[part][:, m, t * P:(t + 1) * P], p1s[:, m],
                                                    start=(m == 0 and part == 0), stop=(m == NT - 1 and part == 1))
                last.then_inc(s_p2, 1)

            @block.vector
            def _(dve):
                nc.vector.tensor_scalar(fcb_all[:], ones[:], col("fcb"), None, ALU.mult)
                nc.vector.tensor_copy(Q[:, 0], ident[:]).then_inc(s_q, 1)
                nc.vector.tensor_scalar(d_col[:], col("d"), 0.0, 1.0, ALU.max, ALU.min).then_inc(s_v, 1)
                dve.wait_ge(s_sig, 1)
                nc.vector.tensor_scalar(alpha_half[:], alpha_half[:], 0.5 * DT, None, ALU.mult).then_inc(s_v, 1)
                dve.wait_ge(s_v, 2)
                nc.vector.tensor_scalar(diag_col[:], alpha_half[:], -1.0, 1.0 - DT, ALU.mult, ALU.add).then_inc(s_v, 1)
                dve.wait_ge(s_wt, 1)
                nc.vector.tensor_copy(wT[:], bank[4][:, 0:D]).then_inc(s_wts, 1)
                nc.vector.tensor_scalar(wTd[:], bank[4][:, 0:D], d_col[:], None, ALU.mult).then_inc(s_wts, 1)
                dve.wait_ge(s_A, 16)
                for t in range(NT):
                    nc.vector.tensor_scalar(Pn[:, t], Pn[:, t], alpha_half[:, t:t + 1], None, ALU.mult).then_inc(s_Pn, 1)
                dve.wait_ge(s_Pn, NT)
                dve.wait_ge(s_v, 3)
                for t in range(NT):
                    blk = Pn[:, t, t * P:(t + 1) * P]
                    last = nc.vector.scalar_tensor_tensor(out=blk, in0=ident[:], scalar=diag_col[:, t:t + 1], in1=blk,
                                                          op0=ALU.mult, op1=ALU.add)
                last.then_inc(s_Pn, 1)
                dve.wait_ge(s_weff, 1)
                nc.vector.tensor_scalar(Q[:, 1], bank[4][:, 0:D], DT, None, ALU.mult).then_inc(s_q, 1)
                dve.wait_ge(s_Pn, NT + 1)
                nc.vector.tensor_reduce(p1[:], Pn[:], AX.X, ALU.add).then_inc(s_p1, 1)
                dve.wait_ge(s_p1, 1)
                nc.vector.tensor_copy(p1s[:, :, 0], p1[:]).then_inc(s_p1, 1)
                dve.wait_ge(s_p1, 2)
                nc.vector.tensor_tensor(p1s[:, :, 1], p1[:], as_f32(p1s[:, :, 0]), ALU.subtract).then_inc(s_p1, 1)
                for t in range(NT):
                    dve.wait_ge(s_Pnhi, t + 1)
                    nc.vector.tensor_tensor(Pns[1][:, t], Pn[:, t], as_f32(Pns[0][:, t]), ALU.subtract).then_inc(s_Pnlo, 1)
                for u in range(NT):
                    dve.wait_ge(s_PThi, u + 1)
                    nc.vector.tensor_tensor(PT[1][:, u], bank[u][:], as_f32(PT[0][:, u]), ALU.subtract).then_inc(s_PTlo, 1)
                for i in range(STEPS + 1):
                    if 1 <= i < STEPS:
                        dve.wait_ge(s_weff, i + 1)
                        nc.vector.tensor_copy(Q[:, i + 1], bank[4][:, 0:D]).then_inc(s_q, 1)
                    dve.wait_ge(s_q, i + 1)
                    if i >= 1:
                        dve.wait_ge(s_m, i)
                    dve.wait_ge(s_F, i + 1)
                    for j in range(STEPS - i):
                        k, o = place(j)
                        if i == 0:
                            nc.vector.tensor_scalar(M[:, k, o], Q[:, 0], DT, None, ALU.mult)
                        else:
                            nc.vector.scalar_tensor_tensor(out=M[:, k, o], in0=Q[:, i], scalar=DT * comb(i + j, j), in1=M[:, k, o],
                                                           op0=ALU.mult, op1=ALU.add)
                    j = STEPS - i
                    k, o = place(j)
                    fr = bank[5 + i % 2]
                    if i == 0:
                        nc.vector.tensor_copy(M[:, k, o], fr[:, 0:D])
                    else:
                        nc.vector.scalar_tensor_tensor(out=M[:, k, o], in0=fr[:, 0:D], scalar=float(comb(STEPS, j)), in1=M[:, k, o],
                                                       op0=ALU.mult, op1=ALU.add)
                    nc.vector.tensor_scalar(R[:, k, o], fr[:, D:2 * D], float(comb(STEPS, j)), None, ALU.mult).then_inc(s_m, 1)
                    if i >= 1:
                        n = i - 1
                        dve.wait_ge(s_powhi, n + 1)
                        m, u = power(n)
                        nc.vector.tensor_tensor(m[1][:, u], bank[u][:], as_f32(m[0][:, u]), ALU.subtract).then_inc(s_powlo, 1)
                dve.wait_ge(s_mhi, 1)
                nc.vector.tensor_tensor(Ms[1][:], M[:], as_f32(Ms[0][:]), ALU.subtract)
                dve.wait_ge(s_p2, 1)
                nc.vector.tensor_copy(p2pair[:].rearrange("p t a -> p (t a)"), bank[7][:, 0:2 * NT]).then_inc(s_b, 1)
                dve.wait_ge(s_b, 1)
                nc.vector.tensor_tensor(p2[:], p2pair[:, :, 0], p2pair[:, :, 1], ALU.add).then_inc(s_b, 1)
                dve.wait_ge(s_m, STEPS + 1)
                for t in range(NT):
                    last = nc.vector.scalar_tensor_tensor(out=bias_w[:, t], in0=R[:, 1], scalar=p1[:, t:t + 1], in1=R[:, 0],
                                                          op0=ALU.mult, op1=ALU.add)
                last.then_inc(s_b, 1)
                dve.wait_ge(s_b, 3)
                for t in range(NT):
                    nc.vector.scalar_tensor_tensor(out=bias_w[:, t], in0=R[:, 2], scalar=p2[:, t:t + 1], in1=bias_w[:, t],
                                                   op0=ALU.mult, op1=ALU.add)

        with stage() as c:
            Y = [[sb2(c, f"Y{k}_{s}", [P, N]) for k in range(KB)] for s in range(2)]
            WF = sb(c, "WF", [P, KI, 4, NT, D])
            Z = sb2(c, "Z", [P, 4, NT, D])
            Z1 = sb2(c, "Z1", [P, 4, NT, D])
            ln = LN(c, "l2")
            s_y = sem(c, "l2_y_done")
            s_yhi = sem(c, "l2_y_hi_ready")
            s_ylo = sem(c, "l2_y_lo_ready")
            s_w = sem(c, "l2_w_done")
            s_we = sem(c, "l2_w_ready")
            s_zhi = sem(c, "l2_z_hi_ready")
            s_z = sem(c, "l2_z_lo_ready")
            s_wx = sem(c, "l2_residual_added")
            s_r1 = sem(c, "l2_first_round_done")
            s_t1 = sem(c, "l2_z1_sum_ready")
            s_z1hi = sem(c, "l2_z1_hi_ready")
            s_z1 = sem(c, "l2_z1_lo_ready")
            s_r2 = sem(c, "l2_second_round_done")
            s_xo = sem(c, "l2_x_ready")
            block = c.enter_context(nc.Block())

            @block.tensor
            def _(pe):
                def y(q, s):
                    pe.wait_ge(ln.ready[s], q + 2)
                    for t in range(NT):
                        out = bank[3 * s][:, t * P:(t + 1) * P]
                        nc.tensor.matmul(out, HN[s][0][:, t], ident_r[:], start=True, stop=False)
                        last = nc.tensor.matmul(out, HN[s][1][:, t], ident_r[:], start=False, stop=True)
                    last.then_inc(s_y, 1)
                    aggregate(bank[3 * s + 1][:], HN[s], PT).then_inc(s_y, 1)
                    aggregate(bank[3 * s + 2][:], HN[s], P2T).then_inc(s_y, 1)

                def w(q, s):
                    b = 2 * q + s
                    pe.wait_ge(s_ylo, KB * b + KB)
                    for t in range(NT):
                        cols = slice(t * P, (t + 1) * P)
                        pe.wait_ge(s_we, NT * b + t + 1)
                        for k in range(KB):
                            last = products(bank[6 + t % 2][:, 0:KI * D], (Y[s][k][0][:, cols], Y[s][k][1][:, cols]),
                                            (Ms[0][:, k].rearrange("p i d -> p (i d)"), Ms[1][:, k].rearrange("p i d -> p (i d)")),
                                            k == 0, k == KB - 1)
                        last.then_inc(s_w, 1)

                def apply_cube(t, z):
                    for m in range(NT):
                        last = products(bank[6 + t % 2][:].rearrange("p (b f) -> p b f", b=4),
                                        (P3T[0][:, m, t * P:(t + 1) * P], P3T[1][:, m, t * P:(t + 1) * P]),
                                        (z[0][:, :, m], z[1][:, :, m]), m == 0, m == NT - 1)
                    return last

                def quad(g, more):
                    pe.wait_ge(s_xo, NT * g + 1)
                    w(2 * g, 0)
                    y(2 * g + 1, 0)
                    w(2 * g, 1)
                    y(2 * g + 1, 1)
                    w(2 * g + 1, 0)
                    w(2 * g + 1, 1)
                    if more:
                        y(2 * g + 2, 0)
                    pe.wait_ge(s_z, 4 * g + 4)
                    for t in range(NT):
                        if t >= 2:
                            pe.wait_ge(s_t1, NT * g + t - 1)
                        apply_cube(t, Z).then_inc(s_r1, 1)
                    if more:
                        y(2 * g + 2, 1)
                    pe.wait_ge(s_z1, NT * g + NT)
                    for t in range(NT):
                        if t >= 2:
                            pe.wait_ge(s_xo, NT * g + t)
                        apply_cube(t, Z1).then_inc(s_r2, 1)

                y(0, 0)
                y(0, 1)
                with pe.Fori(0, QUADS - 1) as g:
                    quad(g, True)
                quad(QUADS - 1, False)

            @block.scalar
            def _(act):
                def y_hi(q, s):
                    for k in range(KB):
                        act.wait_ge(s_y, KB * (2 * q + s) + k + 1)
                        if k == 0 and (not isinstance(q, int) or q > 0):
                            act.wait_ge(s_w, NT * (2 * q + s - 1))
                        nc.scalar.activation(Y[s][k][0][:], bank[3 * s + k][:], ACT.Copy).then_inc(s_yhi, 1)

                def z_hi(q, s, h):
                    act.wait_ge(s_we, 2 + NT * (2 * q + s) + NT)
                    nc.scalar.activation(Z[0][:, 2 * h + s], WF[:, KI - 1, 2 * h + s], ACT.Copy).then_inc(s_zhi, 1)

                def quad(g, more):
                    for h in range(2):
                        q = 2 * g + h
                        if more:
                            ln_std(act, ln, q + 2)
                        if h == 0:
                            z_hi(q, 0, h)
                            y_hi(q + 1, 0)
                            z_hi(q, 1, h)
                        if more:
                            ln_apply(act, ln, 0, q + 2)
                            ln_apply(act, ln, 1, q + 2)
                        if h == 0:
                            y_hi(q + 1, 1)
                        else:
                            z_hi(q, 0, h)
                            z_hi(q, 1, h)
                            if more:
                                y_hi(q + 1, 0)
                    for t in range(NT):
                        act.wait_ge(s_t1, NT * g + t + 1)
                        nc.scalar.activation(Z1[0][:, :, t], WF[:, 1, :, t], ACT.Copy).then_inc(s_z1hi, 1)
                    if more:
                        y_hi(2 * g + 2, 1)

                ln_std(act, ln, 0)
                ln_apply(act, ln, 0, 0)
                ln_apply(act, ln, 1, 0)
                ln_std(act, ln, 1)
                ln_apply(act, ln, 0, 1)
                y_hi(0, 0)
                ln_apply(act, ln, 1, 1)
                y_hi(0, 1)
                with act.Fori(0, QUADS - 1) as g:
                    quad(g, True)
                quad(QUADS - 1, False)

            @block.gpsimd
            def _(pool):
                def residual(g, j):
                    pool.wait_ge(s_we, 2 + NT * (4 * g + j) + NT)
                    nc.gpsimd.tensor_tensor(WF[:, 0, j].rearrange("p t f -> p (t f)"), WF[:, 0, j].rearrange("p t f -> p (t f)"),
                                            X[:, bass.ds(4 * g + j, 1)].rearrange("p a t f -> p (a t f)"), ALU.add).then_inc(s_wx, 1)

                def quad(g, more):
                    for h in range(2):
                        q = 2 * g + h
                        if h == 0 or more:
                            ln_split(pool, ln, 1, q + 1, s_y, KB * (2 * q + 2))
                        if more:
                            ln_split(pool, ln, 0, q + 2, s_y, KB * (2 * q + 3))
                        residual(g, 2 * h)
                        residual(g, 2 * h + 1)

                for s in range(2):
                    pool.sem_inc(ln.ready[s], 1)
                ln_split(pool, ln, 0, 0)
                ln_split(pool, ln, 1, 0)
                ln_split(pool, ln, 0, 1, s_y, KB)
                with pool.Fori(0, QUADS - 1) as g:
                    quad(g, True)
                quad(QUADS - 1, False)

            @block.vector
            def _(dve):
                def y_lo(q, s):
                    for k in range(KB):
                        dve.wait_ge(s_yhi, KB * (2 * q + s) + k + 1)
                        nc.vector.tensor_tensor(Y[s][k][1][:], bank[3 * s + k][:], as_f32(Y[s][k][0][:]), ALU.subtract).then_inc(s_ylo, 1)

                def w_out(q, s, h):
                    j = 2 * h + s
                    for t in range(NT):
                        dve.wait_ge(s_w, NT * (2 * q + s) + t + 1)
                        nc.vector.tensor_tensor(WF[:, :, j, t], bank[6 + t % 2][:, 0:KI * D].rearrange("p (i f) -> p i f", i=KI),
                                                bias_w[:, t], ALU.add).then_inc(s_we, 1)

                def z_lo(g, j):
                    dve.wait_ge(s_zhi, 4 * g + j + 1)
                    nc.vector.tensor_tensor(Z[1][:, j], WF[:, KI - 1, j], as_f32(Z[0][:, j]), ALU.subtract).then_inc(s_z, 1)

                def quad(g, more):
                    for h in range(2):
                        q = 2 * g + h
                        if more:
                            ln_stats(dve, ln, q + 2)
                            ln_rstd(dve, ln, q + 2)
                        w_out(q, 0, h)
                        z_lo(g, 2 * h)
                        if h == 0:
                            y_lo(q + 1, 0)
                        w_out(q, 1, h)
                        z_lo(g, 2 * h + 1)
                        if h == 0:
                            y_lo(q + 1, 1)
                        elif more:
                            y_lo(q + 1, 0)
                    for t in range(NT):
                        dve.wait_ge(s_r1, NT * g + t + 1)
                        nc.vector.tensor_tensor(WF[:, 1, :, t], bank[6 + t % 2][:].rearrange("p (b f) -> p b f", b=4), WF[:, 1, :, t],
                                                ALU.add).then_inc(s_t1, 1)
                        dve.wait_ge(s_z1hi, NT * g + t + 1)
                        nc.vector.tensor_tensor(Z1[1][:, :, t], WF[:, 1, :, t], as_f32(Z1[0][:, :, t]), ALU.subtract).then_inc(s_z1, 1)
                    if more:
                        y_lo(2 * g + 2, 1)
                    dve.wait_ge(s_wx, 4 * g + 4)
                    for t in range(NT):
                        dve.wait_ge(s_r2, NT * g + t + 1)
                        nc.vector.tensor_tensor(X[:, bass.ds(4 * g, 4), t], bank[6 + t % 2][:].rearrange("p (b f) -> p b f", b=4),
                                                WF[:, 0, :, t], ALU.add).then_inc(s_xo, 1)

                dve.sem_inc(s_we, 2)
                dve.sem_inc(s_xo, 1)
                ln_stats(dve, ln, 0)
                ln_rstd(dve, ln, 0)
                ln_stats(dve, ln, 1)
                ln_rstd(dve, ln, 1)
                y_lo(0, 0)
                y_lo(0, 1)
                with dve.Fori(0, QUADS - 1) as g:
                    quad(g, True)
                quad(QUADS - 1, False)
        l2.close()

        WqT = sb2(top, "WqT", [P, NT, N])
        W1s = sb2(top, "W1s", [P, H3A * P])
        W2s = sb2(top, "W2s", [P, H3A, H3B * P])
        W3s = sb2(top, "W3s", [P, H3B, D])
        with stage() as c:
            A3 = sb(c, "A3", [P, NT, N])
            w1f = sb(c, "w1f", [P, H3A * P])
            w2f = sb(c, "w2f", [P, H3A, H3B * P])
            w3f = sb(c, "w3f", [P, H3B, D])
            s_A = sem(c, "l3_adj_loaded")
            s_w = sem(c, "l3_weights_loaded")
            s_sq = sem(c, "l3_adj_squared")
            s_whi = sem(c, "l3_weights_hi_ready")
            s_T = sem(c, "l3_matrix_transposed")
            s_hi = sem(c, "l3_matrix_hi_ready")
            block = c.enter_context(nc.Block())

            @block.sync
            def _(sp):
                sp.dma_start(A3[:], d["adj"].rearrange("(t p) n -> p t n", p=P)).then_inc(s_A, 16)
                sp.dma_start(w1f[:], d["L3_gnn_W1"]).then_inc(s_w, 16)
                sp.dma_start(w2f[:], d["L3_gnn_W2"].rearrange("(t p) n -> p t n", p=P)).then_inc(s_w, 16)
                sp.dma_start(w3f[:], d["L3_gnn_W3"].rearrange("(t p) n -> p t n", p=P)).then_inc(s_w, 16)

            @block.tensor
            def _(pe):
                pe.wait_ge(s_sq, NT)
                for u in range(NT):
                    for t in range(NT):
                        last = nc.tensor.transpose(bank[u][:, t * P:(t + 1) * P], A3[:, t, u * P:(u + 1) * P], ident[:])
                    last.then_inc(s_T, 1)

            @block.scalar
            def _(act):
                act.wait_ge(s_w, 48)
                nc.scalar.activation(W1s[0][:], w1f[:], ACT.Copy).then_inc(s_whi, 1)
                nc.scalar.activation(W2s[0][:], w2f[:], ACT.Copy).then_inc(s_whi, 1)
                nc.scalar.activation(W3s[0][:], w3f[:], ACT.Copy).then_inc(s_whi, 1)
                for u in range(NT):
                    act.wait_ge(s_T, u + 1)
                    nc.scalar.activation(WqT[0][:, u], bank[u][:], ACT.Copy).then_inc(s_hi, 1)

            @block.vector
            def _(dve):
                dve.wait_ge(s_A, 16)
                for t in range(NT):
                    nc.vector.tensor_tensor(A3[:, t], A3[:, t], A3[:, t], ALU.mult).then_inc(s_sq, 1)
                dve.wait_ge(s_whi, 3)
                nc.vector.tensor_tensor(W1s[1][:], w1f[:], as_f32(W1s[0][:]), ALU.subtract)
                nc.vector.tensor_tensor(W2s[1][:], w2f[:], as_f32(W2s[0][:]), ALU.subtract)
                nc.vector.tensor_tensor(W3s[1][:], w3f[:], as_f32(W3s[0][:]), ALU.subtract)
                for u in range(NT):
                    dve.wait_ge(s_hi, u + 1)
                    nc.vector.tensor_tensor(WqT[1][:, u], bank[u][:], as_f32(WqT[0][:, u]), ALU.subtract)

        with stage() as c:
            U1 = [sb2(c, f"U1_{s}", [P, N]) for s in range(2)]
            GH = [sb2(c, f"GH_{s}", [P, NT, H3A * P]) for s in range(2)]
            U2 = [sb2(c, f"U2_{s}", [P, H3A, N]) for s in range(2)]
            H2 = [sb2(c, f"H2_{s}", [P, H3B, N]) for s in range(2)]
            S3T = [sb(c, f"S3T_{s}", [P, N]) for s in range(2)]
            S3 = sb2(c, "S3", [P, 4, NT, D])
            ln = LN(c, "l3")
            s_u1 = sem(c, "l3_u1_done")
            s_u1hi = sem(c, "l3_u1_hi_ready")
            s_u1lo = sem(c, "l3_u1_lo_ready")
            s_h1 = sem(c, "l3_h1_done")
            s_h1hi = sem(c, "l3_h1_hi_ready")
            s_h1lo = sem(c, "l3_h1_lo_ready")
            s_u2 = sem(c, "l3_u2_done")
            s_u2hi = sem(c, "l3_u2_hi_ready")
            s_u2lo = sem(c, "l3_u2_lo_ready")
            s_h2 = sem(c, "l3_h2_done")
            s_h2hi = sem(c, "l3_h2_hi_ready")
            s_h2lo = sem(c, "l3_h2_lo_ready")
            s_s3 = sem(c, "l3_s3_done")
            s_s3c = sem(c, "l3_s3_copied")
            s_tr = sem(c, "l3_s3_transposed")
            s_s3hi = sem(c, "l3_s3_hi_ready")
            s_s3lo = sem(c, "l3_s3_lo_ready")
            s_f = sem(c, "l3_final_sum_done")
            s_fo = sem(c, "l3_x_ready")
            s_out = sem(c, "out_stored")
            block = c.enter_context(nc.Block())
            HB = 2
            FBANK = (3, 0)
            U2BANK = (3, 0)
            H2BANK = (1, 2, 3, 0)

            def split_cols(x, sl):
                return x[0][:, sl], x[1][:, sl]

            @block.tensor
            def _(pe):
                def u1(q, s):
                    pe.wait_ge(ln.ready[s], q + 2)
                    aggregate(bank[4 * s][:], HN[s], WqT).then_inc(s_u1, 1)

                def h1(q, s):
                    pe.wait_ge(s_u1lo, 2 * q + s + 1)
                    pe.wait_ge(s_s3lo, 2 * q + s + 1)
                    for t in range(NT):
                        out = bank[4 * s + 1 + t // 2][:, (t % 2) * H3A * P:(t % 2 + 1) * H3A * P]
                        last = products(out, split_cols(U1[s], slice(t * P, (t + 1) * P)), (W1s[0][:], W1s[1][:]), True, True)
                        if t % 2 == 1:
                            last.then_inc(s_h1, 1)

                def u2(q, s):
                    pe.wait_ge(s_h1lo, HB * (2 * q + s) + HB)
                    for f in range(H3A):
                        for m in range(NT):
                            last = products(bank[4 * s + U2BANK[f]][:], (GH[s][0][:, m, f * P:(f + 1) * P], GH[s][1][:, m, f * P:(f + 1) * P]),
                                            (WqT[0][:, m], WqT[1][:, m]), m == 0, m == NT - 1)
                        last.then_inc(s_u2, 1)

                def h2(q, s):
                    pe.wait_ge(s_u2lo, H3A * (2 * q + s) + H3A)
                    for o in range(H3B):
                        for f in range(H3A):
                            last = products(bank[4 * s + H2BANK[o]][:], (W2s[0][:, f, o * P:(o + 1) * P], W2s[1][:, f, o * P:(o + 1) * P]),
                                            (U2[s][0][:, f], U2[s][1][:, f]), f == 0, f == H3A - 1)
                        last.then_inc(s_h2, 1)

                def s3(q, s):
                    for k in range(H3B):
                        pe.wait_ge(s_h2lo, H3B * (2 * q + s) + k + 1)
                        last = products(bank[4 * s + 1][:], (W3s[0][:, k], W3s[1][:, k]), (H2[s][0][:, k], H2[s][1][:, k]),
                                        k == 0, k == H3B - 1)
                    last.then_inc(s_s3, 1)

                def turn(q, s):
                    pe.wait_ge(s_s3c, 2 * q + s + 1)
                    for t in range(NT):
                        last = nc.tensor.transpose(bank[4 * s + 2][:, t * P:(t + 1) * P], S3T[s][:, t * P:(t + 1) * P], ident[:])
                    last.then_inc(s_tr, 1)

                def pair(q, more):
                    h1(q, 0)
                    if more:
                        pe.wait_ge(s_u1lo, 2 * q + 1)
                        u1(q + 1, 0)
                    h1(q, 1)
                    if more:
                        pe.wait_ge(s_u1lo, 2 * q + 3)
                    u2(q, 0)
                    u2(q, 1)
                    h2(q, 0)
                    h2(q, 1)
                    s3(q, 0)
                    s3(q, 1)
                    turn(q, 0)
                    if more:
                        u1(q + 1, 1)
                    turn(q, 1)

                def quad(g, more):
                    pe.wait_ge(s_fo, NT * g + 1)
                    pair(2 * g, True)
                    pair(2 * g + 1, more)
                    pe.wait_ge(s_s3lo, 2 + 4 * g + 4)
                    for t in range(NT):
                        if t >= 2:
                            pe.wait_ge(s_fo, NT * g + t)
                        for m in range(NT):
                            last = products(bank[FBANK[t % 2]][:].rearrange("p (b f) -> p b f", b=4),
                                            (WqT[0][:, m, t * P:(t + 1) * P], WqT[1][:, m, t * P:(t + 1) * P]),
                                            (S3[0][:, :, m], S3[1][:, :, m]), m == 0, m == NT - 1)
                        last.then_inc(s_f, 1)

                u1(0, 0)
                u1(0, 1)
                with pe.Fori(0, QUADS - 1) as g:
                    quad(g, True)
                quad(QUADS - 1, False)

            @block.scalar
            def _(act):
                def u1_hi(q, s):
                    act.wait_ge(s_u1, 2 * q + s + 1)
                    if not isinstance(q, int) or q > 0:
                        act.wait_ge(s_h1, HB * (2 * q + s - 1))
                    nc.scalar.activation(U1[s][0][:], bank[4 * s][:], ACT.Copy).then_inc(s_u1hi, 1)

                def h1_hi(q, s):
                    for n in range(HB):
                        act.wait_ge(s_h1, HB * (2 * q + s) + n + 1)
                        nc.scalar.activation(GH[s][0][:, 2 * n:2 * n + 2], bank[4 * s + 1 + n][:].rearrange("p (t f) -> p t f", t=2),
                                             ACT.Relu).then_inc(s_h1hi, 1)

                def u2_hi(q, s):
                    for f in range(H3A):
                        act.wait_ge(s_u2, H3A * (2 * q + s) + f + 1)
                        nc.scalar.activation(U2[s][0][:, f], bank[4 * s + U2BANK[f]][:], ACT.Copy).then_inc(s_u2hi, 1)

                def h2_hi(q, s):
                    for o in range(H3B):
                        act.wait_ge(s_h2, H3B * (2 * q + s) + o + 1)
                        nc.scalar.activation(H2[s][0][:, o], bank[4 * s + H2BANK[o]][:], ACT.Relu).then_inc(s_h2hi, 1)

                def s3_copy(q, s):
                    act.wait_ge(s_s3, 2 * q + s + 1)
                    nc.scalar.activation(S3T[s][:], bank[4 * s + 1][:], ACT.Copy).then_inc(s_s3c, 1)

                def s3_hi(q, s, h):
                    act.wait_ge(s_tr, 2 * q + s + 1)
                    nc.scalar.activation(S3[0][:, 2 * h + s].rearrange("p t f -> p (t f)"), bank[4 * s + 2][:], ACT.Copy).then_inc(s_s3hi, 1)

                def pair(q, h, more, more2):
                    h1_hi(q, 0)
                    if more:
                        u1_hi(q + 1, 0)
                    h1_hi(q, 1)
                    if more2:
                        ln_std(act, ln, q + 2)
                    u2_hi(q, 0)
                    if more2:
                        ln_apply(act, ln, 0, q + 2)
                    u2_hi(q, 1)
                    h2_hi(q, 0)
                    if more2:
                        ln_apply(act, ln, 1, q + 2)
                    h2_hi(q, 1)
                    s3_copy(q, 0)
                    s3_copy(q, 1)
                    s3_hi(q, 0, h)
                    if more:
                        u1_hi(q + 1, 1)
                    s3_hi(q, 1, h)

                ln_std(act, ln, 0)
                ln_apply(act, ln, 0, 0)
                ln_apply(act, ln, 1, 0)
                ln_std(act, ln, 1)
                ln_apply(act, ln, 0, 1)
                u1_hi(0, 0)
                ln_apply(act, ln, 1, 1)
                u1_hi(0, 1)
                with act.Fori(0, QUADS - 1) as g:
                    pair(2 * g, 0, True, True)
                    pair(2 * g + 1, 1, True, True)
                pair(PAIRS - 2, 0, True, False)
                pair(PAIRS - 1, 1, False, False)

            @block.gpsimd
            def _(pool):
                ln_split_all(pool, ln, s_u1)

            @block.vector
            def _(dve):
                def u1_lo(q, s):
                    dve.wait_ge(s_u1hi, 2 * q + s + 1)
                    nc.vector.tensor_tensor(U1[s][1][:], bank[4 * s][:], as_f32(U1[s][0][:]), ALU.subtract).then_inc(s_u1lo, 1)

                def h1_lo(q, s):
                    for n in range(HB):
                        dve.wait_ge(s_h1hi, HB * (2 * q + s) + n + 1)
                        nc.vector.scalar_tensor_tensor(out=GH[s][1][:, 2 * n:2 * n + 2], in0=bank[4 * s + 1 + n][:].rearrange("p (t f) -> p t f", t=2),
                                                       scalar=0.0, in1=as_f32(GH[s][0][:, 2 * n:2 * n + 2]), op0=ALU.max, op1=ALU.subtract).then_inc(s_h1lo, 1)

                def u2_lo(q, s):
                    for f in range(H3A):
                        dve.wait_ge(s_u2hi, H3A * (2 * q + s) + f + 1)
                        nc.vector.tensor_tensor(U2[s][1][:, f], bank[4 * s + U2BANK[f]][:], as_f32(U2[s][0][:, f]), ALU.subtract).then_inc(s_u2lo, 1)

                def h2_lo(q, s):
                    for o in range(H3B):
                        dve.wait_ge(s_h2hi, H3B * (2 * q + s) + o + 1)
                        nc.vector.scalar_tensor_tensor(out=H2[s][1][:, o], in0=bank[4 * s + H2BANK[o]][:], scalar=0.0,
                                                       in1=as_f32(H2[s][0][:, o]), op0=ALU.max, op1=ALU.subtract).then_inc(s_h2lo, 1)

                def s3_lo(q, s, h):
                    dve.wait_ge(s_s3hi, 2 * q + s + 1)
                    nc.vector.tensor_tensor(S3[1][:, 2 * h + s].rearrange("p t f -> p (t f)"), bank[4 * s + 2][:],
                                            as_f32(S3[0][:, 2 * h + s]).rearrange("p t f -> p (t f)"), ALU.subtract).then_inc(s_s3lo, 1)

                def pair(q, h, more, more2):
                    h1_lo(q, 0)
                    if more:
                        u1_lo(q + 1, 0)
                    h1_lo(q, 1)
                    if more2:
                        ln_stats(dve, ln, q + 2)
                        ln_rstd(dve, ln, q + 2)
                    u2_lo(q, 0)
                    u2_lo(q, 1)
                    h2_lo(q, 0)
                    h2_lo(q, 1)
                    s3_lo(q, 0, h)
                    if more:
                        u1_lo(q + 1, 1)
                    s3_lo(q, 1, h)

                def final(g):
                    for t in range(NT):
                        dve.wait_ge(s_f, NT * g + t + 1)
                        xt = X[:, bass.ds(4 * g, 4), t]
                        nc.vector.tensor_tensor(xt, bank[FBANK[t % 2]][:].rearrange("p (b f) -> p b f", b=4), xt, ALU.add).then_inc(s_fo, 1)

                dve.sem_inc(s_fo, 1)
                dve.sem_inc(s_s3lo, 2)
                ln_stats(dve, ln, 0)
                ln_rstd(dve, ln, 0)
                ln_stats(dve, ln, 1)
                ln_rstd(dve, ln, 1)
                u1_lo(0, 0)
                u1_lo(0, 1)
                with dve.Fori(0, QUADS - 1) as g:
                    pair(2 * g, 0, True, True)
                    pair(2 * g + 1, 1, True, True)
                    final(g)
                pair(PAIRS - 2, 0, True, False)
                pair(PAIRS - 1, 1, False, False)
                final(QUADS - 1)

            @block.sync
            def _(sp):
                with sp.Fori(0, QUADS) as g:
                    for j in range(4):
                        if j == 0:
                            sp.wait_ge(s_fo, 1 + NT * g + NT)
                        sp.dma_start(d["out"][bass.ds(4 * g + j, 1)].rearrange("a (t p) f -> p (a t) f", p=P),
                                     X[:, bass.ds(4 * g + j, 1)].rearrange("p a t f -> p (a t) f")).then_inc(s_out, 16)
                sp.wait_ge(s_out, 16 * B)


def kernel(**inputs):
    import concourse.bacc as bacc
    from concourse import mybir
    from concourse.bass_utils import run_bass_kernel_spmd

    nc = bacc.Bacc("TRN2", target_bir_lowering=False, num_devices=1)
    arrays, aps = {}, {}
    for name, a in inputs.items():
        a = np.ascontiguousarray(a)
        arrays[name + "_dram"] = a
        aps[name] = nc.dram_tensor(name + "_dram", a.shape, mybir.dt.from_np(a.dtype), kind="ExternalInput").ap()
    aps["out"] = nc.dram_tensor("out_dram", inputs["x"].shape, mybir.dt.float32, kind="ExternalOutput").ap()
    graph_stack_kernel(nc, aps)
    r = run_bass_kernel_spmd(nc, [arrays], core_ids=[0])
    return r.results[0]["out_dram"]
```

```python
import numpy as np


def graph_stack_kernel(nc, d):
    import concourse.bass as bass
    from concourse import mybir
    from concourse.alu_op_type import AluOpType as ALU
    from contextlib import ExitStack, contextmanager
    from math import comb

    ACT = mybir.ActivationFunctionType
    AX = mybir.AxisListType
    f32, f32r = mybir.dt.float32, mybir.dt.float32r

    B, N, D = d["x"].shape
    P = 128
    NT = N // P
    C1 = d["L0_gnn_W1"].shape[0] // P
    H3A = d["L3_gnn_W1"].shape[1] // P
    H3B = d["L3_gnn_W2"].shape[1] // P
    SKIPS = d["L1_gnn_Wih"].shape[0]
    GATES = 4
    EPS = 1e-5
    STEPS = 8
    DT = 1.0 / STEPS
    PAIRS = B // 2
    QUADS = B // 4
    I_, F_, G_, O_ = range(GATES)

    rows = {}
    at = 0
    for name, n in (("bih", 4 * SKIPS), ("bhh", 4 * SKIPS), ("b1", C1), ("g1", C1), ("be1", C1), ("b2", 1),
                    ("g2", 1), ("be2", 1), ("bg1", 1), ("alpha", NT), ("d", 1), ("fcb", 1)):
        rows[name] = (at, n)
        at += n
    NVEC = at

    def as_f32(ap):
        return ap.bitcast(f32)

    def products(out, w, m, first, last):
        nc.tensor.matmul(out, w[0], m[0], start=first, stop=False)
        nc.tensor.matmul(out, w[0], m[1], start=False, stop=False)
        return nc.tensor.matmul(out, w[1], m[0], start=False, stop=last)

    with ExitStack() as top:
        def sb(ctx, name, shape, dt=f32):
            return ctx.enter_context(nc.sbuf_tensor(name, shape, dt))

        def sb2(ctx, name, shape):
            return sb(ctx, name + "_hi", shape, f32r), sb(ctx, name + "_lo", shape, f32r)

        in_stage = []
        windows = [sorted(nc.free_semaphores)[38 * n:38 * (n + 1)] for n in range(4)]

        def sem(ctx, name):
            in_stage.append(nc.alloc_semaphore(name=name, num=windows[0][len(in_stage)]))
            return in_stage[-1]

        @contextmanager
        def stage():
            with ExitStack() as ctx:
                yield ctx
            nc.clear_and_free_semaphores(in_stage)
            in_stage.clear()
            windows.append(windows.pop(0))

        bank = [top.enter_context(nc.psum_tensor(f"bank{i}", [P, 512], f32)) for i in range(8)]

        X = sb(top, "X", [P, B, NT, D])
        adj = sb(top, "adj", [P, NT, N])
        w_n = sb(top, "w_n", [P, D])
        fc_n = sb(top, "fc_n", [P, D])
        ident = sb(top, "ident", [P, P])
        ones = sb(top, "ones", [P, P])
        ones_r = sb(top, "ones_r", [P, P], f32r)
        vec = sb(top, "vec", [P, NVEC])
        lstm_bias = sb(top, "lstm_bias", [P, 4 * SKIPS])
        eps_col = sb(top, "eps_col", [P, 1])
        stats = sb(top, "stats", [P, 2, NT, 6])
        mv = sb(top, "mv", [P, 2, NT, 2])
        std = sb(top, "std", [P, 2, NT])
        rstd = sb(top, "rstd", [P, 2, NT])
        shift = sb(top, "shift", [P, 2, NT])
        XN = [sb(top, f"XN{s}", [P, NT, D]) for s in range(2)]
        HN = [sb2(top, f"HN{s}", [P, NT, D]) for s in range(2)]

        def col(name, i=0):
            a, n = rows[name]
            return vec[:, a + i:a + i + 1]

        last_three = sorted(nc.free_semaphores)[-3:]
        s_passed = [(nc.scalar, nc.alloc_semaphore(name="act_waits_passed", num=last_three[0])),
                    (nc.vector, nc.alloc_semaphore(name="dve_waits_passed", num=last_three[1])),
                    (nc.gpsimd, nc.alloc_semaphore(name="pool_waits_passed", num=last_three[2]))]

        def wait_apart(eng, semaphore, value):
            eng.wait_ge(semaphore, value)
            for engine, passed in s_passed:
                if engine is eng:
                    eng.sem_inc(passed, 1)

        class LN:
            def __init__(self, ctx, tag):
                self.stats_ready = sem(ctx, tag + "_ln_stats_ready")
                self.mv_ready = sem(ctx, tag + "_ln_mv_ready")
                self.std_ready = sem(ctx, tag + "_ln_std_ready")
                self.rstd_ready = sem(ctx, tag + "_ln_rstd_ready")
                self.xn_ready = [sem(ctx, f"{tag}_ln_xn_ready_{s}") for s in range(2)]
                self.hi_ready = [sem(ctx, f"{tag}_ln_hi_ready_{s}") for s in range(2)]
                self.ready = [sem(ctx, f"{tag}_ln_ready_{s}") for s in range(2)]

        def ln_stats(dve, ln, q, of=None):
            of = q if of is None else of
            for s in range(2):
                for t in range(NT):
                    last = nc.vector.bn_stats(stats[:, s, t], X[:, bass.ds(2 * of + s, 1), t].rearrange("p a f -> p (a f)"))
            last.then_inc(ln.stats_ready, 1)
            wait_apart(dve, ln.stats_ready, q + 1)
            for s in range(2):
                for t in range(NT):
                    last = nc.vector.bn_aggr(mv[:, s, t], stats[:, s, t])
            last.then_inc(ln.mv_ready, 1)

        def ln_std(act, ln, q):
            act.wait_ge(ln.mv_ready, q + 1)
            nc.scalar.activation(std[:], mv[:, :, :, 1], ACT.Sqrt, bias=eps_col[:]).then_inc(ln.std_ready, 1)

        def ln_rstd(dve, ln, q):
            dve.wait_ge(ln.std_ready, q + 1)
            if not isinstance(q, int) or q > 0:
                for s in range(2):
                    dve.wait_ge(ln.xn_ready[s], q)
            nc.vector.reciprocal(rstd[:], std[:]).then_inc(ln.rstd_ready, 1)
            dve.wait_ge(ln.rstd_ready, 2 * q + 1)
            nc.vector.scalar_tensor_tensor(out=shift[:], in0=mv[:, :, :, 0], scalar=-1.0, in1=rstd[:],
                                           op0=ALU.mult, op1=ALU.mult).then_inc(ln.rstd_ready, 1)

        def ln_apply(act, ln, s, q, of=None):
            of = q if of is None else of
            act.wait_ge(ln.rstd_ready, 2 * q + 2)
            wait_apart(act, ln.ready[s], q + 1)
            for t in range(NT):
                last = nc.scalar.activation(XN[s][:, t], X[:, bass.ds(2 * of + s, 1), t].rearrange("p a f -> p (a f)"), ACT.Relu,
                                            bias=shift[:, s, t:t + 1], scale=rstd[:, s, t:t + 1])
            last.then_inc(ln.xn_ready[s], 1)

        def ln_split(eng, ln, s, q, used=None, used_at=None):
            if used is not None:
                eng.wait_ge(used, used_at)
            wait_apart(eng, ln.xn_ready[s], q + 1)
            eng.tensor_copy(HN[s][0][:], XN[s][:]).then_inc(ln.hi_ready[s], 1)
            eng.wait_ge(ln.hi_ready[s], q + 1)
            eng.tensor_tensor(HN[s][1][:], XN[s][:], as_f32(HN[s][0][:]), ALU.subtract).then_inc(ln.ready[s], 1)

        def ln_first_act(act, ln):
            ln_std(act, ln, 0)
            ln_apply(act, ln, 0, 0)
            ln_apply(act, ln, 1, 0)

        def ln_first_stats(dve, ln):
            for s in range(2):
                dve.sem_inc(ln.ready[s], 1)
            ln_stats(dve, ln, 0)

        def ln_first_split(dve, ln):
            for s in range(2):
                ln_split(dve, ln, s, 0)

        def ln_taken(eng, ln):
            if eng is nc.vector:
                counts = ((ln.stats_ready, 1), (ln.mv_ready, 1), (ln.rstd_ready, 2))
            elif eng is nc.scalar:
                counts = ((ln.std_ready, 1), (ln.xn_ready[0], 1), (ln.xn_ready[1], 1))
            else:
                counts = ((ln.hi_ready[0], 1), (ln.hi_ready[1], 1), (ln.ready[0], 2), (ln.ready[1], 2))
            for semaphore, n in counts:
                eng.sem_inc(semaphore, n)

        def ln_split_all(pool, ln, used, per=1):
            ln_taken(pool, ln)
            ln_split(pool, ln, 0, 1, used, per)
            with pool.Fori(0, PAIRS - 2) as q:
                ln_split(pool, ln, 1, q + 1, used, per * (2 * q + 2))
                ln_split(pool, ln, 0, q + 2, used, per * (2 * q + 3))
            ln_split(pool, ln, 1, PAIRS - 1, used, per * (2 * PAIRS - 2))

        def all_pairs(eng, pair):
            pair(0, True, 3)
            with eng.Fori(0, PAIRS - 4) as j:
                pair(j + 1, False, 3)
            for left in (2, 1, 0):
                pair(PAIRS - 1 - left, False, left)

        def aggregate(out, h, matT):
            for m in range(NT):
                last = products(out, (h[0][:, m], h[1][:, m]), (matT[0][:, m], matT[1][:, m]), m == 0, m == NT - 1)
            return last

        l1 = top.enter_context(ExitStack())
        AT = sb2(l1, "AT", [P, NT, N])
        bias_g0 = sb(l1, "bias_g0", [P, NT, D])
        bias_g1 = sb(l1, "bias_g1", [P, N])
        Wg0 = sb2(l1, "Wg0", [P, D])
        Wg1 = sb2(l1, "Wg1", [P, D])
        WihT = sb2(l1, "WihT", [P, SKIPS, GATES * D])
        WhhT = sb2(l1, "WhhT", [P, SKIPS - 1, GATES * D])
        l0 = l1.enter_context(ExitStack())
        W1T = sb2(l0, "W1T", [P, C1 * P])
        W2T = sb2(l0, "W2T", [P, C1, D])
        H1 = sb(l0, "H1", [P, C1, B, N])
        st1 = sb(l0, "st1", [P, C1, B, 6])
        st2 = sb(l0, "st2", [P, B, 6])
        bn = sb(l0, "bn", [P, C1 + 1, 2])
        bn_std = sb(l0, "bn_std", [P, C1 + 1])
        bn_rstd = sb(l0, "bn_rstd", [P, C1 + 1])
        bn_scale = sb(l0, "bn_scale", [P, C1 + 1])
        bn_shift = sb(l0, "bn_shift", [P, C1 + 1])

        l0a = l0.enter_context(ExitStack())
        AhT = sb2(l0a, "AhT", [P, NT, N])

        with stage() as c:
            A = H1[:, 0, 0:NT]
            wih = H1[:, 0, 4:4 + SKIPS].rearrange("p l (g k) -> p l g k", g=GATES)
            whh = H1[:, 0, 8:8 + SKIPS].rearrange("p l (g k) -> p l g k", g=GATES)
            vrows = sb(c, "vrows", [NVEC, P])
            bg0_row = sb(c, "bg0_row", [1, D])
            w1n = sb(c, "w1n", [P, C1, D])
            w2n = sb(c, "w2n", [P, C1 * P])
            wgn = sb(c, "wgn", [P, 2, D])
            diag_blocks = sb(c, "diag_blocks", [P, NT, P])
            rowsum = sb(c, "rowsum", [P, NT])
            colsum = sb(c, "colsum", [P, NT])
            diag = sb(c, "diag", [P, NT])
            deg = sb(c, "deg", [P, NT])
            dstd = sb(c, "dstd", [P, NT])
            dinv = sb(c, "dinv", [P, NT])
            s_A = sem(c, "adj_loaded")
            s_vec = sem(c, "vectors_loaded")
            s_w = sem(c, "small_weights_loaded")
            s_lw = sem(c, "lstm_weights_loaded")
            s_x = sem(c, "x_loaded")
            s_x0 = sem(c, "first_batches_loaded")
            ln = LN(c, "first_l0")
            s_const = sem(c, "constants_set")
            s_constr = sem(c, "rounded_constants_set")
            s_vecT = sem(c, "vectors_transposed")
            s_vecs = sem(c, "vector_columns_ready")
            s_tr = sem(c, "weights_transposed")
            s_hi = sem(c, "weight_hi_ready")
            s_lo = sem(c, "weight_lo_ready")
            s_wg = sem(c, "gcn_weights_hi_ready")
            s_AT = sem(c, "adj_transposed")
            s_AThi = sem(c, "AT_hi_ready")
            s_ATlo = sem(c, "AT_lo_ready")
            s_sum = sem(c, "degree_parts_ready")
            s_deg = sem(c, "degree_ready")
            s_dstd = sem(c, "degree_root_ready")
            s_dinv = sem(c, "degree_inverse_root_ready")
            s_scaled = sem(c, "scaled_rows_ready")
            s_AhT = sem(c, "scaled_adj_transposed")
            s_Ahhi = sem(c, "AhT_hi_ready")
            s_bc = sem(c, "broadcasts_ready")
            w_jobs = [([w1n[:, 0], w1n[:, 1]], (W1T[0][:], W1T[1][:])),
                      ([w2n[:, 0:P], w2n[:, P:2 * P]], (W2T[0][:].rearrange("p c d -> p (c d)"), W2T[1][:].rearrange("p c d -> p (c d)")))]
            w_jobs += [([wih[:, l, g] for g in range(GATES)], (WihT[0][:, l], WihT[1][:, l])) for l in range(SKIPS)]
            w_jobs += [([whh[:, l, g] for g in range(GATES)], (WhhT[0][:, l - 1], WhhT[1][:, l - 1])) for l in range(1, SKIPS)]
            W_BANKS = 4

            block = c.enter_context(nc.Block())

            @block.sync
            def _(sp):
                def load_x(q):
                    return sp.dma_start(X[:, 4 * q:4 * q + 4], d["x"][4 * q:4 * q + 4].rearrange("b (t p) f -> p b t f", p=P))

                sp.dma_start(A, d["adj"].rearrange("(t p) n -> p t n", p=P)).then_inc(s_A, 16)
                load_x(0).then_inc(s_x0, 16)
                srcs = {"bih": d["L1_gnn_bih"], "bhh": d["L1_gnn_bhh"]}
                for name in ("bih", "bhh"):
                    a, n = rows[name]
                    sp.dma_start(vrows[a:a + n, :], srcs[name].rearrange("l (g p) -> (l g) p", p=P)).then_inc(s_vec, 16)
                for name, key in (("b1", "L0_gnn_b1"), ("g1", "L0_gnn_g1"), ("be1", "L0_gnn_be1"), ("b2", "L0_gnn_b2"),
                                  ("g2", "L0_gnn_g2"), ("be2", "L0_gnn_be2"), ("bg1", "L1_gnn_bg1"),
                                  ("alpha", "L2_gnn_alpha_train"), ("d", "L2_gnn_d"), ("fcb", "L2_gnn_fc_in_b")):
                    a, n = rows[name]
                    sp.dma_start(vrows[a:a + n, :], d[key].rearrange("(r p) -> r p", p=P)).then_inc(s_vec, 16)
                sp.dma_start(wih, d["L1_gnn_Wih"].rearrange("l (g p) k -> p l g k", p=P)).then_inc(s_lw, 16)
                sp.dma_start(whh, d["L1_gnn_Whh"].rearrange("l (g p) k -> p l g k", p=P)).then_inc(s_lw, 16)
                for q in range(1, QUADS):
                    load_x(q).then_inc(s_x, 16)
                sp.dma_start(adj[:], d["adj"].rearrange("(t p) n -> p t n", p=P)).then_inc(s_x, 16)
                sp.dma_start(w_n[:], d["L2_gnn_w"]).then_inc(s_x, 16)
                sp.dma_start(fc_n[:], d["L2_gnn_fc_in_w"]).then_inc(s_x, 16)

            @block.scalar
            def _(act):
                act.dma_start(w1n[:], d["L0_gnn_W1"].rearrange("(c p) k -> p c k", p=P)).then_inc(s_w, 16)
                act.dma_start(w2n[:], d["L0_gnn_W2"]).then_inc(s_w, 16)
                act.dma_start(wgn[:, 0], d["L1_gnn_Wg0"]).then_inc(s_w, 16)
                act.dma_start(wgn[:, 1], d["L1_gnn_Wg1"]).then_inc(s_w, 16)
                act.dma_start(bg0_row[:], d["L1_gnn_bg0"].rearrange("(a n) -> a n", a=1)).then_inc(s_w, 16)
                for u in range(NT):
                    act.wait_ge(s_AT, u + 1)
                    nc.scalar.activation(AT[0][:, u], bank[u][:], ACT.Copy).then_inc(s_AThi, 1)
                act.wait_ge(s_deg, 1)
                nc.scalar.activation(dstd[:], deg[:], ACT.Sqrt).then_inc(s_dstd, 1)
                ln_std(act, ln, 0)
                act.wait_ge(s_w, 80)
                nc.scalar.activation(Wg0[0][:], wgn[:, 0], ACT.Copy).then_inc(s_wg, 1)
                nc.scalar.activation(Wg1[0][:], wgn[:, 1], ACT.Copy).then_inc(s_wg, 1)
                for u in range(NT):
                    act.wait_ge(s_AhT, u + 1)
                    act.wait_ge(s_dinv, 1)
                    nc.scalar.activation(AhT[0][:, u], bank[u][:], ACT.Copy, scale=dinv[:, u:u + 1]).then_inc(s_Ahhi, 1)
                ln_apply(act, ln, 0, 0)
                ln_apply(act, ln, 1, 0)
                for j, (tiles, dst) in enumerate(w_jobs):
                    act.wait_ge(s_tr, j + 1)
                    nc.scalar.activation(dst[0], bank[4 + j % W_BANKS][:, 0:P * len(tiles)], ACT.Copy).then_inc(s_hi, 1)

            @block.gpsimd
            def _(pool):
                nc.gpsimd.memset(ident[:], 0.0).then_inc(s_const, 1)
                nc.gpsimd.memset(ones[:], 1.0).then_inc(s_const, 1)
                nc.gpsimd.memset(eps_col[:], EPS).then_inc(s_const, 1)
                pool.wait_ge(s_const, 3)
                nc.gpsimd.affine_select(out=ident[:], in_=ident[:], compare_op=ALU.not_equal, fill=1.0, base=0,
                                        pattern=[[-1, P]], channel_multiplier=1).then_inc(s_const, 1)

            @block.tensor
            def _(pe):
                pe.wait_ge(s_const, 4)
                pe.wait_ge(s_A, 16)
                for u in range(NT):
                    for t in range(NT):
                        last = nc.tensor.transpose(bank[u][:, t * P:(t + 1) * P], A[:, t, u * P:(u + 1) * P], ident[:])
                    last.then_inc(s_AT, 1)
                pe.wait_ge(s_w, 80)
                nc.tensor.matmul(bank[4][:, 0:D], ones[0:1, :], bg0_row[:], start=True, stop=True)
                pe.wait_ge(s_constr, 1)
                pe.wait_ge(s_ATlo, NT)
                for u in range(NT):
                    nc.tensor.matmul(bank[5][:], ones_r[:], AT[0][:, u], start=(u == 0), stop=False)
                    last = nc.tensor.matmul(bank[5][:], ones_r[:], AT[1][:, u], start=False, stop=(u == NT - 1))
                last.then_inc(s_bc, 1)
                pe.wait_ge(s_vec, 16 * 12)
                nc.tensor.transpose(bank[7][:, 0:NVEC], vrows[:], ident[0:NVEC, 0:NVEC]).then_inc(s_vecT, 1)
                pe.wait_ge(s_scaled, NT)
                for u in range(NT):
                    for t in range(NT):
                        last = nc.tensor.transpose(bank[u][:, t * P:(t + 1) * P], A[:, t, u * P:(u + 1) * P], ident[:])
                    last.then_inc(s_AhT, 1)
                pe.wait_ge(s_lw, 32)
                pe.wait_ge(s_bc, 3)
                for j, (tiles, dst) in enumerate(w_jobs):
                    if j == 3:
                        pe.wait_ge(s_vecs, 1)
                    if j >= W_BANKS:
                        pe.wait_ge(s_lo, j - W_BANKS + 1)
                    for i, tile in enumerate(tiles):
                        last = nc.tensor.transpose(bank[4 + j % W_BANKS][:, i * P:(i + 1) * P], tile, ident[:])
                    last.then_inc(s_tr, 1)

            @block.vector
            def _(dve):
                dve.wait_ge(s_const, 4)
                nc.vector.tensor_copy(ones_r[:], ones[:]).then_inc(s_constr, 1)
                dve.wait_ge(s_A, 16)
                nc.vector.tensor_reduce(rowsum[:], A, AX.X, ALU.add).then_inc(s_sum, 1)
                for t in range(NT):
                    last = nc.vector.tensor_tensor(diag_blocks[:, t], A[:, t, t * P:(t + 1) * P], ident[:], ALU.mult)
                last.then_inc(s_sum, 1)
                dve.wait_ge(s_sum, 2)
                nc.vector.tensor_reduce(diag[:], diag_blocks[:], AX.X, ALU.add).then_inc(s_sum, 1)
                for u in range(NT):
                    dve.wait_ge(s_AThi, u + 1)
                    nc.vector.tensor_reduce(colsum[:, u:u + 1], bank[u][:], AX.X, ALU.add).then_inc(s_sum, 1)
                dve.wait_ge(s_sum, 3 + NT)
                nc.vector.scalar_tensor_tensor(out=deg[:], in0=rowsum[:], scalar=1.0, in1=colsum[:],
                                               op0=ALU.add, op1=ALU.add).then_inc(s_sum, 1)
                dve.wait_ge(s_sum, 4 + NT)
                nc.vector.tensor_tensor(deg[:], deg[:], diag[:], ALU.subtract).then_inc(s_deg, 1)
                for u in range(NT):
                    dve.wait_ge(s_AThi, u + 1)
                    nc.vector.tensor_tensor(AT[1][:, u], bank[u][:], as_f32(AT[0][:, u]), ALU.subtract).then_inc(s_ATlo, 1)
                dve.wait_ge(s_x0, 16)
                ln_first_stats(dve, ln)
                dve.wait_ge(s_dstd, 1)
                nc.vector.reciprocal(dinv[:], dstd[:]).then_inc(s_dinv, 1)
                for t in range(NT):
                    last = nc.vector.tensor_tensor(A[:, t, t * P:(t + 1) * P], A[:, t, t * P:(t + 1) * P], ident[:], ALU.add)
                last.then_inc(s_deg, 1)
                dve.wait_ge(s_deg, 2)
                dve.wait_ge(s_dinv, 1)
                for t in range(NT):
                    nc.vector.tensor_scalar(A[:, t], A[:, t], dinv[:, t:t + 1], None, ALU.mult).then_inc(s_scaled, 1)
                ln_rstd(dve, ln, 0)
                dve.wait_ge(s_vecT, 1)
                nc.vector.tensor_copy(vec[:], bank[7][:, 0:NVEC]).then_inc(s_vecs, 1)
                dve.wait_ge(s_vecs, 1)
                a, b = rows["bih"][0], rows["bhh"][0]
                nc.vector.tensor_tensor(lstm_bias[:], vec[:, a:a + 4 * SKIPS], vec[:, b:b + 4 * SKIPS], ALU.add).then_inc(s_vecs, 1)
                dve.wait_ge(s_bc, 1)
                for t in range(NT):
                    last = nc.vector.tensor_scalar(bias_g0[:, t], bank[4][:, 0:D], rowsum[:, t:t + 1], None, ALU.mult)
                last.then_inc(s_bc, 1)
                nc.vector.tensor_scalar(bias_g1[:], bank[5][:], col("bg1"), None, ALU.mult).then_inc(s_bc, 1)
                dve.wait_ge(s_wg, 2)
                nc.vector.tensor_tensor(Wg0[1][:], wgn[:, 0], as_f32(Wg0[0][:]), ALU.subtract)
                nc.vector.tensor_tensor(Wg1[1][:], wgn[:, 1], as_f32(Wg1[0][:]), ALU.subtract)
                for u in range(NT):
                    dve.wait_ge(s_Ahhi, u + 1)
                    nc.vector.scalar_tensor_tensor(out=AhT[1][:, u], in0=bank[u][:], scalar=dinv[:, u:u + 1],
                                                   in1=as_f32(AhT[0][:, u]), op0=ALU.mult, op1=ALU.subtract)
                for j, (tiles, dst) in enumerate(w_jobs):
                    dve.wait_ge(s_hi, j + 1)
                    nc.vector.tensor_tensor(dst[1], bank[4 + j % W_BANKS][:, 0:P * len(tiles)], as_f32(dst[0]),
                                            ALU.subtract).then_inc(s_lo, 1)
                ln_first_split(dve, ln)
                dve.wait_ge(s_x, 16 * (QUADS + 2))

        with stage() as c:
            AG = [sb2(c, f"AG{s}", [P, N]) for s in range(2)]
            ln = LN(c, "l0")
            s_agg = sem(c, "l0_aggregated")
            s_ahi = sem(c, "l0_agg_hi_ready")
            s_alo = sem(c, "l0_agg_lo_ready")
            s_w1 = sem(c, "l0_w1_done")
            s_h1 = sem(c, "l0_h1_ready")
            FREE = 2 * C1
            s_st = sem(c, "l0_stats_done")
            block = c.enter_context(nc.Block())

            @block.tensor
            def _(pe):
                def agg(q, s):
                    pe.wait_ge(ln.ready[s], q + 2)
                    aggregate(bank[s][:], HN[s], AhT).then_inc(s_agg, 1)

                def pair(q, first, left):
                    for s in range(2):
                        b = 2 * q + s
                        pe.wait_ge(s_alo, b + 1)
                        for h in range(C1):
                            pe.wait_ge(s_h1, C1 * b + h + 1)
                            products(bank[2 + 2 * s + h][:], (W1T[0][:, h * P:(h + 1) * P], W1T[1][:, h * P:(h + 1) * P]),
                                     (AG[s][0][:], AG[s][1][:]), True, True).then_inc(s_w1, 1)
                        if left:
                            agg(q + 1, s)

                agg(0, 0)
                agg(0, 1)
                all_pairs(pe, pair)

            @block.scalar
            def _(act):
                def agg_hi(q, s):
                    act.wait_ge(s_agg, 2 * q + s + 1)
                    nc.scalar.activation(AG[s][0][:], bank[s][:], ACT.Copy).then_inc(s_ahi, 1)

                def h1(q, s):
                    b = 2 * q + s
                    for h in range(C1):
                        wait_apart(act, s_w1, C1 * b + h + 1)
                        out = H1[:, h, bass.ds(b, 1)].rearrange("p a n -> p (a n)")
                        nc.scalar.activation(out, bank[2 + 2 * s + h][:], ACT.Identity, bias=col("b1", h)).then_inc(s_h1, 1)

                def pair(q, first, left):
                    h1(q, 0)
                    if left >= 2:
                        ln_apply(act, ln, 0, q + 2)
                    if left:
                        agg_hi(q + 1, 0)
                    h1(q, 1)
                    if left >= 2:
                        ln_apply(act, ln, 1, q + 2)
                    if left:
                        agg_hi(q + 1, 1)
                    if left >= 3:
                        ln_std(act, ln, q + 3)

                act.sem_inc(s_h1, FREE)
                ln_taken(act, ln)
                ln_std(act, ln, 1)
                ln_apply(act, ln, 0, 1)
                agg_hi(0, 0)
                ln_apply(act, ln, 1, 1)
                agg_hi(0, 1)
                ln_std(act, ln, 2)
                all_pairs(act, pair)

            @block.gpsimd
            def _(pool):
                ln_split_all(pool, ln, s_agg)

            @block.vector
            def _(dve):
                def agg_lo(q, s):
                    dve.wait_ge(s_ahi, 2 * q + s + 1)
                    nc.vector.tensor_tensor(AG[s][1][:], bank[s][:], as_f32(AG[s][0][:]), ALU.subtract).then_inc(s_alo, 1)

                def h1_stats(q, s):
                    b = 2 * q + s
                    for h in range(C1):
                        dve.wait_ge(s_h1, FREE + C1 * b + h + 1)
                        nc.vector.bn_stats(st1[:, h, bass.ds(b, 1)].rearrange("p a k -> p (a k)"),
                                           H1[:, h, bass.ds(b, 1)].rearrange("p a n -> p (a n)"))

                def pair(q, first, left):
                    if left >= 2:
                        ln_rstd(dve, ln, q + 2)
                    h1_stats(q, 0)
                    if left:
                        agg_lo(q + 1, 0)
                    if left >= 3:
                        ln_stats(dve, ln, q + 3)
                    h1_stats(q, 1)
                    if left:
                        agg_lo(q + 1, 1)

                ln_taken(dve, ln)
                ln_stats(dve, ln, 1)
                ln_rstd(dve, ln, 1)
                agg_lo(0, 0)
                ln_stats(dve, ln, 2)
                agg_lo(0, 1)
                all_pairs(dve, pair)

        l0a.close()
        with stage() as c:
            Y1 = [sb(c, f"Y1_{s}", [P, C1, N]) for s in range(2)]
            Y1s = [sb2(c, f"Y1s_{s}", [P, C1, N]) for s in range(2)]
            DVE_COLS = C1 * N // 2

            def low_part(eng, s, cols):
                y, hi, lo = (v.rearrange("p c n -> p (c n)") for v in (Y1[s][:], as_f32(Y1s[s][0][:]), Y1s[s][1][:]))
                return eng.tensor_tensor(lo[:, cols], y[:, cols], hi[:, cols], ALU.subtract)

            s_mv = sem(c, "bn1_mv_ready")
            s_std = sem(c, "bn1_std_ready")
            s_sc = sem(c, "bn1_scale_ready")
            s_y = sem(c, "bn1_applied")
            s_hi = sem(c, "bn1_hi_ready")
            s_lo = sem(c, "bn1_lo_ready")
            s_lo1 = sem(c, "bn1_lo_second_ready")
            s_w2 = sem(c, "w2_done")
            s_o = sem(c, "out2_ready")
            block = c.enter_context(nc.Block())

            @block.scalar
            def _(act):
                act.wait_ge(s_mv, 1)
                nc.scalar.activation(bn_std[:, 0:C1], bn[:, 0:C1, 1], ACT.Sqrt, bias=eps_col[:]).then_inc(s_std, 1)
                act.wait_ge(s_sc, 4)

                def bn1(q, s, ahead=True):
                    if ahead:
                        act.wait_ge(s_lo, 2 * (q - 1) + s + 1)
                        wait_apart(act, s_lo1, 2 * (q - 1) + s + 1)
                    for h in range(C1):
                        nc.scalar.activation(Y1[s][:, h], H1[:, h, bass.ds(2 * q + s, 1)].rearrange("p a n -> p (a n)"), ACT.Relu,
                                             bias=bn_shift[:, h:h + 1], scale=bn_scale[:, h:h + 1]).then_inc(s_y, 1)

                def out2(q, s):
                    b = 2 * q + s
                    wait_apart(act, s_w2, b + 1)
                    nc.scalar.activation(H1[:, 0, bass.ds(b, 1)].rearrange("p a n -> p (a n)"), bank[s][:], ACT.Identity,
                                         bias=col("b2")).then_inc(s_o, 1)

                act.sem_inc(s_o, 2)
                bn1(0, 0, ahead=False)
                bn1(0, 1, ahead=False)
                with act.Fori(0, PAIRS - 1) as q:
                    for s in range(2):
                        bn1(q + 1, s)
                        out2(q, s)
                out2(PAIRS - 1, 0)
                out2(PAIRS - 1, 1)

            @block.vector
            def _(dve):
                for h in range(C1):
                    last = nc.vector.bn_aggr(bn[:, h], st1[:, h].rearrange("p b k -> p (b k)"))
                last.then_inc(s_mv, 1)
                dve.wait_ge(s_std, 1)
                nc.vector.reciprocal(bn_rstd[:, 0:C1], bn_std[:, 0:C1]).then_inc(s_sc, 1)
                dve.wait_ge(s_sc, 1)
                g, be = rows["g1"][0], rows["be1"][0]
                nc.vector.tensor_tensor(bn_scale[:, 0:C1], bn_rstd[:, 0:C1], vec[:, g:g + C1], ALU.mult).then_inc(s_sc, 1)
                dve.wait_ge(s_sc, 2)
                nc.vector.tensor_tensor(bn_shift[:, 0:C1], bn[:, 0:C1, 0], bn_scale[:, 0:C1], ALU.mult).then_inc(s_sc, 1)
                dve.wait_ge(s_sc, 3)
                nc.vector.tensor_tensor(bn_shift[:, 0:C1], vec[:, be:be + C1], bn_shift[:, 0:C1], ALU.subtract).then_inc(s_sc, 1)

                def split(q, s, ahead=True):
                    b = 2 * q + s
                    dve.wait_ge(s_y, C1 * b + C1)
                    if ahead:
                        dve.wait_ge(s_w2, b - 1)
                    nc.vector.tensor_copy(Y1s[s][0][:], Y1[s][:]).then_inc(s_hi, 1)
                    dve.wait_ge(s_hi, b + 1)
                    low_part(nc.vector, s, slice(0, DVE_COLS)).then_inc(s_lo, 1)

                def out2_stats(q, s):
                    b = 2 * q + s
                    dve.wait_ge(s_o, 2 + b + 1)
                    nc.vector.bn_stats(st2[:, bass.ds(b, 1)].rearrange("p a k -> p (a k)"),
                                       H1[:, 0, bass.ds(b, 1)].rearrange("p a n -> p (a n)"))

                split(0, 0, ahead=False)
                split(0, 1, ahead=False)
                with dve.Fori(0, PAIRS - 1) as q:
                    for s in range(2):
                        split(q + 1, s)
                        out2_stats(q, s)
                out2_stats(PAIRS - 1, 0)
                out2_stats(PAIRS - 1, 1)

            @block.gpsimd
            def _(pool):
                with pool.Fori(0, PAIRS) as i:
                    for s in range(2):
                        b = 2 * i + s
                        pool.wait_ge(s_hi, b + 1)
                        low_part(nc.gpsimd, s, slice(DVE_COLS, C1 * N)).then_inc(s_lo1, 1)

            @block.tensor
            def _(pe):
                with pe.Fori(0, PAIRS) as i:
                    for s in range(2):
                        b = 2 * i + s
                        pe.wait_ge(s_lo, b + 1)
                        pe.wait_ge(s_lo1, b + 1)
                        pe.wait_ge(s_o, b + 1)
                        for h in range(C1):
                            last = products(bank[s][:], (W2T[0][:, h], W2T[1][:, h]), (Y1s[s][0][:, h], Y1s[s][1][:, h]),
                                            h == 0, h == C1 - 1)
                        last.then_inc(s_w2, 1)

        with stage() as c:
            Y2 = [sb(c, f"Y2_{s}", [P, N]) for s in range(4)]
            s_mv = sem(c, "bn2_mv_ready")
            s_std = sem(c, "bn2_std_ready")
            s_sc = sem(c, "bn2_scale_ready")
            s_y = sem(c, "bn2_applied")
            s_t = sem(c, "bn2_transposed")
            s_x = sem(c, "l0_x_added")
            ln = LN(c, "first_l1")
            block = c.enter_context(nc.Block())

            @block.scalar
            def _(act):
                act.wait_ge(s_mv, 1)
                nc.scalar.activation(bn_std[:, C1:C1 + 1], bn[:, C1, 1:2], ACT.Sqrt, bias=eps_col[:]).then_inc(s_std, 1)
                act.wait_ge(s_sc, 4)

                def normed(i):
                    for s in range(4):
                        b = 4 * i + s
                        wait_apart(act, s_t, b + 1)
                        nc.scalar.activation(Y2[s][:], H1[:, 0, bass.ds(b, 1)].rearrange("p a n -> p (a n)"), ACT.Identity,
                                             bias=bn_shift[:, C1:C1 + 1], scale=bn_scale[:, C1:C1 + 1]).then_inc(s_y, 1)

                with act.Fori(0, QUADS - 1) as i:
                    normed(i)
                ln_std(act, ln, 0)
                normed(QUADS - 1)
                ln_apply(act, ln, 0, 0)
                ln_apply(act, ln, 1, 0)

            @block.tensor
            def _(pe):
                pe.sem_inc(s_t, 4)
                with pe.Fori(0, QUADS) as i:
                    for s in range(4):
                        b = 4 * i + s
                        pe.wait_ge(s_y, b + 1)
                        pe.wait_ge(s_x, b + 1)
                        for t in range(NT):
                            last = nc.tensor.transpose(bank[s][:, t * P:(t + 1) * P], Y2[s][:, t * P:(t + 1) * P], ident[:])
                        last.then_inc(s_t, 1)

            @block.vector
            def _(dve):
                dve.sem_inc(s_x, 4)
                nc.vector.bn_aggr(bn[:, C1], st2[:].rearrange("p b k -> p (b k)")).then_inc(s_mv, 1)
                dve.wait_ge(s_std, 1)
                nc.vector.reciprocal(bn_rstd[:, C1:C1 + 1], bn_std[:, C1:C1 + 1]).then_inc(s_sc, 1)
                dve.wait_ge(s_sc, 1)
                nc.vector.tensor_tensor(bn_scale[:, C1:C1 + 1], bn_rstd[:, C1:C1 + 1], col("g2"), ALU.mult).then_inc(s_sc, 1)
                dve.wait_ge(s_sc, 2)
                nc.vector.tensor_tensor(bn_shift[:, C1:C1 + 1], bn[:, C1, 0:1], bn_scale[:, C1:C1 + 1], ALU.mult).then_inc(s_sc, 1)
                dve.wait_ge(s_sc, 3)
                nc.vector.tensor_tensor(bn_shift[:, C1:C1 + 1], col("be2"), bn_shift[:, C1:C1 + 1], ALU.subtract).then_inc(s_sc, 1)

                def add(i):
                    for s in range(4):
                        b = 4 * i + s
                        dve.wait_ge(s_t, 4 + b + 1)
                        xb = X[:, bass.ds(b, 1)].rearrange("p a t f -> p (a t f)")
                        nc.vector.tensor_tensor(xb, bank[s][:], xb, ALU.add).then_inc(s_x, 1)

                add(0)
                dve.wait_ge(s_x, 4 + 2)
                ln_first_stats(dve, ln)
                add(1)
                ln_rstd(dve, ln, 0)
                with dve.Fori(0, QUADS - 2) as i:
                    add(i + 2)
                ln_first_split(dve, ln)
        l0.close()

        H = sb2(l1, "H", [P, B, N])
        with stage() as c:
            AG = [sb2(c, f"AG1_{s}", [P, N]) for s in range(2)]
            T1 = [sb(c, f"T1_{s}", [P, NT, D]) for s in range(2)]
            G1 = [sb2(c, f"G1_{s}", [P, NT, D]) for s in range(2)]
            AG2 = [sb2(c, f"AG2_{s}", [P, N]) for s in range(2)]
            T2 = [sb(c, f"T2_{s}", [P, N]) for s in range(2)]
            ln = LN(c, "l1")
            s_a1 = sem(c, "l1_first_aggregated")
            s_a1hi = sem(c, "l1_first_agg_hi_ready")
            s_a1lo = sem(c, "l1_first_agg_lo_ready")
            s_g0 = sem(c, "l1_wg0_done")
            s_t1 = sem(c, "l1_first_sum_ready")
            s_h1hi = sem(c, "l1_h1_hi_ready")
            s_h1lo = sem(c, "l1_h1_lo_ready")
            s_a2 = sem(c, "l1_second_aggregated")
            s_a2hi = sem(c, "l1_second_agg_hi_ready")
            s_a2lo = sem(c, "l1_second_agg_lo_ready")
            s_g1 = sem(c, "l1_wg1_done")
            s_t2 = sem(c, "l1_second_sum_ready")
            s_Hhi = sem(c, "l1_H_hi_ready")
            block = c.enter_context(nc.Block())

            @block.tensor
            def _(pe):
                def agg1(q, s):
                    pe.wait_ge(ln.ready[s], q + 2)
                    aggregate(bank[s][:], HN[s], AT).then_inc(s_a1, 1)

                def wg0(q, s):
                    pe.wait_ge(s_a1lo, 2 * q + s + 1)
                    for t in range(NT):
                        cols = slice(t * P, (t + 1) * P)
                        last = products(bank[2 + s][:, cols], (AG[s][0][:, cols], AG[s][1][:, cols]), (Wg0[0][:], Wg0[1][:]), True, True)
                    last.then_inc(s_g0, 1)

                def agg2(q, s):
                    pe.wait_ge(s_h1lo, 2 * q + s + 1)
                    aggregate(bank[4 + s][:], G1[s], AT).then_inc(s_a2, 1)

                def wg1(q, s):
                    pe.wait_ge(s_a2lo, 2 * q + s + 1)
                    pe.wait_ge(s_t2, 2 * q + s + 1)
                    products(bank[6 + s][:], (Wg1[0][:], Wg1[1][:]), (AG2[s][0][:], AG2[s][1][:]), True, True).then_inc(s_g1, 1)

                def pair(q, first, left):
                    wg0(q, 0)
                    if not first:
                        wg1(q - 1, 1)
                    if left:
                        agg1(q + 1, 0)
                    wg0(q, 1)
                    agg2(q, 0)
                    if left:
                        agg1(q + 1, 1)
                    agg2(q, 1)
                    wg1(q, 0)

                agg1(0, 0)
                agg1(0, 1)
                all_pairs(pe, pair)
                wg1(PAIRS - 1, 1)

            @block.scalar
            def _(act):
                def agg1_hi(q, s):
                    act.wait_ge(s_a1, 2 * q + s + 1)
                    nc.scalar.activation(AG[s][0][:], bank[s][:], ACT.Copy).then_inc(s_a1hi, 1)

                def h1_hi(q, s):
                    act.wait_ge(s_t1, 2 * q + s + 1)
                    nc.scalar.activation(G1[s][0][:], T1[s][:], ACT.Relu).then_inc(s_h1hi, 1)

                def agg2_hi(q, s):
                    act.wait_ge(s_a2, 2 * q + s + 1)
                    nc.scalar.activation(AG2[s][0][:], bank[4 + s][:], ACT.Copy).then_inc(s_a2hi, 1)

                def H_hi(q, s):
                    b = 2 * q + s
                    wait_apart(act, s_t2, 2 + b + 1)
                    nc.scalar.activation(H[0][:, bass.ds(b, 1)].rearrange("p a n -> p (a n)"), T2[s][:], ACT.Relu).then_inc(s_Hhi, 1)

                def pair(q, first, left):
                    if not first:
                        agg2_hi(q - 1, 1)
                        H_hi(q - 1, 0)
                    h1_hi(q, 0)
                    if not first:
                        H_hi(q - 1, 1)
                    if left:
                        agg1_hi(q + 1, 0)
                    if left >= 2:
                        ln_std(act, ln, q + 2)
                    h1_hi(q, 1)
                    if left >= 2:
                        ln_apply(act, ln, 0, q + 2)
                    agg2_hi(q, 0)
                    if left >= 2:
                        ln_apply(act, ln, 1, q + 2)
                    if left:
                        agg1_hi(q + 1, 1)

                ln_taken(act, ln)
                ln_std(act, ln, 1)
                ln_apply(act, ln, 0, 1)
                agg1_hi(0, 0)
                ln_apply(act, ln, 1, 1)
                agg1_hi(0, 1)
                all_pairs(act, pair)
                agg2_hi(PAIRS - 1, 1)
                H_hi(PAIRS - 1, 0)
                H_hi(PAIRS - 1, 1)

            @block.gpsimd
            def _(pool):
                ln_split_all(pool, ln, s_a1)

            @block.vector
            def _(dve):
                def agg1_lo(q, s):
                    dve.wait_ge(s_a1hi, 2 * q + s + 1)
                    nc.vector.tensor_tensor(AG[s][1][:], bank[s][:], as_f32(AG[s][0][:]), ALU.subtract).then_inc(s_a1lo, 1)

                def t1(q, s):
                    dve.wait_ge(s_g0, 2 * q + s + 1)
                    nc.vector.tensor_tensor(T1[s][:].rearrange("p t f -> p (t f)"), bank[2 + s][:],
                                            bias_g0[:].rearrange("p t f -> p (t f)"), ALU.add).then_inc(s_t1, 1)

                def h1_lo(q, s):
                    dve.wait_ge(s_h1hi, 2 * q + s + 1)
                    nc.vector.scalar_tensor_tensor(out=G1[s][1][:], in0=T1[s][:], scalar=0.0, in1=as_f32(G1[s][0][:]),
                                                   op0=ALU.max, op1=ALU.subtract).then_inc(s_h1lo, 1)

                def agg2_lo(q, s):
                    dve.wait_ge(s_a2hi, 2 * q + s + 1)
                    nc.vector.tensor_tensor(AG2[s][1][:], bank[4 + s][:], as_f32(AG2[s][0][:]), ALU.subtract).then_inc(s_a2lo, 1)

                def t2(q, s):
                    dve.wait_ge(s_g1, 2 * q + s + 1)
                    nc.vector.tensor_tensor(T2[s][:], bank[6 + s][:], bias_g1[:], ALU.add).then_inc(s_t2, 1)

                def H_lo(q, s):
                    b = 2 * q + s
                    dve.wait_ge(s_Hhi, b + 1)
                    nc.vector.scalar_tensor_tensor(out=H[1][:, bass.ds(b, 1)].rearrange("p a n -> p (a n)"), in0=T2[s][:], scalar=0.0,
                                                   in1=as_f32(H[0][:, bass.ds(b, 1)]).rearrange("p a n -> p (a n)"),
                                                   op0=ALU.max, op1=ALU.subtract)

                def pair(q, first, left):
                    if not first:
                        agg2_lo(q - 1, 1)
                        t2(q - 1, 0)
                    t1(q, 0)
                    if not first:
                        H_lo(q - 1, 0)
                        t2(q - 1, 1)
                    h1_lo(q, 0)
                    if not first:
                        H_lo(q - 1, 1)
                    if left >= 2:
                        ln_stats(dve, ln, q + 2)
                    if left:
                        agg1_lo(q + 1, 0)
                    t1(q, 1)
                    if left >= 2:
                        ln_rstd(dve, ln, q + 2)
                    h1_lo(q, 1)
                    agg2_lo(q, 0)
                    if left:
                        agg1_lo(q + 1, 1)

                dve.sem_inc(s_t2, 2)
                ln_taken(dve, ln)
                ln_stats(dve, ln, 1)
                ln_rstd(dve, ln, 1)
                agg1_lo(0, 0)
                agg1_lo(0, 1)
                all_pairs(dve, pair)
                agg2_lo(PAIRS - 1, 1)
                t2(PAIRS - 1, 0)
                H_lo(PAIRS - 1, 0)
                t2(PAIRS - 1, 1)
                H_lo(PAIRS - 1, 1)

        class Span:
            def __init__(self, p, before):
                self.p = p
                self.W = N // p
                self.CB = {1: 1, 2: 2, 3: 2, 4: 4}[p]
                self.CC = self.CB * self.W
                self.ITERS = B // self.CB // 2
                self.GC = 3 + 4 * (p - 1)
                self.steps = [(t, s) for t in range(p) for s in range(2)]
                self.before = before
                self.gates0 = before.gates0 + before.GC * before.ITERS if before else 0
                self.steps0 = before.steps0 + before.p * before.ITERS if before else 0
                self.sums0 = before.sums0 + (before.p - 1) * before.ITERS if before else 0

            def order(self, t):
                return (I_, G_, O_) if t % self.p == 0 else (F_, I_, G_, O_)

            def gates(self, i, t):
                return self.gates0 + self.GC * i + (0 if t == 0 else 3 + 4 * (t - 1))

            def done(self, i, t):
                return self.steps0 + self.p * i + t

            def view(self, buffer):
                return buffer[:, 0:self.CC].rearrange("p (b w) -> p b w", b=self.CB)

            def columns(self, h, i, t, s):
                p = self.p
                return h[:, bass.ds((2 * i + s) * self.CB, self.CB), t:t + (self.W - 1) * p + 1:p]

        spans = []
        for p in range(1, SKIPS + 1):
            spans.append(Span(p, spans[-1] if spans else None))

        def prior(w, i, n):
            if n > 0:
                return (w, i, *w.steps[n - 1])
            if isinstance(i, int) and i == 0:
                return (w.before, w.before.ITERS - 1, *w.before.steps[-1]) if w.before else None
            return (w, i - 1, *w.steps[-1])

        def all_turns(eng, turn):
            for w in spans:
                turn(w, 0)
                with eng.Fori(0, w.ITERS - 1) as j:
                    turn(w, j + 1)

        with stage() as c:
            gate = [[sb(c, f"lstm_gate{g}_{s}", [P, N]) for g in range(GATES)] for s in range(2)]
            cell = [sb(c, f"lstm_cell_{s}", [P, N]) for s in range(2)]
            inp = [XN[s][:].rearrange("p t f -> p (t f)") for s in range(2)]
            th = [sb(c, f"lstm_tanh_{s}", [P, N]) for s in range(2)]
            hf = [sb(c, f"lstm_h_{s}", [P, N]) for s in range(2)]
            hs = [sb2(c, f"lstm_hs_{s}", [P, N]) for s in range(2)]
            s_mm = [sem(c, f"lstm_gate_summed_{s}") for s in range(2)]
            s_gate = [sem(c, f"lstm_gate_ready_{s}") for s in range(2)]
            s_dve = [sem(c, f"lstm_cell_parts_{s}") for s in range(2)]
            s_cell = [sem(c, f"lstm_cell_ready_{s}") for s in range(2)]
            s_th = [sem(c, f"lstm_tanh_ready_{s}") for s in range(2)]
            s_hf = [sem(c, f"lstm_h_ready_{s}") for s in range(2)]
            s_h = [sem(c, f"lstm_h_split_{s}") for s in range(2)]
            block = c.enter_context(nc.Block())

            @block.tensor
            def _(pe):
                def turn(w, i):
                    opening = isinstance(i, int) and w.before is not None
                    if w.before:
                        need = w.before.done(w.CB // w.before.CB, 0) if opening else w.steps0
                        for s in range(2):
                            pe.wait_ge(s_h[s], 1 + need)
                    for t, s in w.steps:
                        last_order = w.before.order(-1) if opening and t == 0 else w.order(t - 1)
                        for g in w.order(t):
                            if g in last_order:
                                pe.wait_ge(s_gate[s], 4 + w.gates(i, t) - len(last_order) + last_order.index(g) + 1)
                            wx = (WihT[0][:, w.p - 1, g * P:(g + 1) * P], WihT[1][:, w.p - 1, g * P:(g + 1) * P])
                            last = products(w.view(bank[4 * s + g]), wx, (w.columns(H[0], i, t, s), w.columns(H[1], i, t, s)),
                                            True, t == 0)
                            if t == 0:
                                last.then_inc(s_mm[s], 1)
                        if t > 0:
                            pe.wait_ge(s_h[s], 1 + w.done(i, t))
                            for g in w.order(t):
                                wh = (WhhT[0][:, w.p - 2, g * P:(g + 1) * P], WhhT[1][:, w.p - 2, g * P:(g + 1) * P])
                                products(bank[4 * s + g][:, 0:w.CC], wh, (hs[s][0][:, 0:w.CC], hs[s][1][:, 0:w.CC]),
                                         False, True).then_inc(s_mm[s], 1)

                all_turns(pe, turn)

            @block.scalar
            def _(act):
                def gate_out(w, i, t, s, n, g):
                    act.wait_ge(s_mm[s], w.gates(i, t) + n + 1)
                    nc.scalar.activation(gate[s][g][:, 0:w.CC], bank[4 * s + g][:, 0:w.CC], ACT.Tanh if g == G_ else ACT.Sigmoid,
                                         bias=lstm_bias[:, 4 * (w.p - 1) + g:4 * (w.p - 1) + g + 1]).then_inc(s_gate[s], 1)

                def tanh_cell(w, i, t, s):
                    act.wait_ge(s_cell[s], w.done(i, t) + 1)
                    nc.scalar.activation(th[s][:, 0:w.CC], cell[s][:, 0:w.CC], ACT.Tanh).then_inc(s_th[s], 1)

                def turn(w, i):
                    for n, (t, s) in enumerate(w.steps):
                        early = (1 if w.p == 1 else 2 if s == 0 else 0) if t == 0 else 0
                        for m, g in enumerate(w.order(t)):
                            if m == early and prior(w, i, n):
                                tanh_cell(*prior(w, i, n))
                            if t == 0 and g == O_:
                                act.wait_ge(s_hf[s], 2 * w.done(i, 0) + 1)
                            gate_out(w, i, t, s, m, g)

                for s in range(2):
                    act.sem_inc(s_gate[s], 4)
                all_turns(act, turn)
                tanh_cell(*prior(spans[-1], spans[-1].ITERS, 0))

            @block.vector
            def _(dve):
                def new_cell(w, i, t, s):
                    done = 4 + w.gates(i, t)
                    c_, i_, f_, g_ = (v[:, 0:w.CC] for v in (cell[s], gate[s][I_], gate[s][F_], gate[s][G_]))
                    if t == 0:
                        dve.wait_ge(s_gate[s], done + 2)
                        nc.vector.tensor_tensor(c_, i_, g_, ALU.mult).then_inc(s_cell[s], 1)
                    else:
                        dve.wait_ge(s_gate[s], done + 1)
                        nc.vector.tensor_tensor(c_, f_, c_, ALU.mult)
                        dve.wait_ge(s_gate[s], done + 3)
                        nc.vector.tensor_tensor(inp[s][:, 0:w.CC], i_, g_, ALU.mult).then_inc(s_dve[s], 1)
                        dve.wait_ge(s_dve[s], w.sums0 + (w.p - 1) * i + t)
                        nc.vector.tensor_tensor(c_, c_, inp[s][:, 0:w.CC], ALU.add).then_inc(s_cell[s], 1)

                def new_h(w, i, t, s):
                    dve.wait_ge(s_th[s], w.done(i, t) + 1)
                    nc.vector.tensor_tensor(hf[s][:, 0:w.CC], gate[s][O_][:, 0:w.CC], th[s][:, 0:w.CC], ALU.mult).then_inc(s_hf[s], 1)

                def split_h(w, i, t, s):
                    hi, lo = (w.columns(H[part], i, t, s) if t == w.p - 1 else w.view(hs[s][part]) for part in range(2))
                    dve.wait_ge(s_hf[s], 2 * w.done(i, t) + 3)
                    nc.vector.tensor_copy(hi, w.view(hf[s])).then_inc(s_hf[s], 1)
                    dve.wait_ge(s_hf[s], 2 * w.done(i, t) + 4)
                    nc.vector.tensor_tensor(lo, w.view(hf[s]), as_f32(hi), ALU.subtract).then_inc(s_h[s], 1)

                def turn(w, i):
                    for n, (t, s) in enumerate(w.steps):
                        step_before = prior(w, i, n)
                        place = 1 if w.p == 1 else 0 if t == 0 and s == 0 else 2
                        if place == 0:
                            new_cell(w, i, t, s)
                        if step_before:
                            new_h(*step_before)
                        if place == 1:
                            new_cell(w, i, t, s)
                        if step_before:
                            split_h(*step_before)
                        if place == 2:
                            new_cell(w, i, t, s)

                for s in range(2):
                    dve.sem_inc(s_h[s], 1)
                    dve.sem_inc(s_hf[s], 2)
                all_turns(dve, turn)
                new_h(*prior(spans[-1], spans[-1].ITERS, 0))
                split_h(*prior(spans[-1], spans[-1].ITERS, 0))

        with stage() as c:
            SLOTS = 8
            BY_VECTOR = (0, 2, 5)
            Y = [sb(c, f"Yl1_{s}", [P, N]) for s in range(SLOTS)]
            s_y = [sem(c, f"l1_h_joined_{s}") for s in range(SLOTS)]
            s_t = sem(c, "l1_h_transposed")
            s_x = sem(c, "l1_x_added")
            block = c.enter_context(nc.Block())

            def join(eng, g, s):
                b = SLOTS * g + s
                eng.wait_ge(s_t, b + 1)
                eng.tensor_tensor(Y[s][:], as_f32(H[0][:, bass.ds(b, 1)]).rearrange("p a n -> p (a n)"),
                                  as_f32(H[1][:, bass.ds(b, 1)]).rearrange("p a n -> p (a n)"), ALU.add).then_inc(s_y[s], 1)

            @block.gpsimd
            def _(pool):
                with pool.Fori(0, B // SLOTS) as g:
                    for s in range(SLOTS):
                        if s not in BY_VECTOR:
                            join(nc.gpsimd, g, s)

            @block.tensor
            def _(pe):
                pe.sem_inc(s_t, SLOTS)
                with pe.Fori(0, B // SLOTS) as g:
                    for s in range(SLOTS):
                        b = SLOTS * g + s
                        pe.wait_ge(s_y[s], g + 1)
                        pe.wait_ge(s_x, b + 1)
                        for t in range(NT):
                            last = nc.tensor.transpose(bank[s][:, t * P:(t + 1) * P], Y[s][:, t * P:(t + 1) * P], ident[:])
                        last.then_inc(s_t, 1)

            @block.vector
            def _(dve):
                def add(g, s):
                    b = SLOTS * g + s
                    dve.wait_ge(s_t, SLOTS + b + 1)
                    xb = X[:, bass.ds(b, 1)].rearrange("p a t f -> p (a t f)")
                    nc.vector.tensor_tensor(xb, bank[s][:], xb, ALU.add).then_inc(s_x, 1)

                def batches(g, more):
                    for s in range(SLOTS):
                        add(g, s)
                        if s == 1:
                            join(nc.vector, g, 5)
                        if s == 3 and more:
                            join(nc.vector, g + 1, 0)
                        if s == 5 and more:
                            join(nc.vector, g + 1, 2)

                dve.sem_inc(s_x, SLOTS)
                join(nc.vector, 0, 0)
                join(nc.vector, 0, 2)
                with dve.Fori(0, B // SLOTS - 1) as g:
                    batches(g, True)
                batches(B // SLOTS - 1, False)
        l1.close()

        KB = 3
        KI = (STEPS + KB) // KB
        assert KB * KI == STEPS + 1
        l2 = top.enter_context(ExitStack())
        PT = sb2(l2, "PT", [P, NT, N])
        P2T = sb2(l2, "P2T", [P, NT, N])
        P3T = sb2(l2, "P3T", [P, NT, N])
        Ms = sb2(l2, "Ms", [P, KB, KI, D])
        bias_w = sb(l2, "bias_w", [P, NT, KI, D])
        with stage() as c:
            Pn = sb(c, "Pn", [P, NT, N])
            Pns = sb2(c, "Pns", [P, NT, N])
            alpha_half = sb(c, "alpha_half", [P, NT])
            diag_col = sb(c, "diag_col", [P, NT])
            d_col = sb(c, "d_col", [P, 1])
            wT = sb(c, "wT", [P, D])
            wTd = sb(c, "wTd", [P, D])
            fcb_all = sb(c, "fcb_all", [P, P])
            Q = sb(c, "Q", [P, STEPS + 1, D])
            M = sb(c, "M", [P, KB, KI, D])
            R = sb(c, "R", [P, KB, KI, D])
            p1 = sb(c, "p1", [P, NT])
            p1s = sb(c, "p1s", [P, NT, 2], f32r)
            p2 = sb(c, "p2", [P, NT])
            p2pair = sb(c, "p2pair", [P, NT, 2])
            s_sig = sem(c, "l2_alpha_ready")
            s_v = sem(c, "l2_columns_ready")
            s_Pn = sem(c, "P_rows_ready")
            s_wt = sem(c, "l2_w_transposed")
            s_wts = sem(c, "l2_w_columns_ready")
            s_weff = sem(c, "Q_product_done")
            s_q = sem(c, "Q_power_ready")
            s_F = sem(c, "F_and_r_done")
            s_m = sem(c, "M_terms_added")
            s_PT = sem(c, "P_transposed")
            s_PThi = sem(c, "PT_hi_ready")
            s_PTlo = sem(c, "PT_lo_ready")
            s_Pnhi = sem(c, "Pn_hi_ready")
            s_Pnlo = sem(c, "Pn_lo_ready")
            s_pow = sem(c, "P_power_tile_done")
            s_powhi = sem(c, "P_power_hi_ready")
            s_powlo = sem(c, "P_power_lo_ready")
            s_p1 = sem(c, "p1_ready")
            s_p2 = sem(c, "p2_done")
            s_mhi = sem(c, "M_hi_ready")
            s_b = sem(c, "bias_parts_ready")
            ln = LN(c, "first_l2")
            block = c.enter_context(nc.Block())

            def place(j):
                return j % KB, j // KB

            def power(n):
                return (P2T, n) if n < NT else (P3T, n - NT)

            @block.scalar
            def _(act):
                a = rows["alpha"][0]
                nc.scalar.activation(alpha_half[:], vec[:, a:a + NT], ACT.Sigmoid).then_inc(s_sig, 1)
                act.wait_ge(s_Pn, NT + 1)
                for t in range(NT):
                    nc.scalar.activation(Pns[0][:, t], Pn[:, t], ACT.Copy).then_inc(s_Pnhi, 1)
                for u in range(NT):
                    act.wait_ge(s_PT, u + 1)
                    nc.scalar.activation(PT[0][:, u], bank[u][:], ACT.Copy).then_inc(s_PThi, 1)
                ln_std(act, ln, 0)
                for n in range(2 * NT):
                    act.wait_ge(s_pow, n + 1)
                    m, u = power(n)
                    nc.scalar.activation(m[0][:, u], bank[u][:], ACT.Copy).then_inc(s_powhi, 1)
                    if 1 <= n <= 2:
                        ln_apply(act, ln, n - 1, 0)
                act.wait_ge(s_m, STEPS + 1)
                nc.scalar.activation(Ms[0][:], M[:], ACT.Copy).then_inc(s_mhi, 1)

            @block.tensor
            def _(pe):
                nc.tensor.transpose(bank[4][:, 0:D], w_n[:], ident[:]).then_inc(s_wt, 1)
                pe.wait_ge(s_wts, 2)
                nc.tensor.matmul(bank[4][:, 0:D], wTd[:], wT[:], start=True, stop=True).then_inc(s_weff, 1)
                pe.wait_ge(s_Pn, NT + 1)
                for u in range(NT):
                    for t in range(NT):
                        last = nc.tensor.transpose(bank[u][:, t * P:(t + 1) * P], Pn[:, t, u * P:(u + 1) * P], ident[:])
                    last.then_inc(s_PT, 1)
                for i in range(STEPS + 1):
                    pe.wait_ge(s_q, i + 1)
                    if i >= 2:
                        pe.wait_ge(s_m, i - 1)
                    fr = bank[5 + i % 2]
                    nc.tensor.matmul(fr[:, 0:D], fc_n[:], Q[:, i], start=True, stop=True)
                    nc.tensor.matmul(fr[:, D:2 * D], fcb_all[:], Q[:, i], start=True, stop=True).then_inc(s_F, 1)
                    if 1 <= i < STEPS:
                        nc.tensor.matmul(bank[4][:, 0:D], Q[:, i], Q[:, 1], start=True, stop=True).then_inc(s_weff, 1)
                    if i >= 1:
                        n = i - 1
                        if n == 0:
                            pe.wait_ge(s_PTlo, NT)
                            pe.wait_ge(s_Pnlo, NT)
                        if n == NT:
                            pe.wait_ge(s_p1, 3)
                            for t in range(NT):
                                for m in range(NT):
                                    for part in range(2):
                                        last = nc.tensor.matmul(bank[7][:, 2 * t:2 * t + 2], PT[part][:, m, t * P:(t + 1) * P], p1s[:, m],
                                                                start=(m == 0 and part == 0), stop=(m == NT - 1 and part == 1))
                            last.then_inc(s_p2, 1)
                            pe.wait_ge(s_powlo, NT)
                        rhs = PT if n < NT else P2T
                        u = n % NT
                        for k in range(NT):
                            last = products(bank[u][:], (Pns[0][:, k, u * P:(u + 1) * P], Pns[1][:, k, u * P:(u + 1) * P]),
                                            (rhs[0][:, k], rhs[1][:, k]), k == 0, k == NT - 1)
                        last.then_inc(s_pow, 1)

            @block.vector
            def _(dve):
                nc.vector.tensor_scalar(fcb_all[:], ones[:], col("fcb"), None, ALU.mult)
                nc.vector.tensor_copy(Q[:, 0], ident[:]).then_inc(s_q, 1)
                nc.vector.tensor_scalar(d_col[:], col("d"), 0.0, 1.0, ALU.max, ALU.min).then_inc(s_v, 1)
                dve.wait_ge(s_sig, 1)
                nc.vector.tensor_scalar(alpha_half[:], alpha_half[:], 0.5 * DT, None, ALU.mult).then_inc(s_v, 1)
                dve.wait_ge(s_v, 2)
                nc.vector.tensor_scalar(diag_col[:], alpha_half[:], -1.0, 1.0 - DT, ALU.mult, ALU.add).then_inc(s_v, 1)
                dve.wait_ge(s_wt, 1)
                nc.vector.tensor_copy(wT[:], bank[4][:, 0:D]).then_inc(s_wts, 1)
                nc.vector.tensor_scalar(wTd[:], bank[4][:, 0:D], d_col[:], None, ALU.mult).then_inc(s_wts, 1)
                for t in range(NT):
                    nc.vector.tensor_scalar(Pn[:, t], adj[:, t], alpha_half[:, t:t + 1], None, ALU.mult).then_inc(s_Pn, 1)
                dve.wait_ge(s_Pn, NT)
                dve.wait_ge(s_v, 3)
                for t in range(NT):
                    blk = Pn[:, t, t * P:(t + 1) * P]
                    last = nc.vector.scalar_tensor_tensor(out=blk, in0=ident[:], scalar=diag_col[:, t:t + 1], in1=blk,
                                                          op0=ALU.mult, op1=ALU.add)
                last.then_inc(s_Pn, 1)
                dve.wait_ge(s_weff, 1)
                nc.vector.tensor_scalar(Q[:, 1], bank[4][:, 0:D], DT, None, ALU.mult).then_inc(s_q, 1)
                for t in range(NT):
                    dve.wait_ge(s_Pnhi, t + 1)
                    nc.vector.tensor_tensor(Pns[1][:, t], Pn[:, t], as_f32(Pns[0][:, t]), ALU.subtract).then_inc(s_Pnlo, 1)
                for u in range(NT):
                    dve.wait_ge(s_PThi, u + 1)
                    nc.vector.tensor_tensor(PT[1][:, u], bank[u][:], as_f32(PT[0][:, u]), ALU.subtract).then_inc(s_PTlo, 1)
                for i in range(STEPS + 1):
                    if 1 <= i < STEPS:
                        dve.wait_ge(s_weff, i + 1)
                        nc.vector.tensor_copy(Q[:, i + 1], bank[4][:, 0:D]).then_inc(s_q, 1)
                    dve.wait_ge(s_q, i + 1)
                    if i >= 1:
                        dve.wait_ge(s_m, i)
                    dve.wait_ge(s_F, i + 1)
                    for j in range(STEPS - i):
                        k, o = place(j)
                        if i == 0:
                            nc.vector.tensor_scalar(M[:, k, o], Q[:, 0], DT, None, ALU.mult)
                        else:
                            nc.vector.scalar_tensor_tensor(out=M[:, k, o], in0=Q[:, i], scalar=DT * comb(i + j, j), in1=M[:, k, o],
                                                           op0=ALU.mult, op1=ALU.add)
                    j = STEPS - i
                    k, o = place(j)
                    fr = bank[5 + i % 2]
                    if i == 0:
                        nc.vector.tensor_copy(M[:, k, o], fr[:, 0:D])
                    else:
                        nc.vector.scalar_tensor_tensor(out=M[:, k, o], in0=fr[:, 0:D], scalar=float(comb(STEPS, j)), in1=M[:, k, o],
                                                       op0=ALU.mult, op1=ALU.add)
                    nc.vector.tensor_scalar(R[:, k, o], fr[:, D:2 * D], float(comb(STEPS, j)), None, ALU.mult).then_inc(s_m, 1)
                    if i >= 1:
                        n = i - 1
                        dve.wait_ge(s_powhi, n + 1)
                        m, u = power(n)
                        nc.vector.tensor_tensor(m[1][:, u], bank[u][:], as_f32(m[0][:, u]), ALU.subtract).then_inc(s_powlo, 1)
                    if i == 0:
                        ln_first_stats(dve, ln)
                    if i == 1:
                        ln_rstd(dve, ln, 0)
                    if i == 3:
                        ln_first_split(dve, ln)
                    if i == STEPS - 2:
                        dve.wait_ge(s_p2, 1)
                        nc.vector.tensor_copy(p2pair[:].rearrange("p t a -> p (t a)"), bank[7][:, 0:2 * NT]).then_inc(s_b, 1)
                        dve.wait_ge(s_b, 1)
                        nc.vector.tensor_tensor(p2[:], p2pair[:, :, 0], p2pair[:, :, 1], ALU.add).then_inc(s_b, 1)
                        dve.wait_ge(s_m, i + 1)
                        dve.wait_ge(s_b, 2)
                        for t in range(NT):
                            last = nc.vector.tensor_scalar(bias_w[:, t], R[:, 2], p2[:, t:t + 1], None, ALU.mult)
                        last.then_inc(s_b, 1)
                    if i == STEPS - 1:
                        dve.wait_ge(s_m, i + 1)
                        dve.wait_ge(s_b, 3)
                        for t in range(NT):
                            last = nc.vector.scalar_tensor_tensor(out=bias_w[:, t], in0=R[:, 1], scalar=p1[:, t:t + 1], in1=bias_w[:, t],
                                                                  op0=ALU.mult, op1=ALU.add)
                        last.then_inc(s_b, 1)
                    if i == 2:
                        dve.wait_ge(s_Pn, NT + 1)
                        nc.vector.tensor_reduce(p1[:], Pn[:], AX.X, ALU.add).then_inc(s_p1, 1)
                        dve.wait_ge(s_p1, 1)
                        nc.vector.tensor_copy(p1s[:, :, 0], p1[:]).then_inc(s_p1, 1)
                        dve.wait_ge(s_p1, 2)
                        nc.vector.tensor_tensor(p1s[:, :, 1], p1[:], as_f32(p1s[:, :, 0]), ALU.subtract).then_inc(s_p1, 1)
                dve.wait_ge(s_m, STEPS + 1)
                dve.wait_ge(s_b, 4)
                for t in range(NT):
                    nc.vector.tensor_tensor(bias_w[:, t], bias_w[:, t], R[:, 0], ALU.add)
                dve.wait_ge(s_mhi, 1)
                nc.vector.tensor_tensor(Ms[1][:], M[:], as_f32(Ms[0][:]), ALU.subtract)

        with stage() as c:
            Y = [[sb2(c, f"Y{k}_{s}", [P, N]) for k in range(KB)] for s in range(2)]
            WF = sb(c, "WF", [P, KI, 4, NT, D])
            Z = sb2(c, "Z", [P, 4, NT, D])
            Z1 = sb2(c, "Z1", [P, 4, NT, D])
            ln = LN(c, "l2")
            s_y = sem(c, "l2_y_done")
            s_yhi = sem(c, "l2_y_hi_ready")
            s_ylo = sem(c, "l2_y_lo_ready")
            s_w = sem(c, "l2_w_done")
            s_we = sem(c, "l2_w_ready")
            s_zhi = sem(c, "l2_z_hi_ready")
            s_z = sem(c, "l2_z_lo_ready")
            s_wx = sem(c, "l2_residual_added")
            s_r1 = sem(c, "l2_first_round_done")
            s_t1 = sem(c, "l2_z1_sum_ready")
            s_z1hi = sem(c, "l2_z1_hi_ready")
            s_z1 = sem(c, "l2_z1_lo_ready")
            s_r2 = sem(c, "l2_second_round_done")
            s_xo = sem(c, "l2_x_ready")
            block = c.enter_context(nc.Block())

            @block.tensor
            def _(pe):
                def y(q, s):
                    pe.wait_ge(ln.ready[s], q + 2)
                    for t in range(NT):
                        last = nc.tensor.transpose(bank[3 * s][:, t * P:(t + 1) * P], XN[s][:, t], ident[:])
                    last.then_inc(s_y, 1)
                    aggregate(bank[3 * s + 1][:], HN[s], PT).then_inc(s_y, 1)
                    aggregate(bank[3 * s + 2][:], HN[s], P2T).then_inc(s_y, 1)

                def w(q, s, begins=None):
                    b = 2 * q + s
                    pe.wait_ge(s_ylo, KB * b + KB)
                    for t in range(NT):
                        cols = slice(t * P, (t + 1) * P)
                        if begins is not None and t < 2:
                            pe.wait_ge(s_xo, NT * begins + t + 1)
                        pe.wait_ge(s_we, NT * b + t + 1)
                        for k in range(KB):
                            last = products(bank[6 + t % 2][:, 0:KI * D], (Y[s][k][0][:, cols], Y[s][k][1][:, cols]),
                                            (Ms[0][:, k].rearrange("p i d -> p (i d)"), Ms[1][:, k].rearrange("p i d -> p (i d)")),
                                            k == 0, k == KB - 1)
                        last.then_inc(s_w, 1)

                def apply_cube(t, z):
                    for m in range(NT):
                        last = products(bank[6 + t % 2][:].rearrange("p (b f) -> p b f", b=4),
                                        (P3T[0][:, m, t * P:(t + 1) * P], P3T[1][:, m, t * P:(t + 1) * P]),
                                        (z[0][:, :, m], z[1][:, :, m]), m == 0, m == NT - 1)
                    return last

                def quad(g, more):
                    w(2 * g, 0, g)
                    y(2 * g + 1, 0)
                    w(2 * g, 1)
                    y(2 * g + 1, 1)
                    w(2 * g + 1, 0)
                    w(2 * g + 1, 1)
                    if more:
                        y(2 * g + 2, 0)
                    pe.wait_ge(s_z, 4 * g + 4)
                    for t in range(NT):
                        if t >= 2:
                            pe.wait_ge(s_t1, NT * g + t - 1)
                        apply_cube(t, Z).then_inc(s_r1, 1)
                    if more:
                        y(2 * g + 2, 1)
                    pe.wait_ge(s_z1, NT * g + NT)
                    for t in range(NT):
                        if t >= 2:
                            pe.wait_ge(s_xo, NT * g + t + 1)
                        apply_cube(t, Z1).then_inc(s_r2, 1)

                y(0, 0)
                y(0, 1)
                with pe.Fori(0, QUADS - 1) as g:
                    quad(g, True)
                quad(QUADS - 1, False)

            @block.scalar
            def _(act):
                def y_hi(q, s):
                    for k in range(KB):
                        act.wait_ge(s_y, KB * (2 * q + s) + k + 1)
                        if k == 0 and (not isinstance(q, int) or q > 0):
                            act.wait_ge(s_w, NT * (2 * q + s - 1))
                        nc.scalar.activation(Y[s][k][0][:], bank[3 * s + k][:], ACT.Copy).then_inc(s_yhi, 1)

                def z_hi(q, s, h):
                    act.wait_ge(s_we, 2 + NT * (2 * q + s) + NT)
                    nc.scalar.activation(Z[0][:, 2 * h + s], WF[:, KI - 1, 2 * h + s], ACT.Copy).then_inc(s_zhi, 1)

                def quad(g, more):
                    q = 2 * g
                    of = None if more else 0
                    z_hi(q, 0, 0)
                    ln_std(act, ln, q + 2)
                    y_hi(q + 1, 0)
                    ln_apply(act, ln, 0, q + 2, of)
                    z_hi(q, 1, 0)
                    y_hi(q + 1, 1)
                    ln_apply(act, ln, 1, q + 2, of)
                    z_hi(q + 1, 0, 1)
                    z_hi(q + 1, 1, 1)
                    if more:
                        ln_std(act, ln, q + 3)
                        y_hi(q + 2, 0)
                        ln_apply(act, ln, 0, q + 3)
                    for t in range(NT):
                        act.wait_ge(s_t1, NT * g + t + 1)
                        nc.scalar.activation(Z1[0][:, :, t], WF[:, 1, :, t], ACT.Copy).then_inc(s_z1hi, 1)
                    if more:
                        y_hi(q + 2, 1)
                        ln_apply(act, ln, 1, q + 3)

                ln_taken(act, ln)
                ln_std(act, ln, 1)
                y_hi(0, 0)
                ln_apply(act, ln, 0, 1)
                y_hi(0, 1)
                ln_apply(act, ln, 1, 1)
                with act.Fori(0, QUADS - 1) as g:
                    quad(g, True)
                quad(QUADS - 1, False)

            @block.gpsimd
            def _(pool):
                def residual(g, j):
                    pool.wait_ge(s_we, 2 + NT * (4 * g + j) + NT)
                    nc.gpsimd.tensor_tensor(WF[:, 0, j].rearrange("p t f -> p (t f)"), WF[:, 0, j].rearrange("p t f -> p (t f)"),
                                            X[:, bass.ds(4 * g + j, 1)].rearrange("p a t f -> p (a t f)"), ALU.add).then_inc(s_wx, 1)

                def quad(g, more):
                    for h in range(2):
                        q = 2 * g + h
                        ln_split(pool, ln, 1, q + 1, s_y, KB * (2 * q + 2))
                        if h == 0 or more:
                            ln_split(pool, ln, 0, q + 2, s_y, KB * (2 * q + 3))
                        residual(g, 2 * h)
                        residual(g, 2 * h + 1)

                ln_taken(pool, ln)
                ln_split(pool, ln, 0, 1, s_y, KB)
                with pool.Fori(0, QUADS - 1) as g:
                    quad(g, True)
                quad(QUADS - 1, False)

            @block.vector
            def _(dve):
                def y_lo(q, s):
                    for k in range(KB):
                        dve.wait_ge(s_yhi, KB * (2 * q + s) + k + 1)
                        nc.vector.tensor_tensor(Y[s][k][1][:], bank[3 * s + k][:], as_f32(Y[s][k][0][:]), ALU.subtract).then_inc(s_ylo, 1)

                def w_out(q, s, h):
                    j = 2 * h + s
                    for t in range(NT):
                        dve.wait_ge(s_w, NT * (2 * q + s) + t + 1)
                        nc.vector.tensor_tensor(WF[:, :, j, t], bank[6 + t % 2][:, 0:KI * D].rearrange("p (i f) -> p i f", i=KI),
                                                bias_w[:, t], ALU.add).then_inc(s_we, 1)

                def z_lo(g, j):
                    dve.wait_ge(s_zhi, 4 * g + j + 1)
                    nc.vector.tensor_tensor(Z[1][:, j], WF[:, KI - 1, j], as_f32(Z[0][:, j]), ALU.subtract).then_inc(s_z, 1)

                def quad(g, more):
                    q = 2 * g
                    w_out(q, 0, 0)
                    ln_stats(dve, ln, q + 2, None if more else 0)
                    z_lo(g, 0)
                    ln_rstd(dve, ln, q + 2)
                    y_lo(q + 1, 0)
                    w_out(q, 1, 0)
                    z_lo(g, 1)
                    y_lo(q + 1, 1)
                    w_out(q + 1, 0, 1)
                    w_out(q + 1, 1, 1)
                    z_lo(g, 2)
                    z_lo(g, 3)
                    if more:
                        ln_stats(dve, ln, q + 3)
                        ln_rstd(dve, ln, q + 3)
                        y_lo(q + 2, 0)
                    for t in range(NT):
                        dve.wait_ge(s_r1, NT * g + t + 1)
                        nc.vector.tensor_tensor(WF[:, 1, :, t], bank[6 + t % 2][:].rearrange("p (b f) -> p b f", b=4), WF[:, 1, :, t],
                                                ALU.add).then_inc(s_t1, 1)
                        dve.wait_ge(s_z1hi, NT * g + t + 1)
                        nc.vector.tensor_tensor(Z1[1][:, :, t], WF[:, 1, :, t], as_f32(Z1[0][:, :, t]), ALU.subtract).then_inc(s_z1, 1)
                    if more:
                        y_lo(2 * g + 2, 1)
                    dve.wait_ge(s_wx, 4 * g + 4)
                    for t in range(NT):
                        dve.wait_ge(s_r2, NT * g + t + 1)
                        nc.vector.tensor_tensor(X[:, bass.ds(4 * g, 4), t], bank[6 + t % 2][:].rearrange("p (b f) -> p b f", b=4),
                                                WF[:, 0, :, t], ALU.add).then_inc(s_xo, 1)

                dve.sem_inc(s_we, 2)
                dve.sem_inc(s_xo, 2)
                ln_taken(dve, ln)
                ln_stats(dve, ln, 1)
                ln_rstd(dve, ln, 1)
                y_lo(0, 0)
                y_lo(0, 1)
                with dve.Fori(0, QUADS - 1) as g:
                    quad(g, True)
                quad(QUADS - 1, False)
        l2.close()

        WqT = sb2(top, "WqT", [P, NT, N])
        W1s = sb2(top, "W1s", [P, H3A * P])
        W2s = sb2(top, "W2s", [P, H3A, H3B * P])
        W3s = sb2(top, "W3s", [P, H3B, D])
        with stage() as c:
            A3 = sb(c, "A3", [P, NT, N])
            w1f = sb(c, "w1f", [P, H3A * P])
            w2f = sb(c, "w2f", [P, H3A, H3B * P])
            w3f = sb(c, "w3f", [P, H3B, D])
            s_w = sem(c, "l3_weights_loaded")
            s_sq = sem(c, "l3_adj_squared")
            s_whi = sem(c, "l3_weights_hi_ready")
            s_T = sem(c, "l3_matrix_transposed")
            s_hi = sem(c, "l3_matrix_hi_ready")
            block = c.enter_context(nc.Block())

            @block.sync
            def _(sp):
                sp.dma_start(w1f[:], d["L3_gnn_W1"]).then_inc(s_w, 16)
                sp.dma_start(w2f[:], d["L3_gnn_W2"].rearrange("(t p) n -> p t n", p=P)).then_inc(s_w, 16)
                sp.dma_start(w3f[:], d["L3_gnn_W3"].rearrange("(t p) n -> p t n", p=P)).then_inc(s_w, 16)

            @block.tensor
            def _(pe):
                pe.wait_ge(s_sq, NT)
                for u in range(NT):
                    for t in range(NT):
                        last = nc.tensor.transpose(bank[u][:, t * P:(t + 1) * P], A3[:, t, u * P:(u + 1) * P], ident[:])
                    last.then_inc(s_T, 1)

            @block.gpsimd
            def _(pool):
                for t in range(NT - 1, NT):
                    nc.gpsimd.tensor_tensor(A3[:, t], adj[:, t], adj[:, t], ALU.mult).then_inc(s_sq, 1)

            @block.scalar
            def _(act):
                for u in range(NT):
                    act.wait_ge(s_T, u + 1)
                    nc.scalar.activation(WqT[0][:, u], bank[u][:], ACT.Copy).then_inc(s_hi, 1)
                act.wait_ge(s_w, 48)
                nc.scalar.activation(W1s[0][:], w1f[:], ACT.Copy).then_inc(s_whi, 1)
                nc.scalar.activation(W2s[0][:], w2f[:], ACT.Copy).then_inc(s_whi, 1)
                nc.scalar.activation(W3s[0][:], w3f[:], ACT.Copy).then_inc(s_whi, 1)

            @block.vector
            def _(dve):
                for t in range(NT - 1):
                    nc.vector.tensor_tensor(A3[:, t], adj[:, t], adj[:, t], ALU.mult).then_inc(s_sq, 1)
                for u in range(NT):
                    dve.wait_ge(s_hi, u + 1)
                    nc.vector.tensor_tensor(WqT[1][:, u], bank[u][:], as_f32(WqT[0][:, u]), ALU.subtract)
                dve.wait_ge(s_whi, 3)
                nc.vector.tensor_tensor(W1s[1][:], w1f[:], as_f32(W1s[0][:]), ALU.subtract)
                nc.vector.tensor_tensor(W2s[1][:], w2f[:], as_f32(W2s[0][:]), ALU.subtract)
                nc.vector.tensor_tensor(W3s[1][:], w3f[:], as_f32(W3s[0][:]), ALU.subtract)

        with stage() as c:
            U1 = [sb2(c, f"U1_{s}", [P, N]) for s in range(2)]
            GH = [sb2(c, f"GH_{s}", [P, NT, H3A * P]) for s in range(2)]
            U2 = [sb2(c, f"U2_{s}", [P, H3A, N]) for s in range(2)]
            H2 = [sb2(c, f"H2_{s}", [P, H3B, N]) for s in range(2)]
            S3T = [sb(c, f"S3T_{s}", [P, N]) for s in range(2)]
            S3 = sb2(c, "S3", [P, 4, NT, D])
            ln = LN(c, "l3")
            s_u1 = sem(c, "l3_u1_done")
            s_u1hi = sem(c, "l3_u1_hi_ready")
            s_u1lo = sem(c, "l3_u1_lo_ready")
            s_h1 = sem(c, "l3_h1_done")
            s_h1hi = sem(c, "l3_h1_hi_ready")
            s_h1lo = sem(c, "l3_h1_lo_ready")
            s_u2 = sem(c, "l3_u2_done")
            s_u2hi = sem(c, "l3_u2_hi_ready")
            s_u2lo = sem(c, "l3_u2_lo_ready")
            s_h2 = sem(c, "l3_h2_done")
            s_h2hi = sem(c, "l3_h2_hi_ready")
            s_h2lo = sem(c, "l3_h2_lo_ready")
            s_s3 = sem(c, "l3_s3_done")
            s_s3c = sem(c, "l3_s3_copied")
            s_tr = sem(c, "l3_s3_transposed")
            s_s3hi = sem(c, "l3_s3_hi_ready")
            s_s3lo = sem(c, "l3_s3_lo_ready")
            s_f = sem(c, "l3_final_sum_done")
            s_fo = sem(c, "l3_x_ready")
            s_out = sem(c, "out_stored")
            block = c.enter_context(nc.Block())
            HB = 2
            FBANK = (3, 0)
            U2BANK = (3, 0)
            H2BANK = (1, 2, 3, 0)

            def split_cols(x, sl):
                return x[0][:, sl], x[1][:, sl]

            @block.tensor
            def _(pe):
                def u1(q, s):
                    pe.wait_ge(ln.ready[s], q + 2)
                    aggregate(bank[4 * s][:], HN[s], WqT).then_inc(s_u1, 1)

                def h1(q, s):
                    pe.wait_ge(s_u1lo, 2 * q + s + 1)
                    pe.wait_ge(s_s3lo, 2 * q + s + 1)
                    for t in range(NT):
                        out = bank[4 * s + 1 + t // 2][:, (t % 2) * H3A * P:(t % 2 + 1) * H3A * P]
                        last = products(out, split_cols(U1[s], slice(t * P, (t + 1) * P)), (W1s[0][:], W1s[1][:]), True, True)
                        if t % 2 == 1:
                            last.then_inc(s_h1, 1)

                def u2(q, s, beside=None):
                    pe.wait_ge(s_h1lo, HB * (2 * q + s) + HB)
                    for f in range(H3A):
                        if beside is not None and U2BANK[f] == 0:
                            pe.wait_ge(s_u1lo, beside)
                        for m in range(NT):
                            last = products(bank[4 * s + U2BANK[f]][:], (GH[s][0][:, m, f * P:(f + 1) * P], GH[s][1][:, m, f * P:(f + 1) * P]),
                                            (WqT[0][:, m], WqT[1][:, m]), m == 0, m == NT - 1)
                        last.then_inc(s_u2, 1)

                def h2(q, s):
                    pe.wait_ge(s_u2lo, H3A * (2 * q + s) + H3A)
                    for o in range(H3B):
                        for f in range(H3A):
                            last = products(bank[4 * s + H2BANK[o]][:], (W2s[0][:, f, o * P:(o + 1) * P], W2s[1][:, f, o * P:(o + 1) * P]),
                                            (U2[s][0][:, f], U2[s][1][:, f]), f == 0, f == H3A - 1)
                        last.then_inc(s_h2, 1)

                def s3(q, s):
                    for k in range(H3B):
                        pe.wait_ge(s_h2lo, H3B * (2 * q + s) + k + 1)
                        last = products(bank[4 * s + 1][:], (W3s[0][:, k], W3s[1][:, k]), (H2[s][0][:, k], H2[s][1][:, k]),
                                        k == 0, k == H3B - 1)
                    last.then_inc(s_s3, 1)

                def turn(q, s):
                    pe.wait_ge(s_s3c, 2 * q + s + 1)
                    for t in range(NT):
                        last = nc.tensor.transpose(bank[4 * s + 2][:, t * P:(t + 1) * P], S3T[s][:, t * P:(t + 1) * P], ident[:])
                    last.then_inc(s_tr, 1)

                def pair(q, more, opens):
                    if opens is None:
                        h1(q, 0)
                        if more:
                            u1(q + 1, 0)
                        h1(q, 1)
                    else:
                        h1(q, 1)
                        pe.wait_ge(s_fo, NT * opens + 1)
                        u1(q + 1, 0)
                    u2(q, 0, 2 * q + 3 if more else None)
                    u2(q, 1)
                    h2(q, 0)
                    h2(q, 1)
                    s3(q, 0)
                    s3(q, 1)
                    turn(q, 0)
                    if more:
                        u1(q + 1, 1)
                    turn(q, 1)

                def quad(g, more):
                    pair(2 * g, True, g)
                    pair(2 * g + 1, more, None)
                    if more:
                        h1(2 * g + 2, 0)
                    pe.wait_ge(s_s3lo, 2 + 4 * g + 4)
                    for t in range(NT):
                        if t >= 2:
                            pe.wait_ge(s_fo, NT * g + t)
                        for m in range(NT):
                            last = products(bank[FBANK[t % 2]][:].rearrange("p (b f) -> p b f", b=4),
                                            (WqT[0][:, m, t * P:(t + 1) * P], WqT[1][:, m, t * P:(t + 1) * P]),
                                            (S3[0][:, :, m], S3[1][:, :, m]), m == 0, m == NT - 1)
                        last.then_inc(s_f, 1)

                u1(0, 0)
                u1(0, 1)
                h1(0, 0)
                with pe.Fori(0, QUADS - 1) as g:
                    quad(g, True)
                quad(QUADS - 1, False)

            @block.scalar
            def _(act):
                def u1_hi(q, s):
                    act.wait_ge(s_u1, 2 * q + s + 1)
                    if not isinstance(q, int) or q > 0:
                        act.wait_ge(s_h1, HB * (2 * q + s - 1))
                    nc.scalar.activation(U1[s][0][:], bank[4 * s][:], ACT.Copy).then_inc(s_u1hi, 1)

                def h1_hi(q, s):
                    for n in range(HB):
                        act.wait_ge(s_h1, HB * (2 * q + s) + n + 1)
                        nc.scalar.activation(GH[s][0][:, 2 * n:2 * n + 2], bank[4 * s + 1 + n][:].rearrange("p (t f) -> p t f", t=2),
                                             ACT.Relu).then_inc(s_h1hi, 1)

                def u2_hi(q, s):
                    for f in range(H3A):
                        act.wait_ge(s_u2, H3A * (2 * q + s) + f + 1)
                        nc.scalar.activation(U2[s][0][:, f], bank[4 * s + U2BANK[f]][:], ACT.Copy).then_inc(s_u2hi, 1)

                def h2_hi(q, s):
                    for o in range(H3B):
                        act.wait_ge(s_h2, H3B * (2 * q + s) + o + 1)
                        nc.scalar.activation(H2[s][0][:, o], bank[4 * s + H2BANK[o]][:], ACT.Relu).then_inc(s_h2hi, 1)

                def s3_copy(q, s):
                    act.wait_ge(s_s3, 2 * q + s + 1)
                    nc.scalar.activation(S3T[s][:], bank[4 * s + 1][:], ACT.Copy).then_inc(s_s3c, 1)

                def s3_hi(q, s, h):
                    act.wait_ge(s_tr, 2 * q + s + 1)
                    nc.scalar.activation(S3[0][:, 2 * h + s].rearrange("p t f -> p (t f)"), bank[4 * s + 2][:], ACT.Copy).then_inc(s_s3hi, 1)

                def pair(q, h, more, more2):
                    if h == 0:
                        h1_hi(q, 1)
                        u1_hi(q + 1, 0)
                    else:
                        h1_hi(q, 0)
                        if more:
                            u1_hi(q + 1, 0)
                        h1_hi(q, 1)
                    if more2:
                        ln_std(act, ln, q + 2)
                    u2_hi(q, 0)
                    if more2:
                        ln_apply(act, ln, 0, q + 2)
                    u2_hi(q, 1)
                    h2_hi(q, 0)
                    if more2:
                        ln_apply(act, ln, 1, q + 2)
                    h2_hi(q, 1)
                    s3_copy(q, 0)
                    s3_copy(q, 1)
                    s3_hi(q, 0, h)
                    if more:
                        u1_hi(q + 1, 1)
                    s3_hi(q, 1, h)

                ln_taken(act, ln)
                ln_std(act, ln, 1)
                ln_apply(act, ln, 0, 1)
                u1_hi(0, 0)
                ln_apply(act, ln, 1, 1)
                u1_hi(0, 1)
                h1_hi(0, 0)
                with act.Fori(0, QUADS - 1) as g:
                    pair(2 * g, 0, True, True)
                    pair(2 * g + 1, 1, True, True)
                    h1_hi(2 * g + 2, 0)
                pair(PAIRS - 2, 0, True, False)
                pair(PAIRS - 1, 1, False, False)

            @block.gpsimd
            def _(pool):
                ln_split_all(pool, ln, s_u1)

            @block.vector
            def _(dve):
                def u1_lo(q, s):
                    dve.wait_ge(s_u1hi, 2 * q + s + 1)
                    nc.vector.tensor_tensor(U1[s][1][:], bank[4 * s][:], as_f32(U1[s][0][:]), ALU.subtract).then_inc(s_u1lo, 1)

                def h1_lo(q, s):
                    for n in range(HB):
                        dve.wait_ge(s_h1hi, HB * (2 * q + s) + n + 1)
                        nc.vector.scalar_tensor_tensor(out=GH[s][1][:, 2 * n:2 * n + 2], in0=bank[4 * s + 1 + n][:].rearrange("p (t f) -> p t f", t=2),
                                                       scalar=0.0, in1=as_f32(GH[s][0][:, 2 * n:2 * n + 2]), op0=ALU.max, op1=ALU.subtract).then_inc(s_h1lo, 1)

                def u2_lo(q, s):
                    for f in range(H3A):
                        dve.wait_ge(s_u2hi, H3A * (2 * q + s) + f + 1)
                        nc.vector.tensor_tensor(U2[s][1][:, f], bank[4 * s + U2BANK[f]][:], as_f32(U2[s][0][:, f]), ALU.subtract).then_inc(s_u2lo, 1)

                def h2_lo(q, s):
                    for o in range(H3B):
                        dve.wait_ge(s_h2hi, H3B * (2 * q + s) + o + 1)
                        nc.vector.scalar_tensor_tensor(out=H2[s][1][:, o], in0=bank[4 * s + H2BANK[o]][:], scalar=0.0,
                                                       in1=as_f32(H2[s][0][:, o]), op0=ALU.max, op1=ALU.subtract).then_inc(s_h2lo, 1)

                def s3_lo(q, s, h):
                    dve.wait_ge(s_s3hi, 2 * q + s + 1)
                    nc.vector.tensor_tensor(S3[1][:, 2 * h + s].rearrange("p t f -> p (t f)"), bank[4 * s + 2][:],
                                            as_f32(S3[0][:, 2 * h + s]).rearrange("p t f -> p (t f)"), ALU.subtract).then_inc(s_s3lo, 1)

                def pair(q, h, more, more2):
                    if h == 0:
                        h1_lo(q, 1)
                        u1_lo(q + 1, 0)
                    else:
                        h1_lo(q, 0)
                        if more:
                            u1_lo(q + 1, 0)
                        h1_lo(q, 1)
                    if more2:
                        ln_stats(dve, ln, q + 2)
                        ln_rstd(dve, ln, q + 2)
                    u2_lo(q, 0)
                    u2_lo(q, 1)
                    h2_lo(q, 0)
                    h2_lo(q, 1)
                    s3_lo(q, 0, h)
                    if more:
                        u1_lo(q + 1, 1)
                    s3_lo(q, 1, h)

                def final(g):
                    for t in range(NT):
                        dve.wait_ge(s_f, NT * g + t + 1)
                        xt = X[:, bass.ds(4 * g, 4), t]
                        nc.vector.tensor_tensor(xt, bank[FBANK[t % 2]][:].rearrange("p (b f) -> p b f", b=4), xt, ALU.add).then_inc(s_fo, 1)

                dve.sem_inc(s_fo, 1)
                dve.sem_inc(s_s3lo, 2)
                ln_taken(dve, ln)
                ln_stats(dve, ln, 1)
                ln_rstd(dve, ln, 1)
                u1_lo(0, 0)
                u1_lo(0, 1)
                h1_lo(0, 0)
                with dve.Fori(0, QUADS - 1) as g:
                    pair(2 * g, 0, True, True)
                    pair(2 * g + 1, 1, True, True)
                    h1_lo(2 * g + 2, 0)
                    final(g)
                pair(PAIRS - 2, 0, True, False)
                pair(PAIRS - 1, 1, False, False)
                final(QUADS - 1)

            @block.sync
            def _(sp):
                with sp.Fori(0, QUADS) as g:
                    for t in range(NT):
                        sp.wait_ge(s_fo, 1 + NT * g + t + 1)
                        sp.dma_start(d["out"][bass.ds(4 * g, 4), t * P:(t + 1) * P, :].rearrange("b p f -> p b f"),
                                     X[:, bass.ds(4 * g, 4), t]).then_inc(s_out, 16)
                sp.wait_ge(s_out, 16 * NT * QUADS)


def kernel(**inputs):
    import concourse.bacc as bacc
    from concourse import mybir
    from concourse.bass_utils import run_bass_kernel_spmd

    nc = bacc.Bacc("TRN2", target_bir_lowering=False, num_devices=1)
    arrays, aps = {}, {}
    for name, a in inputs.items():
        a = np.ascontiguousarray(a)
        arrays[name + "_dram"] = a
        aps[name] = nc.dram_tensor(name + "_dram", a.shape, mybir.dt.from_np(a.dtype), kind="ExternalInput").ap()
    aps["out"] = nc.dram_tensor("out_dram", inputs["x"].shape, mybir.dt.float32, kind="ExternalOutput").ap()
    graph_stack_kernel(nc, aps)
    r = run_bass_kernel_spmd(nc, [arrays], core_ids=[0])
    return r.results[0]["out_dram"]
```
